# Optimizing a Trainium2 kernel written in Bass

```python
import numpy as np
import jax
import jax.numpy as jnp

def _softmax(x, axis=-1):
    return jax.nn.softmax(x, axis=axis)

def _gelu(x):
    return jax.nn.gelu(x, approximate=True)

def _silu(x):
    return jax.nn.silu(x)

def _sigmoid(x):
    return jax.nn.sigmoid(x)

def _layernorm(x, axis=-1, eps=1e-05):
    m = jnp.mean(x, axis=axis, keepdims=True)
    v = jnp.var(x, axis=axis, keepdims=True)
    return (x - m) / jnp.sqrt(v + eps)

def _scatter_add(tgt, idx, src, axis=0):
    return tgt.at[idx].add(src)

def _segment_sum(src, seg, n):
    return jax.ops.segment_sum(src, seg, n)
kernel_name = 'mk_adj_resnorm_d2_adj_r2_992918'

def setup_inputs(seed: int=0):
    np.random.seed(seed)
    _w = jnp.asarray

    def _rec_inputs():
        import jax
        import jax.numpy as jnp
        _gk = jax.random.key(seed)
        x = -6.813e-05 + 0.02003 * jax.random.normal(jax.random.fold_in(_gk, 1), (64, 128, 128), jnp.float32)
        _w = (1.0 + jnp.arange(128, dtype=jnp.float32)) ** (-0.5)
        _w = _w / _w.mean()
        _pij = jnp.clip(0.03125 * _w[:, None] * _w[None, :], 0.0, 1.0)
        _a = jax.random.uniform(jax.random.fold_in(_gk, 2), (64, 128, 128)) < _pij
        _af = _a.astype(jnp.float32)
        adj = _af
        return (x, adj)
    x, adj = _rec_inputs()

    def _L0_gnn_setup():
        import jax, jax.numpy as jnp
        import numpy as np
        C = 1.0
        MIN_NORM = 1e-15
        EPS = 1e-07

        def _sqnorm(x):
            return jnp.sum(x * x, axis=-1, keepdims=True)

        def _norm(x):
            return jnp.sqrt(jnp.maximum(_sqnorm(x), MIN_NORM))

        def _atanh(u):
            return jnp.arctanh(jnp.clip(u, -1.0 + EPS, 1.0 - EPS))

        def mobius_add(x, y, c):
            x2 = _sqnorm(x)
            y2 = _sqnorm(y)
            xy = jnp.sum(x * y, axis=-1, keepdims=True)
            num = (1.0 + 2.0 * c * xy + c * y2) * x + (1.0 - c * x2) * y
            den = 1.0 + 2.0 * c * xy + c * c * x2 * y2
            return num / jnp.maximum(den, MIN_NORM)

        def logmap0(p, c):
            sc = jnp.sqrt(c)
            pn = _norm(p)
            return p / pn / sc * _atanh(sc * pn)

        def logmap(p1, p2, c):
            sub = mobius_add(-p1, p2, c)
            sn = _norm(sub)
            lam = 2.0 / jnp.maximum(1.0 - c * _sqnorm(p1), MIN_NORM)
            sc = jnp.sqrt(c)
            return 2.0 / sc / lam * _atanh(sc * sn) * sub / sn

        def expmap(p, u, c):
            un = _norm(u)
            lam = 2.0 / jnp.maximum(1.0 - c * _sqnorm(p), MIN_NORM)
            sc = jnp.sqrt(c)
            second = jnp.tanh(sc * lam * un / 2.0) * u / (sc * un)
            return mobius_add(p, second, c)
        key = jax.random.key(seed)
        k1, k2, k3 = jax.random.split(key, 3)
        B, N, D = (1, 512, 128)
        x = jax.random.normal(k1, (B, N, D), jnp.float32) * 0.02
        adj = (jax.random.uniform(k2, (B, N, N)) < 0.05).astype(jnp.float32)
        att_w = jax.random.normal(k3, (2 * D,), jnp.float32) * 0.1
        att_b = jnp.zeros((), jnp.float32)
        return {'x': x, 'adj': adj, 'att_w': att_w, 'att_b': att_b}
    _L0_gnn_all = _L0_gnn_setup()
    _L0_gnn_in = {k: v for k, v in _L0_gnn_all.items() if k in ('att_w', 'att_b')}
    del _L0_gnn_all

    def _L1_gnn_setup():
        import jax, jax.numpy as jnp
        import numpy as np
        B, S, H, HID = (1, 512, 128, 128)
        LN_EPS = 1e-05

        def _layernorm(y, gamma, beta):
            mu = jnp.mean(y, axis=-1, keepdims=True)
            var = jnp.mean(jnp.square(y - mu), axis=-1, keepdims=True)
            return (y - mu) * jax.lax.rsqrt(var + LN_EPS) * gamma + beta
        key = jax.random.key(seed)
        ks = jax.random.split(key, 8)
        x = jax.random.normal(ks[0], (B, S, H), dtype=jnp.float32)
        adj = jax.random.uniform(ks[1], (B, S, S), dtype=jnp.float32)
        W1 = jax.random.normal(ks[2], (2 * H, HID), dtype=jnp.float32) / np.sqrt(2 * H)
        b1 = jnp.zeros((HID,), dtype=jnp.float32)
        W2 = jax.random.normal(ks[3], (HID, HID), dtype=jnp.float32) / np.sqrt(HID)
        b2 = jnp.zeros((HID,), dtype=jnp.float32)
        gamma = jnp.ones((HID,), dtype=jnp.float32)
        beta = jnp.zeros((HID,), dtype=jnp.float32)
        return {'x': x, 'adj': adj, 'W1': W1, 'b1': b1, 'W2': W2, 'b2': b2, 'gamma': gamma, 'beta': beta}
    _L1_gnn_all = _L1_gnn_setup()
    _L1_gnn_in = {k: v for k, v in _L1_gnn_all.items() if k in ('W1', 'b1', 'W2', 'b2', 'gamma', 'beta')}
    del _L1_gnn_all
    return {'x': x, 'adj': adj, 'L0_gnn_att_w': _L0_gnn_in['att_w'], 'L0_gnn_att_b': _L0_gnn_in['att_b'], 'L1_gnn_W1': _L1_gnn_in['W1'], 'L1_gnn_b1': _L1_gnn_in['b1'], 'L1_gnn_W2': _L1_gnn_in['W2'], 'L1_gnn_b2': _L1_gnn_in['b2'], 'L1_gnn_gamma': _L1_gnn_in['gamma'], 'L1_gnn_beta': _L1_gnn_in['beta']}

def reference(x, adj, L0_gnn_att_w, L0_gnn_att_b, L1_gnn_W1, L1_gnn_b1, L1_gnn_W2, L1_gnn_b2, L1_gnn_gamma, L1_gnn_beta):
    import jax
    import jax.numpy as jnp

    def _L0_gnn_ref(x, adj, att_w, att_b):
        import jax, jax.numpy as jnp
        import numpy as np
        C = 1.0
        MIN_NORM = 1e-15
        EPS = 1e-07

        def _sqnorm(x):
            return jnp.sum(x * x, axis=-1, keepdims=True)

        def _norm(x):
            return jnp.sqrt(jnp.maximum(_sqnorm(x), MIN_NORM))

        def _atanh(u):
            return jnp.arctanh(jnp.clip(u, -1.0 + EPS, 1.0 - EPS))

        def mobius_add(x, y, c):
            x2 = _sqnorm(x)
            y2 = _sqnorm(y)
            xy = jnp.sum(x * y, axis=-1, keepdims=True)
            num = (1.0 + 2.0 * c * xy + c * y2) * x + (1.0 - c * x2) * y
            den = 1.0 + 2.0 * c * xy + c * c * x2 * y2
            return num / jnp.maximum(den, MIN_NORM)

        def logmap0(p, c):
            sc = jnp.sqrt(c)
            pn = _norm(p)
            return p / pn / sc * _atanh(sc * pn)

        def logmap(p1, p2, c):
            sub = mobius_add(-p1, p2, c)
            sn = _norm(sub)
            lam = 2.0 / jnp.maximum(1.0 - c * _sqnorm(p1), MIN_NORM)
            sc = jnp.sqrt(c)
            return 2.0 / sc / lam * _atanh(sc * sn) * sub / sn

        def expmap(p, u, c):
            un = _norm(u)
            lam = 2.0 / jnp.maximum(1.0 - c * _sqnorm(p), MIN_NORM)
            sc = jnp.sqrt(c)
            second = jnp.tanh(sc * lam * un / 2.0) * u / (sc * un)
            return mobius_add(p, second, c)
        B, N, D = x.shape
        x_t = logmap0(x, C)
        left = x_t @ att_w[:D]
        right = x_t @ att_w[D:]
        att = jax.nn.sigmoid(left[:, :, None] + right[:, None, :] + att_b) * adj
        x_local = logmap(x[:, :, None, :], x[:, None, :, :], C)
        support_t = jnp.einsum('bij,bijd->bid', att, x_local)
        return expmap(x, support_t, C)

    def _L1_gnn_ref(x, adj, W1, b1, W2, b2, gamma, beta):
        import jax, jax.numpy as jnp
        import numpy as np
        B, S, H, HID = (1, 512, 128, 128)
        LN_EPS = 1e-05

        def _layernorm(y, gamma, beta):
            mu = jnp.mean(y, axis=-1, keepdims=True)
            var = jnp.mean(jnp.square(y - mu), axis=-1, keepdims=True)
            return (y - mu) * jax.lax.rsqrt(var + LN_EPS) * gamma + beta
        hi = jnp.einsum('bsh,hk->bsk', x, W1[:H])
        hj = jnp.einsum('bsh,hk->bsk', x, W1[H:])
        h = jax.nn.relu(hi[:, :, None, :] + hj[:, None, :, :] + b1)
        y = jnp.einsum('bijk,kl->bijl', h, W2) + b2
        y = _layernorm(y, gamma, beta)
        out = jnp.einsum('bij,bijh->bih', adj, y)
        return out
    x = _layernorm(x + _L0_gnn_ref(x, adj, L0_gnn_att_w, L0_gnn_att_b), axis=-1)
    x = _layernorm(x + _L1_gnn_ref(x, adj, L1_gnn_W1, L1_gnn_b1, L1_gnn_W2, L1_gnn_b2, L1_gnn_gamma, L1_gnn_beta), axis=-1)
    return x

_drawn_inputs = setup_inputs


def setup_inputs(seed=0):
    import zlib

    import numpy as np

    out = dict(_drawn_inputs(seed))
    spreads = {'L1_gnn_b1': (0.0, 0.1),
     'L1_gnn_b2': (0.0, 0.1),
     'L1_gnn_gamma': (1.0, 0.2),
     'L1_gnn_beta': (0.0, 0.1)}
    factors = {'L0_gnn_att_w': 3.809}
    for name, (base, spread) in spreads.items():
        noise = np.random.default_rng([zlib.crc32(name.encode()), seed]).standard_normal(out[name].shape)
        drawn = base * np.exp(spread * noise) if base else spread * noise
        out[name] = jnp.asarray(drawn.astype(out[name].dtype))
    for name, factor in factors.items():
        out[name] = (out[name] * factor).astype(out[name].dtype)
    return out
```

```python
from contextlib import ExitStack

import concourse.bass as bass
from concourse import mybir

NB = 64
N = 128
D = 128
GB = 4
NG = NB // GB
W = GB * N
CH = 4
T = CH * 128
TILES = GB + 1
CAP = T + 128
PARTS = 3
ROWS = 4 * GB
X2, BB, LL, RR = range(4)

MIN_NORM = 1e-15
CLIP = 1.0 - 1e-7
LN_EPS = 1e-5
LOG_MIN_NORM = -34.538776394910684
ROW_STEPS, COL_STEPS, DENSE_ROW_STEPS = 37, 13, 8
TINY = 2.0 ** -60
SIG_MAX = 1e19

ALU = mybir.AluOpType
ACT = mybir.ActivationFunctionType
F32 = mybir.dt.float32
BF16 = mybir.dt.bfloat16
FP16 = mybir.dt.float16
I32 = mybir.dt.int32
AX_X = mybir.AxisListType.X

GROUP_STEPS = """loaded adj_loaded adjt_loaded xt_loaded xm2 lr sqx x2 x2m lpn pn pcl at1 at2 xcol lrc rowsb rowst_ps rowst d2 bj_ps
lg bjs esig esigc lse den nm denc lnn lnd ls lsc uu ucl l1 l2 qe q2e w0 dl w1 wt mm sw xmp sqm sws uqm lun un zz ez
ga tx hh bns bna vare lv rs x1s x1a x1t_ps x1t scan degs dega off offc mid vt bsq bdiff bad
fin1 fin2 fin3 fbns fbna fvare flv frs fout stored rows frows cols""".split()
BATCH_STEPS = "tab t0 r1 t1 t2b absd si vg ie ies sj hps ht yps z sq ss lnv rstd sit ops osb".split()
ONCE_STEPS = "const selb w2sum w2c b2sum b2c ones badr nall badn okm okn flagf flag".split()
DENSE_STEPS = "loaded x1 x1t_ps x1t hps hidden_ready h y z sq lv r w o turned rows bns var lv2 rs out stored".split()


def two_graph_layers(nc, x_n, x_t, adj_n, adj_t, att_w, att_b, W1, b1, W2, b2, gamma, beta,
                     c_f32, c_fp16, c_sel, out, groups=NG):
    with ExitStack() as ctx:
        def sb(name, shape, dt=F32):
            return ctx.enter_context(nc.sbuf_tensor(name, shape, dt))

        sem = {n: ctx.enter_context(nc.semaphore(f"s_{n}"))
                                 for n in GROUP_STEPS + ["e_" + b for b in BATCH_STEPS] + ONCE_STEPS
                                 + ["dense_" + d for d in DENSE_STEPS]
                                 }

        x_all = sb("x_all", [128, NB * D])
        x1_all = sb("x1_all", [128, NB * D])
        vt_all = sb("vt_all", [128, NB * N], FP16)
        deg_all = sb("deg_all", [128, NB])
        half_all = sb("half_all", [128, NB])
        mid_all = sb("mid_all", [128, NB])
        bad_all = sb("bad_all", [128, NG])

        cf = sb("cf", [128, 3 * 128 + 512 + 1])
        tri, ident, ones_f = cf[:, 0:128], cf[:, 128:256], cf[:, 256:384]
        reset = cf[:, 384:896]
        ch = sb("ch", [128, CAP + 2 * T + 128 + 1], FP16)
        iota_e = ch[:, 0:CAP]
        rank_main = ch[:, CAP:CAP + T]
        rank_tail = ch[:, CAP + T:CAP + 2 * T]
        iota_i1, col_i1 = ch[:, CAP + 2 * T:CAP + 2 * T + 128], ch[:, CAP + 2 * T + 128:CAP + 2 * T + 129]
        colb = sb("colb", [128, 1], BF16)
        identb = sb("identb", [128, 128], BF16)
        self_ = sb("self", [PARTS * ROWS, 4 * GB * 128], FP16)
        selb = sb("selb", [PARTS * ROWS, 4 * GB * 128], BF16)
        selv = selb[:, :].rearrange("k (t b n) -> k t b n", t=4, b=GB)
        wlr = sb("wlr", [128, 2])
        attb = sb("attb", [128, 1])
        w1c = sb("w1c", [128, 256])
        b1c = sb("b1c", [128, 1])
        w2 = sb("w2", [128, 128])
        w2s = sb("w2s", [128, 1])
        w2c = sb("w2c", [128, 128])
        b2b = sb("b2b", [128, 128])
        b2s = sb("b2s", [128, 1])
        b2c = sb("b2c", [128, 128])
        gab = sb("gab", [128, 128])
        beb = sb("beb", [128, 128])
        eps1 = sb("eps1", [128, 1])
        one1 = sb("one1", [128, 1])

        xts = sb("xts", [128, W])
        xm2 = sb("xm2", [128, W])
        adjt = sb("adjt", [128, W])
        adjs = sb("adjs", [128, W])
        sqx, bjs, esig, lse, den, nm, lnn, lnd, ls, uw, ucl, l1, l2, qe, q2e, w0, dl, w1, wt = (
            sb(n, [128, W]) for n in "sqx bjs esig lse den nm lnn lnd ls uw ucl l1 l2 qe q2e w0 dl w1 wt".split())
        xmp, sqm, tx, hh, x1s, x1t = (sb(n, [128, W]) for n in "xmp sqm tx hh x1s x1t".split())
        tiny = sb("tiny", [128, 64 * GB])
        tiny_names = """x2 bc bm x2m lpn pn pcl at1 at2 rpn dat fac lcol xmr mmr c1 cc al be ax bx xu t2 t3 t4 t5 t6
        uq uqm lun un rbm zz ez e1 re th run rho r2 s1 rxu tw nx de dec rd rr gg ga2 ga t7 t8 t9 vare lv rs ra rb rc
        rsn dg""".split()
        c = {n: tiny[:, GB * k:GB * (k + 1)] for k, n in enumerate(tiny_names)}
        vals = sb("vals", [128, ROWS])
        vv = vals[:, :].rearrange("p (b t) -> p t b", t=4)
        q1 = sb("q1", [128, ROWS])
        q2 = sb("q2", [128, ROWS])
        rowsb = sb("rowsb", [128, 128], BF16)
        rowst = sb("rowst", [PARTS * ROWS, 128], BF16)
        onex2 = sb("onex2", [128, 2 * GB])
        lrs = sb("lrs", [128, 2 * GB])
        sws = sb("sws", [128, 2 * GB])
        bns = sb("bns", [128, 6 * GB])
        mv = sb("mv", [128, 2 * GB])
        scan = sb("scan", [128, W])
        offc = sb("offc", [128, GB])
        bsq = sb("bsq", [128, W])
        bdiff = sb("bdiff", [128, W])

        tb = sb("tb", [128, GB, PARTS, 256], BF16)
        r1 = sb("r1", [128, 512])
        absd = sb("absd", [128, T], FP16)
        si = sb("si", [128, 3, T], BF16)
        sj = sb("sj", [128, 3, T], BF16)
        ies = sb("ies", [128, 3, CH])
        ht = sb("ht", [128, T])
        z = sb("z", [128, 3, T])
        sq = sb("sq", [128, T])
        ss = sb("ss", [128, 3, CH])
        lnv = sb("lnv", [128, 3, CH])
        rstd = sb("rstd", [128, 3, CH])
        sit = sb("sit", [128, 3, T])
        osb = sb("osb", [128, W])
        fin1 = sb("fin1", [128, W])
        fbns = sb("fbns", [128, 6 * GB])
        fmv = sb("fmv", [128, 2 * GB])
        ftiny = sb("ftiny", [128, 8 * GB])
        f = {n: ftiny[:, GB * k:GB * (k + 1)]
                               for k, n in enumerate("vare lv rs ra rb rc rsn".split())}
        fo = sb("fo", [128, W])
        okn = sb("okn", [128, NB])
        fl = sb("fl", [128, 8])
        flagi = sb("flagi", [128, 1], I32)

        g_x1, g_x1t, g_hi, g_hj = xts[:, 0:128], xts[:, 128:256], xts[:, 256:384], xts[:, 384:512]
        g_h, g_z, g_sq, g_o = xm2[:, 0:128], xm2[:, 128:256], xm2[:, 256:384], xm2[:, 384:512]
        g_adj, g_adjt, g_rows, g_out = adjs[:, 0:128], adjt[:, 0:128], sqx[:, 0:128], fo[:, 0:128]
        g_ss, g_lv, g_r, g_w, g_deg, g_var, g_lv2, g_rs = (fbns[:, k:k + 1] for k in range(8))
        g_tiny = dict(vare=g_var, rs=g_rs, ra=fbns[:, 8:9], rb=fbns[:, 9:10], rsn=fbns[:, 10:11])
        g_bns, g_mv = bns[:, 0:6], mv[:, 0:2]

        banks = [ctx.enter_context(nc.psum_tensor(f"bank{k}", [128, 512], F32)) for k in range(8)]
        vg_ps, h_ps, y_ps = (b[:, :] for b in banks[0:3])
        o_ps, ie_ps, off_ps = banks[3][:, 0:128], banks[3][:, 128:128 + CH], banks[3][:, 136:136 + GB]
        lg_ps = banks[4][:, :]
        d2_ps = banks[5][:, :]
        bj_ps = banks[6][:, :]
        lr_ps, rt_ps, sw_ps = banks[6][:, 0:8], banks[6][:, 64:128].bitcast(BF16), banks[6][:, 128:136]

        def grp(t, g, width=W):
            return t[:, bass.ds(g * width, width)]

        def bt(t, b, width=128):
            return t[:, bass.ds(b * width, width)]

        def cut(u):
            return slice(128 * u, 128 * (u + 1))

        def wide(a):
            return a.rearrange("p (b n) -> p b n", b=GB)

        def spread(col):
            return col.unsqueeze(2).to_broadcast([128, GB, 128])

        def settle(eng):
            eng.wait_ge(sem["ones"], 2)

        def where_dense(eng, body):
            eng.wait_ge(sem["flag"], 1)
            found = eng.value_load(flagi[0:1, 0:1], min_val=0, max_val=1)
            with eng.If(found > 0):
                body()

        def slot(k):
            return 0 if k == 0 else 1 + (k - 1) % 2

        def reuse(g, k):
            if first(g) and k < 3:
                return None
            return TILES * g + k - (5, 3, 3, 2, 2)[k] + 1

        def first(g):
            return isinstance(g, int) and g == 0

        block = ctx.enter_context(nc.Block())

        def run_groups(eng, body):
            body(0)
            if groups > 1:
                with eng.Fori(1, groups) as g:
                    body(g)

        @block.sync
        def _(sp):
            def load(dst, src):
                sp.dma_start(dst, src).then_inc(sem["const"], 16)

            load(cf[:, :], c_f32)
            load(ch[:, :], c_fp16)
            load(self_[:, :], c_sel)
            load(wlr[:, :], att_w)
            load(attb[:, :], att_b.partition_broadcast(128))
            load(w1c[:, :], W1)
            load(b1c[:, :], b1)
            load(w2[:, :], W2)
            load(b2b[:, :], b2.partition_broadcast(128))
            load(gab[:, :], gamma.partition_broadcast(128))
            load(beb[:, :], beta.partition_broadcast(128))

            def body(g):
                if not first(g):
                    sp.wait_ge(sem["loaded"], 16 * g)
                    sp.wait_ge(sem["d2"], g)
                    sp.wait_ge(sem["lr"], g)
                    sp.wait_ge(sem["xm2"], g)
                sp.dma_start(xts[:, :], grp(x_t, g)).then_inc(sem["xt_loaded"], 16)
                sp.dma_start(grp(x_all, g), grp(x_n, g)).then_inc(sem["loaded"], 16)
                if not first(g):
                    sp.wait_ge(sem["w1"], g)
                sp.dma_start(adjt[:, :], grp(adj_t, g)).then_inc(sem["adjt_loaded"], 16)
                if not first(g):
                    sp.wait_ge(sem["scan"], g)
                    sp.wait_ge(sem["vt"], g)
                    sp.wait_ge(sem["bdiff"], g)
                sp.dma_start(adjs[:, :], grp(adj_n, g)).then_inc(sem["adj_loaded"], 16)

            run_groups(sp, body)

            def dense():
                sp.wait_ge(sem["stored"], 16 * groups)
                sp.dma_start(g_out, bt(out, 0)).then_inc(sem["dense_stored"], 16)
                with sp.Fori(0, NB) as b:
                    sp.dma_start(g_adj, bt(adj_n, b)).then_inc(sem["dense_loaded"], 16)
                    sp.dma_start(g_adjt, bt(adj_t, b)).then_inc(sem["dense_loaded"], 16)
                    settle(sp)
                    sp.wait_ge(sem["dense_out"], b + 1)
                    sp.dma_start(bt(out, b), g_out).then_inc(sem["dense_stored"], 16)
                sp.wait_ge(sem["dense_stored"], 16 * NB + 16)

            where_dense(sp, dense)

        @block.gpsimd
        def _(pool):
            tt = nc.gpsimd.tensor_tensor

            def badness(g):
                pool.wait_ge(sem["adj_loaded"], 16 * g + 16)
                tt(bsq[:, :], adjs[:, :], adjs[:, :], ALU.mult).then_inc(sem["bsq"], 1)
                pool.wait_ge(sem["bsq"], g + 1)
                if not first(g):
                    pool.wait_ge(sem["bad"], g)
                tt(bdiff[:, :], bsq[:, :], adjs[:, :], ALU.subtract).then_inc(sem["bdiff"], 1)

            def weights(g):
                pool.wait_ge(sem["qe"], g + 1)
                pool.wait_ge(sem["lse"], g + 1)
                tt(q2e[:, :], qe[:, :], lse[:, :], ALU.add).then_inc(sem["q2e"], 1)
                pool.wait_ge(sem["l1"], g + 1)
                pool.wait_ge(sem["l2"], g + 1)
                tt(dl[:, :], l1[:, :], l2[:, :], ALU.subtract).then_inc(sem["dl"], 1)
                settle(pool)
                pool.wait_ge(sem["dl"], g + 1)
                pool.wait_ge(sem["adjt_loaded"], 16 * g + 16)
                tt(w1[:, :], dl[:, :], adjt[:, :], ALU.mult).then_inc(sem["w1"], 1)
                pool.wait_ge(sem["w1"], g + 1)
                pool.wait_ge(sem["w0"], g + 1)
                if not first(g):
                    pool.wait_ge(sem["mm"], g)
                    pool.wait_ge(sem["sw"], g)
                tt(wt[:, :], w1[:, :], w0[:, :], ALU.mult).then_inc(sem["wt"], 1)

            def h_part(g):
                settle(pool)
                pool.wait_ge(sem["ga"], g + 1)
                tt(wide(tx[:, :]), wide(grp(x_all, g)), spread(c["ga"]), ALU.mult).then_inc(sem["tx"], 1)

            def keep_x1(g):
                settle(pool)
                pool.wait_ge(sem["x1s"], g + 1)
                nc.gpsimd.tensor_copy(grp(x1_all, g), x1s[:, :]).then_inc(sem["x1a"], 1)

            def finish(g):
                settle(pool)
                if not first(g):
                    pool.wait_ge(sem["fbns"], g)
                    pool.wait_ge(sem["fout"], g)
                pool.wait_ge(sem["dega"], 2 * g + 2)
                pool.wait_ge(sem["const"], 16 * 11)
                tt(wide(fin1[:, :]), beb[:, :].unsqueeze(1).to_broadcast([128, GB, 128]),
                   spread(bt(deg_all, g, GB)), ALU.mult).then_inc(sem["fin1"], 1)
                pool.wait_ge(sem["fin1"], g + 1)
                pool.wait_ge(sem["e_osb"], GB * g + GB)
                tt(fin1[:, :], fin1[:, :], osb[:, :], ALU.add).then_inc(sem["fin2"], 1)
                settle(pool)
                pool.wait_ge(sem["fin2"], g + 1)
                pool.wait_ge(sem["x1a"], g + 1)
                tt(fin1[:, :], fin1[:, :], grp(x1_all, g), ALU.add).then_inc(sem["fin3"], 1)

            def body(g):
                badness(g)
                weights(g)
                h_part(g)
                keep_x1(g)
                finish(g)

            run_groups(pool, body)

        @block.scalar
        def _(act):
            fn = nc.scalar.activation

            nc.scalar.preload_act_table_set("natural_log_exp_and_others")
            act.wait_ge(sem["const"], 16 * 11)
            act.wait_ge(sem["ones"], 1)
            fn(selb[:, :], self_[:, :], ACT.Copy).then_inc(sem["selb"], 1)
            fn(identb[:, :], ident, ACT.Copy).then_inc(sem["selb"], 1)
            fn(colb[:, :], col_i1, ACT.Copy).then_inc(sem["selb"], 1)

            def l0_a(g):
                act.wait_ge(sem["xt_loaded"], 16 * g + 16)
                if not first(g):
                    act.wait_ge(sem["d2"], g)
                fn(xm2[:, :], xts[:, :], ACT.Copy, scale=-2.0).then_inc(sem["xm2"], 1)
                settle(act)
                act.wait_ge(sem["loaded"], 16 * g + 16)
                if not first(g):
                    act.wait_ge(sem["x2"], g)
                fn(sqx[:, :], grp(x_all, g), ACT.Square).then_inc(sem["sqx"], 1)
                act.wait_ge(sem["x2m"], g + 1)
                fn(c["lpn"], c["x2m"], ACT.Ln).then_inc(sem["lpn"], 1)
                act.wait_ge(sem["lpn"], g + 1)
                fn(c["pn"], c["lpn"], ACT.Exp, scale=0.5).then_inc(sem["pn"], 1)
                act.wait_ge(sem["pcl"], g + 1)
                fn(c["at1"], c["pcl"], ACT.Ln, bias=one1[:, :]).then_inc(sem["at1"], 1)
                fn(c["at2"], c["pcl"], ACT.Ln, bias=one1[:, :], scale=-1.0).then_inc(sem["at2"], 1)

            def l0_rows(g):
                act.wait_ge(sem["rowst_ps"], g + 1)
                if not first(g):
                    act.wait_ge(sem["d2"], g)
                    act.wait_ge(sem["bj_ps"], g)
                    act.wait_ge(sem["lg"], g)
                fn(rowst[:, :], rt_ps[0:PARTS * ROWS, :], ACT.Copy).then_inc(sem["rowst"], 1)

            def l0_b(g):
                act.wait_ge(sem["bj_ps"], g + 1)
                if not first(g):
                    act.wait_ge(sem["den"], g)
                fn(bjs[:, :], bj_ps, ACT.Copy).then_inc(sem["bjs"], 1)
                act.wait_ge(sem["lg"], g + 1)
                if not first(g):
                    act.wait_ge(sem["q2e"], g)
                fn(esig[:, :], lg_ps, ACT.Exp, scale=-1.0).then_inc(sem["esig"], 1)
                act.wait_ge(sem["esigc"], g + 1)
                fn(lse[:, :], esig[:, :], ACT.Ln, bias=one1[:, :]).then_inc(sem["lse"], 1)

            def l0_c(g):
                act.wait_ge(sem["nm"], g + 1)
                fn(lnn[:, :], nm[:, :], ACT.Ln).then_inc(sem["lnn"], 1)
                act.wait_ge(sem["denc"], g + 1)
                fn(lnd[:, :], den[:, :], ACT.Ln).then_inc(sem["lnd"], 1)

            def l0_d(g):
                act.wait_ge(sem["lsc"], g + 1)
                fn(uw[:, :], ls[:, :], ACT.Exp, scale=0.5).then_inc(sem["uu"], 1)
                act.wait_ge(sem["ucl"], g + 1)
                if not first(g):
                    act.wait_ge(sem["dl"], g)
                fn(l1[:, :], ucl[:, :], ACT.Ln, bias=one1[:, :]).then_inc(sem["l1"], 1)
                fn(l2[:, :], ucl[:, :], ACT.Ln, bias=one1[:, :], scale=-1.0).then_inc(sem["l2"], 1)
                act.wait_ge(sem["q2e"], g + 1)
                if not first(g):
                    act.wait_ge(sem["wt"], g)
                fn(w0[:, :], q2e[:, :], ACT.Exp, scale=-1.0).then_inc(sem["w0"], 1)

            def l0_e(g):
                act.wait_ge(sem["sw"], g + 1)
                if not first(g):
                    act.wait_ge(sem["rows"], ROW_STEPS * g - ROW_STEPS + 1)
                fn(sws[:, :], sw_ps, ACT.Copy).then_inc(sem["sws"], 1)
                act.wait_ge(sem["xmp"], g + 1)
                fn(sqm[:, :], d2_ps, ACT.Square).then_inc(sem["sqm"], 1)
                act.wait_ge(sem["uqm"], g + 1)
                fn(c["lun"], c["uqm"], ACT.Ln).then_inc(sem["lun"], 1)
                act.wait_ge(sem["lun"], g + 1)
                fn(c["un"], c["lun"], ACT.Exp, scale=0.5).then_inc(sem["un"], 1)
                act.wait_ge(sem["zz"], g + 1)
                fn(c["ez"], c["zz"], ACT.Exp, scale=2.0).then_inc(sem["ez"], 1)

            def l0_f(g):
                act.wait_ge(sem["vare"], g + 1)
                fn(c["lv"], c["vare"], ACT.Ln).then_inc(sem["lv"], 1)
                act.wait_ge(sem["lv"], g + 1)
                fn(c["rs"], c["lv"], ACT.Exp, scale=-0.5).then_inc(sem["rs"], 1)
                act.wait_ge(sem["x1t_ps"], g + 1)
                if not first(g):
                    act.wait_ge(sem["e_tab"], 2 * g)
                fn(x1t[:, :], lg_ps, ACT.Copy).then_inc(sem["x1t"], 1)

            def bad(g):
                settle(act)
                act.wait_ge(sem["bdiff"], g + 1)
                fn(bdiff[:, :], bdiff[:, :], ACT.Abs, accum_out=bt(bad_all, g, 1)).then_inc(sem["bad"], 1)

            def split0(g, half):
                act.wait_ge(sem["e_tab"], 2 * g + half + 1)
                if not first(g):
                    act.wait_ge(sem["e_hps"], TILES * g)
                fn(tb[:, 2 * half:2 * half + 2, 0, :], lg_ps.rearrange("p (b k) -> p b k", b=2),
                   ACT.Copy).then_inc(sem["e_t0"], 1)

            def split1(g, half):
                act.wait_ge(sem["e_r1"], 2 * g + half + 1)
                fn(tb[:, 2 * half:2 * half + 2, 1, :], r1[:, :].rearrange("p (b k) -> p b k", b=2),
                   ACT.Copy).then_inc(sem["e_t1"], 1)

            def distance(g, k):
                q = TILES * g + k
                settle(act)
                act.wait_ge(sem["mid"], g + 1)
                if not (first(g) and k == 0):
                    act.wait_ge(sem["e_si"], q)
                if k == 0:
                    for u in range(GB):
                        last = fn(absd[:, cut(u)], iota_e[:, T:CAP], ACT.Abs, bias=bt(mid_all, GB * g + u, 1), scale=-1.0)
                else:
                    last = fn(absd[:, :], iota_e[:, 0:T], ACT.Abs, bias=bt(mid_all, GB * g + k - 1, 1), scale=-1.0)
                last.then_inc(sem["e_absd"], 1)

            def relu(g, k):
                q = TILES * g + k
                act.wait_ge(sem["e_hps"], q + 1)
                if not (first(g) and k == 0):
                    act.wait_ge(sem["e_yps"], q)
                fn(ht[:, :], h_ps, ACT.Relu, bias=b1c[:, :]).then_inc(sem["e_ht"], 1)

            def square(g, k):
                q = TILES * g + k
                act.wait_ge(sem["e_z"], q + 1)
                if not (first(g) and k == 0):
                    act.wait_ge(sem["e_ss"], q)
                fn(sq[:, :], z[:, slot(k), :], ACT.Square).then_inc(sem["e_sq"], 1)

            def inv_std(g, k):
                q, s = TILES * g + k, slot(k)
                act.wait_ge(sem["e_ss"], q + 1)
                fn(lnv[:, s, :], ss[:, s, :], ACT.Ln, scale=1.0 / D, bias=eps1[:, :]).then_inc(sem["e_lnv"], 1)
                act.wait_ge(sem["e_lnv"], q + 1)
                if reuse(g, k) is not None:
                    act.wait_ge(sem["e_sit"], reuse(g, k))
                fn(rstd[:, s, :], lnv[:, s, :], ACT.Exp, scale=-0.5).then_inc(sem["e_rstd"], 1)

            def finish(g):
                act.wait_ge(sem["fvare"], g + 1)
                fn(f["lv"], f["vare"], ACT.Ln).then_inc(sem["flv"], 1)
                act.wait_ge(sem["flv"], g + 1)
                fn(f["rs"], f["lv"], ACT.Exp, scale=-0.5).then_inc(sem["frs"], 1)
                act.wait_ge(sem["fout"], g + 1)
                act.dma_start(grp(out, g), fo[:, :]).then_inc(sem["stored"], 16)

            def body(g):
                l0_a(g)
                l0_rows(g)
                l0_b(g)
                l0_c(g)
                l0_d(g)
                l0_e(g)
                bad(g)
                l0_f(g)
                for half in range(2):
                    split0(g, half)
                    split1(g, half)
                for k in range(TILES):
                    distance(g, k)
                    relu(g, k)
                    square(g, k)
                    inv_std(g, k)
                finish(g)

            run_groups(act, body)
            act.wait_ge(sem["stored"], 16 * groups)

            def dense():
                with act.Fori(0, NB) as b:
                    act.wait_ge(sem["dense_loaded"], 32 * b + 32)
                    fn(g_x1, bt(x1_all, b), ACT.Copy).then_inc(sem["dense_x1"], 1)
                    act.wait_ge(sem["dense_x1t_ps"], b + 1)
                    fn(g_x1t, lg_ps[:, 0:128], ACT.Copy).then_inc(sem["dense_x1t"], 1)
                    act.wait_ge(sem["dense_hps"], b + 1)
                    fn(g_hi, h_ps[:, 0:128], ACT.Identity, bias=b1c[:, :]).then_inc(sem["dense_hidden_ready"], 1)
                    fn(g_hj, h_ps[:, 128:256], ACT.Copy).then_inc(sem["dense_hidden_ready"], 1)
                    with act.Fori(0, N) as i:
                        q = N * b + i
                        act.wait_ge(sem["dense_z"], q + 1)
                        fn(g_sq, g_z, ACT.Square, accum_out=g_ss).then_inc(sem["dense_sq"], 1)
                        act.wait_ge(sem["dense_sq"], q + 1)
                        fn(g_lv, g_ss, ACT.Ln, scale=1.0 / D, bias=eps1[:, :]).then_inc(sem["dense_lv"], 1)
                        act.wait_ge(sem["dense_lv"], q + 1)
                        fn(g_r, g_lv, ACT.Exp, scale=-0.5).then_inc(sem["dense_r"], 1)
                        settle(act)
                        act.wait_ge(sem["dense_o"], q + 1)
                        fn(g_o[:, bass.ds(i, 1)], o_ps[:, 0:1], ACT.Copy).then_inc(sem["dense_hidden_ready"], 1)
                    act.wait_ge(sem["dense_var"], b + 1)
                    fn(g_lv2, g_var, ACT.Ln).then_inc(sem["dense_lv2"], 1)
                    act.wait_ge(sem["dense_lv2"], b + 1)
                    fn(g_rs, g_lv2, ACT.Exp, scale=-0.5).then_inc(sem["dense_rs"], 1)

            where_dense(act, dense)

        @block.vector
        def _(dve):
            v = nc.vector
            tt, ts, stt = v.tensor_tensor, v.tensor_scalar, v.scalar_tensor_tensor

            v.memset(one1[:, :], 1.0).then_inc(sem["ones"], 1)
            v.memset(eps1[:, :], LN_EPS)
            v.memset(rowsb[:, :], 0.0)
            v.memset(onex2[:, :], 1.0).then_inc(sem["ones"], 1)
            dve.wait_ge(sem["const"], 16 * 11)
            dve.wait_ge(sem["ones"], 2)
            v.tensor_reduce(w2s[:, :], w2[:, :], AX_X, ALU.add).then_inc(sem["w2sum"], 1)
            v.tensor_reduce(b2s[:, :], b2b[:, :], AX_X, ALU.add).then_inc(sem["b2sum"], 1)
            dve.wait_ge(sem["w2sum"], 1)
            ts(w2s[:, :], w2s[:, :], -1.0 / D, None, ALU.mult).then_inc(sem["w2sum"], 1)
            dve.wait_ge(sem["b2sum"], 1)
            ts(b2s[:, :], b2s[:, :], -1.0 / D, None, ALU.mult).then_inc(sem["b2sum"], 1)
            dve.wait_ge(sem["w2sum"], 2)
            ts(w2c[:, :], w2[:, :], w2s[:, :], None, ALU.add).then_inc(sem["w2c"], 1)
            dve.wait_ge(sem["b2sum"], 2)
            ts(b2c[:, :], b2b[:, :], b2s[:, :], None, ALU.add).then_inc(sem["b2c"], 1)
            dve.wait_ge(sem["b2c"], 1)

            class Chain:

                def __init__(self, sem_, steps):
                    self.sem, self.steps = sem_, steps

                def start(self, g):
                    self.base, self.k = g * self.steps, 0

                def __call__(self, ins):
                    self.k += 1
                    ins.then_inc(self.sem, 1)
                    dve.wait_ge(self.sem, self.base + self.k)

                def end(self):
                    assert self.k == self.steps, self.k

            cols, rows, frows = Chain(sem["cols"], COL_STEPS), Chain(sem["rows"], ROW_STEPS), Chain(sem["frows"], 3)

            def x_col(g):
                cols.start(g)
                dve.wait_ge(sem["sqx"], g + 1)
                v.tensor_reduce(c["x2"], wide(sqx[:, :]), AX_X, ALU.add).then_inc(sem["x2"], 1)
                dve.wait_ge(sem["x2"], g + 1)
                ts(c["x2m"], c["x2"], MIN_NORM, None, ALU.max).then_inc(sem["x2m"], 1)
                if not first(g):
                    dve.wait_ge(sem["sw"], g)
                ts(onex2[:, 1:2 * GB:2], c["x2"], 1.0, None, ALU.mult).then_inc(sem["xcol"], 1)
                cols(ts(c["bc"], c["x2"], -1.0, 1.0, ALU.mult, ALU.add))
                cols(ts(vv[:, X2, :], c["x2"], 1.0, None, ALU.mult))
                cols(ts(c["bm"], c["bc"], MIN_NORM, None, ALU.max))
                cols(ts(vv[:, BB, :], c["bc"], 1.0, None, ALU.mult))
                dve.wait_ge(sem["pn"], g + 1)
                ts(c["pcl"], c["pn"], CLIP, None, ALU.min).then_inc(sem["pcl"], 1)
                cols(v.reciprocal(c["rpn"], c["pn"]))
                dve.wait_ge(sem["at1"], g + 1)
                dve.wait_ge(sem["at2"], g + 1)
                cols(tt(c["dat"], c["at1"], c["at2"], ALU.subtract))
                cols(stt(c["fac"], c["dat"], 0.5, c["rpn"], ALU.mult, ALU.mult))
                dve.wait_ge(sem["lr"], g + 1)
                tt(c["lcol"], lr_ps[:, 0:2 * GB:2], c["fac"], ALU.mult).then_inc(sem["lrc"], 1)
                tt(vv[:, RR, :], lr_ps[:, 1:2 * GB:2], c["fac"], ALU.mult).then_inc(sem["lrc"], 1)
                dve.wait_ge(sem["lrc"], 2 * g + 2)
                cols(ts(vv[:, LL, :], c["lcol"], attb[:, :], None, ALU.add))

            def split_rows(g):
                if not first(g):
                    dve.wait_ge(sem["rowst_ps"], g)
                cols(ts(rowsb[:, 0:ROWS], vals[:, :], 1.0, None, ALU.mult))
                cols(tt(q1[:, :], vals[:, :], rowsb[:, 0:ROWS], ALU.subtract))
                cols(ts(rowsb[:, ROWS:2 * ROWS], q1[:, :], 1.0, None, ALU.mult))
                cols(tt(q2[:, :], q1[:, :], rowsb[:, ROWS:2 * ROWS], ALU.subtract))
                cols(v.reciprocal(c["rbm"], c["bm"]))
                ts(rowsb[:, 2 * ROWS:3 * ROWS], q2[:, :], 1.0, None, ALU.mult).then_inc(sem["rowsb"], 1)
                cols.end()

            def pairs_a(g):
                dve.wait_ge(sem["esig"], g + 1)
                ts(esig[:, :], esig[:, :], SIG_MAX, None, ALU.min).then_inc(sem["esigc"], 1)
                dve.wait_ge(sem["d2"], g + 1)
                if not first(g):
                    dve.wait_ge(sem["lnn"], g)
                    dve.wait_ge(sem["lnd"], g)
                ts(nm[:, :], d2_ps, TINY, None, ALU.max).then_inc(sem["nm"], 1)
                dve.wait_ge(sem["bjs"], g + 1)
                for u in range(GB):
                    last = stt(den[:, cut(u)], bjs[:, cut(u)], c["bc"][:, u:u + 1], d2_ps[:, cut(u)], ALU.mult, ALU.add)
                last.then_inc(sem["den"], 1)
                dve.wait_ge(sem["den"], g + 1)
                ts(den[:, :], den[:, :], MIN_NORM, None, ALU.max).then_inc(sem["denc"], 1)

            def pairs_b(g):
                dve.wait_ge(sem["lnn"], g + 1)
                dve.wait_ge(sem["lnd"], g + 1)
                tt(ls[:, :], lnn[:, :], lnd[:, :], ALU.subtract).then_inc(sem["ls"], 1)
                dve.wait_ge(sem["ls"], g + 1)
                ts(ls[:, :], ls[:, :], LOG_MIN_NORM, None, ALU.max).then_inc(sem["lsc"], 1)
                dve.wait_ge(sem["lsc"], g + 1)
                if not first(g):
                    dve.wait_ge(sem["q2e"], g)
                stt(qe[:, :], ls[:, :], 0.5, lnd[:, :], ALU.mult, ALU.add).then_inc(sem["qe"], 1)
                dve.wait_ge(sem["uu"], g + 1)
                ts(ucl[:, :], uw[:, :], CLIP, None, ALU.min).then_inc(sem["ucl"], 1)

            def rows_a(g):
                rows.start(g)
                dve.wait_ge(sem["mm"], g + 1)
                tt(xmp[:, :], d2_ps, grp(x_all, g), ALU.mult).then_inc(sem["xmp"], 1)
                dve.wait_ge(sem["sws"], g + 1)
                rows(tt(c["c1"], sws[:, 0:2 * GB:2], sws[:, 1:2 * GB:2], ALU.add))
                rows(stt(c["be"], c["bc"], 0.5, c["bm"], ALU.mult, ALU.mult))
                dve.wait_ge(sem["xmp"], g + 1)
                rows(v.tensor_reduce(c["xmr"], wide(xmp[:, :]), AX_X, ALU.add))
                rows(stt(c["cc"], c["xmr"], -2.0, c["c1"], ALU.mult, ALU.add))
                rows(stt(c["al"], c["cc"], -0.5, c["bm"], ALU.mult, ALU.mult))
                dve.wait_ge(sem["sqm"], g + 1)
                rows(v.tensor_reduce(c["mmr"], wide(sqm[:, :]), AX_X, ALU.add))
                rows(tt(c["bx"], c["be"], c["xmr"], ALU.mult))
                rows(tt(c["ax"], c["al"], c["x2"], ALU.mult))
                rows(tt(c["xu"], c["ax"], c["bx"], ALU.add))
                rows(tt(c["t2"], c["al"], c["xu"], ALU.mult))
                rows(tt(c["t3"], c["al"], c["xmr"], ALU.mult))
                rows(tt(c["t4"], c["be"], c["mmr"], ALU.mult))
                rows(tt(c["t5"], c["t3"], c["t4"], ALU.add))
                rows(tt(c["t6"], c["be"], c["t5"], ALU.mult))
                rows(tt(c["uq"], c["t2"], c["t6"], ALU.add))
                ts(c["uqm"], c["uq"], MIN_NORM, None, ALU.max).then_inc(sem["uqm"], 1)

            def rows_b(g):
                dve.wait_ge(sem["un"], g + 1)
                tt(c["zz"], c["un"], c["rbm"], ALU.mult).then_inc(sem["zz"], 1)
                rows(v.reciprocal(c["run"], c["un"]))
                dve.wait_ge(sem["ez"], g + 1)
                rows(ts(c["e1"], c["ez"], 1.0, None, ALU.add))
                rows(v.reciprocal(c["re"], c["e1"]))
                rows(ts(c["th"], c["re"], -2.0, 1.0, ALU.mult, ALU.add))
                rows(tt(c["rho"], c["th"], c["run"], ALU.mult))
                rows(tt(c["r2"], c["rho"], c["rho"], ALU.mult))
                rows(tt(c["s1"], c["r2"], c["uqm"], ALU.mult))
                rows(tt(c["rxu"], c["rho"], c["xu"], ALU.mult))
                rows(ts(c["tw"], c["rxu"], 2.0, 1.0, ALU.mult, ALU.add))
                rows(tt(c["nx"], c["tw"], c["s1"], ALU.add))
                rows(tt(c["t7"], c["x2"], c["s1"], ALU.mult))
                rows(tt(c["de"], c["t7"], c["tw"], ALU.add))
                rows(ts(c["dec"], c["de"], MIN_NORM, None, ALU.max))
                rows(v.reciprocal(c["rd"], c["dec"]))
                rows(tt(c["rr"], c["rd"], c["rho"], ALU.mult))
                rows(tt(c["gg"], c["rr"], c["bc"], ALU.mult))
                rows(tt(c["ga2"], c["gg"], c["be"], ALU.mult))
                rows(tt(c["t8"], c["gg"], c["al"], ALU.mult))
                rows(tt(c["t9"], c["rd"], c["nx"], ALU.mult))
                stt(c["ga"], c["t8"], 1.0, c["t9"], ALU.add, ALU.add).then_inc(sem["ga"], 1)

            def newton(w, chain):
                chain(tt(w["ra"], w["rs"], w["rs"], ALU.mult))
                chain(stt(w["rb"], w["ra"], -0.5, w["vare"], ALU.mult, ALU.mult))
                chain(stt(w["rsn"], w["rb"], 1.5, w["rs"], ALU.add, ALU.mult))
                chain.end()

            def norm0_a(g):
                dve.wait_ge(sem["tx"], g + 1)
                dve.wait_ge(sem["sqm"], g + 1)
                for u in range(GB):
                    last = stt(hh[:, cut(u)], d2_ps[:, cut(u)], c["ga2"][:, u:u + 1], tx[:, cut(u)], ALU.mult, ALU.add)
                last.then_inc(sem["hh"], 1)
                dve.wait_ge(sem["hh"], g + 1)
                for u in range(GB):
                    last = v.bn_stats(bns[:, 6 * u:6 * u + 6], hh[:, cut(u)])
                last.then_inc(sem["bns"], 1)
                settle(dve)
                dve.wait_ge(sem["bns"], g + 1)
                for u in range(GB):
                    last = v.bn_aggr(mv[:, 2 * u:2 * u + 2], bns[:, 6 * u:6 * u + 6])
                last.then_inc(sem["bna"], 1)
                dve.wait_ge(sem["bna"], g + 1)
                ts(c["vare"], mv[:, 1:2 * GB:2], LN_EPS, None, ALU.add).then_inc(sem["vare"], 1)

            def norm0_b(g):
                dve.wait_ge(sem["rs"], g + 1)
                newton(c, rows)
                if not first(g):
                    dve.wait_ge(sem["x1t_ps"], g)
                    dve.wait_ge(sem["x1a"], g)
                for u in range(GB):
                    last = ts(x1s[:, cut(u)], hh[:, cut(u)], mv[:, 2 * u:2 * u + 1], c["rsn"][:, u:u + 1],
                              ALU.subtract, ALU.mult)
                last.then_inc(sem["x1s"], 1)

            def ranks_a(g):
                dve.wait_ge(sem["adj_loaded"], 16 * g + 16)
                v.tensor_tensor_scan(scan[:, :], reset, adjs[:, :], 0.0, ALU.mult, ALU.add).then_inc(sem["scan"], 1)
                dve.wait_ge(sem["scan"], g + 1)
                if not first(g):
                    dve.wait_ge(sem["off"], g)
                ts(c["dg"], scan[:, 127:W:128], 1.0, None, ALU.mult).then_inc(sem["degs"], 1)
                dve.wait_ge(sem["degs"], g + 1)
                ts(bt(deg_all, g, GB), c["dg"], 1.0, None, ALU.mult).then_inc(sem["dega"], 1)
                ts(bt(half_all, g, GB), c["dg"], 0.5, -0.5, ALU.mult, ALU.add).then_inc(sem["dega"], 1)

            def ranks_b(g):
                dve.wait_ge(sem["off"], g + 1)
                ts(offc[:, :], off_ps, 1.0, None, ALU.mult).then_inc(sem["offc"], 1)
                dve.wait_ge(sem["offc"], g + 1)
                dve.wait_ge(sem["dega"], 2 * g + 2)
                tt(bt(mid_all, g, GB), offc[:, :], bt(half_all, g, GB), ALU.add).then_inc(sem["mid"], 1)
                for u in range(GB):
                    last = stt(bt(vt_all, GB * g + u), scan[:, cut(u)], offc[:, u:u + 1], adjs[:, cut(u)],
                               ALU.add, ALU.mult)
                last.then_inc(sem["vt"], 1)
                dve.wait_ge(sem["mid"], g + 1)

            def split_r1(g, half):
                dve.wait_ge(sem["e_t0"], 2 * g + half + 1)
                if not (first(g) and half == 0):
                    dve.wait_ge(sem["e_t1"], 2 * g + half)
                    dve.wait_ge(sem["e_t2b"], 2 * g + half)
                tt(r1[:, :].rearrange("p (b k) -> p b k", b=2), lg_ps.rearrange("p (b k) -> p b k", b=2),
                   tb[:, 2 * half:2 * half + 2, 0, :], ALU.subtract).then_inc(sem["e_r1"], 1)

            def split_t2(g, half):
                dve.wait_ge(sem["e_t1"], 2 * g + half + 1)
                tt(tb[:, 2 * half:2 * half + 2, 2, :], r1[:, :].rearrange("p (b k) -> p b k", b=2),
                   tb[:, 2 * half:2 * half + 2, 1, :], ALU.subtract).then_inc(sem["e_t2b"], 1)

            def row_hot(g, k):
                q, s = TILES * g + k, slot(k)
                dve.wait_ge(sem["e_absd"], q + 1)
                if reuse(g, k) is not None:
                    dve.wait_ge(sem["e_hps"], reuse(g, k))
                    dve.wait_ge(sem["e_ie"], reuse(g, k))
                if k == 0:
                    for u in range(GB):
                        last = ts(si[:, s, cut(u)], absd[:, cut(u)], bt(half_all, GB * g + u, 1), None, ALU.is_le)
                else:
                    last = ts(si[:, s, :], absd[:, :], bt(half_all, GB * g + k - 1, 1), None, ALU.is_le)
                last.then_inc(sem["e_si"], 1)

            def col_hot(g, k):
                q, s = TILES * g + k, slot(k)
                dve.wait_ge(sem["e_vg"], q + 1)
                if reuse(g, k) is not None:
                    dve.wait_ge(sem["e_hps"], reuse(g, k))
                tt(sj[:, s, :], vg_ps, rank_tail if k == 0 else rank_main, ALU.is_equal).then_inc(sem["e_sj"], 1)

            def ie_copy(g, k):
                q, s = TILES * g + k, slot(k)
                dve.wait_ge(sem["e_ie"], q + 1)
                ts(ies[:, s, :], ie_ps, 1.0, None, ALU.mult).then_inc(sem["e_ies"], 1)

            def add_b2(g, k):
                q, s = TILES * g + k, slot(k)
                dve.wait_ge(sem["e_yps"], q + 1)
                if reuse(g, k) is not None:
                    dve.wait_ge(sem["e_ops"], GB * g if k == 0 else GB * g + k - 1 - (0, 2, 2, 2, 2)[k] + 1)
                    dve.wait_ge(sem["e_sq"], reuse(g, k))
                tt(z[:, s, :].rearrange("p (c l) -> p c l", c=CH), y_ps.rearrange("p (c l) -> p c l", c=CH),
                   b2c[:, :].unsqueeze(1).to_broadcast([128, CH, 128]), ALU.add).then_inc(sem["e_z"], 1)

            def sum_sq(g, k):
                q, s = TILES * g + k, slot(k)
                dve.wait_ge(sem["e_sq"], q + 1)
                if reuse(g, k) is not None:
                    dve.wait_ge(sem["e_lnv"], reuse(g, k))
                v.tensor_reduce(ss[:, s, :], sq[:, :].rearrange("p (c l) -> p c l", c=CH), AX_X,
                                ALU.add).then_inc(sem["e_ss"], 1)

            def row_hot_t(g, k):
                q, s = TILES * g + k, slot(k)
                dve.wait_ge(sem["e_rstd"], q + 1)
                dve.wait_ge(sem["e_ies"], q + 1)
                if reuse(g, k) is not None:
                    dve.wait_ge(sem["e_ops"], GB * g if k == 0 else GB * g + k - 1 - (0, 2, 2, 2, 2)[k] + 1)
                for n in range(CH):
                    last = ts(sit[:, s, cut(n)], iota_i1, ies[:, s, n:n + 1], rstd[:, s, n:n + 1],
                              ALU.is_equal, ALU.mult)
                last.then_inc(sem["e_sit"], 1)

            def gamma_out(g, u):
                dve.wait_ge(sem["e_ops"], GB * g + u + 1)
                if not first(g):
                    dve.wait_ge(sem["fin2"], g)
                tt(osb[:, cut(u)], o_ps, gab[:, :], ALU.mult).then_inc(sem["e_osb"], 1)

            def finish_a(g):
                dve.wait_ge(sem["fin3"], g + 1)
                for u in range(GB):
                    last = v.bn_stats(fbns[:, 6 * u:6 * u + 6], fin1[:, cut(u)])
                last.then_inc(sem["fbns"], 1)
                settle(dve)
                dve.wait_ge(sem["fbns"], g + 1)
                for u in range(GB):
                    last = v.bn_aggr(fmv[:, 2 * u:2 * u + 2], fbns[:, 6 * u:6 * u + 6])
                last.then_inc(sem["fbna"], 1)
                dve.wait_ge(sem["fbna"], g + 1)
                ts(f["vare"], fmv[:, 1:2 * GB:2], LN_EPS, None, ALU.add).then_inc(sem["fvare"], 1)

            def finish_b(g):
                frows.start(g)
                dve.wait_ge(sem["frs"], g + 1)
                newton(f, frows)
                if not first(g):
                    dve.wait_ge(sem["stored"], 16 * g)
                for u in range(GB):
                    last = ts(fo[:, cut(u)], fin1[:, cut(u)], fmv[:, 2 * u:2 * u + 1], f["rsn"][:, u:u + 1],
                              ALU.subtract, ALU.mult)
                last.then_inc(sem["fout"], 1)

            def body(g):
                x_col(g)
                split_rows(g)
                pairs_a(g)
                pairs_b(g)
                rows_a(g)
                rows_b(g)
                norm0_a(g)
                norm0_b(g)
                ranks_a(g)
                ranks_b(g)
                for half in range(2):
                    split_r1(g, half)
                    split_t2(g, half)
                for k in range(TILES):
                    row_hot(g, k)
                    col_hot(g, k)
                    ie_copy(g, k)
                    add_b2(g, k)
                    sum_sq(g, k)
                    row_hot_t(g, k)
                    if k > 0:
                        gamma_out(g, k - 1)
                finish_a(g)
                finish_b(g)

            run_groups(dve, body)

            dve.wait_ge(sem["bad"], groups)
            v.tensor_reduce(fl[:, 0:1], bad_all[:, 0:groups], AX_X, ALU.add).then_inc(sem["badr"], 1)
            dve.wait_ge(sem["nall"], 2)
            ts(okn[:, 0:GB * groups], y_ps[:, 0:GB * groups], float(CAP), None, ALU.is_le).then_inc(sem["okn"], 1)
            ts(fl[:, 1:2], y_ps[:, 128:129], 0.0, None, ALU.is_le).then_inc(sem["badn"], 1)
            dve.wait_ge(sem["okn"], 1)
            v.tensor_reduce(fl[:, 2:3], okn[:, 0:GB * groups], AX_X, ALU.min).then_inc(sem["okm"], 1)
            dve.wait_ge(sem["okm"], 1)
            dve.wait_ge(sem["badn"], 1)
            tt(fl[:, 3:4], fl[:, 1:2], fl[:, 2:3], ALU.mult).then_inc(sem["flagf"], 1)
            dve.wait_ge(sem["flagf"], 1)
            dve.wait_ge(sem["e_osb"], GB * groups)
            ts(flagi[:, :], fl[:, 3:4], -1.0, 1.0, ALU.mult, ALU.add).then_inc(sem["flag"], 1)

            def dense():
                drows = Chain(sem["dense_rows"], DENSE_ROW_STEPS)
                with dve.Fori(0, NB) as b:
                    with dve.Fori(0, N) as i:
                        q = N * b + i
                        settle(dve)
                        dve.wait_ge(sem["dense_hidden_ready"], (N + 2) * b + i + 2)
                        ts(g_h, g_hj, g_hi[:, bass.ds(i, 1)], 0.0, ALU.add, ALU.max).then_inc(sem["dense_h"], 1)
                        dve.wait_ge(sem["dense_y"], q + 1)
                        tt(g_z, y_ps[:, 0:128], b2c[:, :], ALU.add).then_inc(sem["dense_z"], 1)
                        settle(dve)
                        dve.wait_ge(sem["dense_r"], q + 1)
                        tt(g_w, g_r, g_adjt[:, bass.ds(i, 1)], ALU.mult).then_inc(sem["dense_w"], 1)
                    drows.start(b)
                    dve.wait_ge(sem["dense_turned"], b + 1)
                    drows(tt(g_rows, lg_ps[:, 0:128], gab[:, :], ALU.mult))
                    drows(v.tensor_reduce(g_deg, g_adj, AX_X, ALU.add))
                    drows(stt(g_rows, beb[:, :], g_deg, g_rows, ALU.mult, ALU.add))
                    drows(tt(g_rows, g_rows, g_x1, ALU.add))
                    v.bn_stats(g_bns, g_rows).then_inc(sem["dense_bns"], 1)
                    settle(dve)
                    dve.wait_ge(sem["dense_bns"], b + 1)
                    v.bn_aggr(g_mv, g_bns).then_inc(sem["dense_rows"], 1)
                    drows.k += 1
                    dve.wait_ge(sem["dense_rows"], drows.base + drows.k)
                    ts(g_var, g_mv[:, 1:2], LN_EPS, None, ALU.add).then_inc(sem["dense_var"], 1)
                    dve.wait_ge(sem["dense_rs"], b + 1)
                    newton(g_tiny, drows)
                    dve.wait_ge(sem["dense_stored"], 16 * b + 16)
                    ts(g_out, g_rows, g_mv[:, 0:1], g_tiny["rsn"], ALU.subtract, ALU.mult).then_inc(sem["dense_out"], 1)

            where_dense(dve, dense)

        @block.tensor
        def _(pe):
            mm = nc.tensor.matmul

            pe.wait_ge(sem["const"], 16 * 11)
            pe.wait_ge(sem["selb"], 3)
            pe.wait_ge(sem["w2c"], 1)

            def logits_raw(g):
                pe.wait_ge(sem["xt_loaded"], 16 * g + 16)
                if not first(g):
                    pe.wait_ge(sem["sws"], g)
                for u in range(GB):
                    last = mm(lr_ps[:, 2 * u:2 * u + 2], xts[:, cut(u)], wlr[:, :], start=True, stop=True)
                last.then_inc(sem["lr"], 1)

            def turn_rows(g):
                pe.wait_ge(sem["rowsb"], g + 1)
                pe.wait_ge(sem["lrc"], 2 * g + 2)
                nc.tensor.transpose(rt_ps, rowsb[:, :], identb[:, :]).then_inc(sem["rowst_ps"], 1)

            def spread_rows(g):
                pe.wait_ge(sem["rowst"], g + 1)
                for u in range(GB):
                    last = mm(bj_ps[:, cut(u)], selv[:, BB, u, :], rowst[:, :], start=True, stop=True)
                last.then_inc(sem["bj_ps"], 1)
                if not first(g):
                    pe.wait_ge(sem["e_r1"], 2 * g)
                for u in range(GB):
                    mm(lg_ps[:, cut(u)], rowst[:, :], selv[:, RR, u, :], start=True, stop=False)
                    last = mm(lg_ps[:, cut(u)], selv[:, LL, u, :], rowst[:, :], start=False, stop=True)
                last.then_inc(sem["lg"], 1)

            def gram(g):
                pe.wait_ge(sem["xm2"], g + 1)
                if not first(g):
                    pe.wait_ge(sem["hh"], g)
                for u in range(GB):
                    d2 = d2_ps[:, cut(u)]
                    mm(d2, xts[:, cut(u)], xm2[:, cut(u)], start=True, stop=False)
                    mm(d2, rowst[:, :], selv[:, X2, u, :], start=False, stop=False)
                    last = mm(d2, selv[:, X2, u, :], rowst[:, :], start=False, stop=True)
                last.then_inc(sem["d2"], 1)

            def with_x(g):
                pe.wait_ge(sem["wt"], g + 1)
                pe.wait_ge(sem["nm"], g + 1)
                pe.wait_ge(sem["den"], g + 1)
                pe.wait_ge(sem["bjs"], g + 1)
                pe.wait_ge(sem["xcol"], g + 1)
                for u in range(GB):
                    last = mm(sw_ps[:, 2 * u:2 * u + 2], wt[:, cut(u)], onex2[:, 2 * u:2 * u + 2], start=True, stop=True)
                last.then_inc(sem["sw"], 1)
                for u in range(GB):
                    last = mm(d2_ps[:, cut(u)], wt[:, cut(u)], bt(x_all, GB * g + u), start=True, stop=True)
                last.then_inc(sem["mm"], 1)

            def turn_x1(g):
                pe.wait_ge(sem["x1s"], g + 1)
                pe.wait_ge(sem["esig"], g + 1)
                for u in range(GB):
                    last = nc.tensor.transpose(lg_ps[:, cut(u)], x1s[:, cut(u)], ident)
                last.then_inc(sem["x1t_ps"], 1)

            def offsets(g):
                pe.wait_ge(sem["degs"], g + 1)
                if not first(g):
                    pe.wait_ge(sem["e_osb"], GB * g)
                mm(off_ps, tri, c["dg"], start=True, stop=True).then_inc(sem["off"], 1)

            def tables(g, half):
                pe.wait_ge(sem["x1t"], g + 1)
                if half == 1:
                    pe.wait_ge(sem["e_r1"], 2 * g + 1)
                for u in range(2):
                    last = mm(lg_ps[:, 256 * u:256 * u + 256], x1t[:, cut(2 * half + u)], w1c[:, :], start=True, stop=True)
                last.then_inc(sem["e_tab"], 1)

            def row_ranks(g, k):
                q, s = TILES * g + k, slot(k)
                pe.wait_ge(sem["e_si"], q + 1)
                pe.wait_ge(sem["vt"], g + 1)
                if not (first(g) and k == 0):
                    pe.wait_ge(sem["e_sj"], q)
                if k == 0:
                    for u in range(GB):
                        last = mm(vg_ps[:, cut(u)], bt(vt_all, GB * g + u), si[:, s, cut(u)], start=True, stop=True)
                else:
                    last = mm(vg_ps, bt(vt_all, GB * g + k - 1), si[:, s, :], start=True, stop=True)
                last.then_inc(sem["e_vg"], 1)

            def row_numbers(g, k):
                q, s = TILES * g + k, slot(k)
                pe.wait_ge(sem["e_si"], q + 1)
                pe.wait_ge(sem["offc"], g + 1)
                if not (first(g) and k == 0):
                    pe.wait_ge(sem["e_ies"], q)
                if k > 1:
                    pe.wait_ge(sem["e_osb"], GB * g + k - 1)
                elif not first(g):
                    pe.wait_ge(sem["e_osb"], GB * g)
                for n in range(CH):
                    last = mm(ie_ps[:, n:n + 1], si[:, s, cut(n)], colb[:, :], start=True, stop=True)
                last.then_inc(sem["e_ie"], 1)

            def gather(g, k):
                q, s = TILES * g + k, slot(k)
                pe.wait_ge(sem["e_sj"], q + 1)
                pe.wait_ge(sem["e_t2b"], 2 * g + 2)
                if not (first(g) and k == 0):
                    pe.wait_ge(sem["e_ht"], q)
                spans = [(u, cut(u)) for u in range(GB)] if k == 0 else [(k - 1, slice(0, T))]
                for u, cols_ in spans:
                    for n in range(PARTS):
                        mm(h_ps[:, cols_], tb[:, u, n, 0:128], si[:, s, cols_], start=(n == 0), stop=False)
                        last = mm(h_ps[:, cols_], tb[:, u, n, 128:256], sj[:, s, cols_],
                                  start=False, stop=(n == PARTS - 1))
                last.then_inc(sem["e_hps"], 1)

            def second(g, k):
                q = TILES * g + k
                pe.wait_ge(sem["e_ht"], q + 1)
                if not (first(g) and k == 0):
                    pe.wait_ge(sem["e_z"], q)
                for n in range(CH):
                    last = mm(y_ps[:, cut(n)], ht[:, cut(n)], w2c[:, :], start=True, stop=True)
                last.then_inc(sem["e_yps"], 1)

            def add_rows(g, k):
                q, s = TILES * g + k, slot(k)
                pe.wait_ge(sem["e_sit"], q + 1)
                pe.wait_ge(sem["e_z"], q + 1)
                pe.wait_ge(sem["e_ies"], q + 1)
                if not (first(g) and k == 1):
                    pe.wait_ge(sem["e_osb"], GB * g + k - 1)
                mm(o_ps, sit[:, 0, cut(k - 1)], z[:, 0, cut(k - 1)], start=True, stop=False)
                for n in range(CH):
                    last = mm(o_ps, sit[:, s, cut(n)], z[:, s, cut(n)], start=False, stop=(n == CH - 1))
                last.then_inc(sem["e_ops"], 1)

            def body(g):
                logits_raw(g)
                turn_rows(g)
                spread_rows(g)
                gram(g)
                with_x(g)
                turn_x1(g)
                offsets(g)
                for half in range(2):
                    tables(g, half)
                for k in range(TILES):
                    row_ranks(g, k)
                    row_numbers(g, k)
                    gather(g, k)
                    second(g, k)
                    if k > 0:
                        add_rows(g, k)

            run_groups(pe, body)
            pe.wait_ge(sem["dega"], 2 * groups)
            pe.wait_ge(sem["badr"], 1)
            mm(y_ps[:, 0:GB * groups], ones_f, deg_all[:, 0:GB * groups], start=True, stop=True).then_inc(sem["nall"], 1)
            mm(y_ps[:, 128:129], ones_f, fl[:, 0:1], start=True, stop=True).then_inc(sem["nall"], 1)

            def dense():
                with pe.Fori(0, NB) as b:
                    pe.wait_ge(sem["dense_x1"], b + 1)
                    nc.tensor.transpose(lg_ps[:, 0:128], g_x1, ident).then_inc(sem["dense_x1t_ps"], 1)
                    pe.wait_ge(sem["dense_x1t"], b + 1)
                    mm(h_ps[:, 0:128], w1c[:, 0:128], g_x1t, start=True, stop=True)
                    mm(h_ps[:, 128:256], w1c[:, 128:256], g_x1t, start=True, stop=True).then_inc(sem["dense_hps"], 1)
                    with pe.Fori(0, N) as i:
                        q = N * b + i
                        pe.wait_ge(sem["dense_h"], q + 1)
                        mm(y_ps[:, 0:128], g_h, w2c[:, :], start=True, stop=True).then_inc(sem["dense_y"], 1)
                        pe.wait_ge(sem["dense_w"], q + 1)
                        mm(o_ps[:, 0:1], g_z, g_w, start=True, stop=True).then_inc(sem["dense_o"], 1)
                    pe.wait_ge(sem["dense_hidden_ready"], (N + 2) * b + N + 2)
                    nc.tensor.transpose(lg_ps[:, 0:128], g_o, ident).then_inc(sem["dense_turned"], 1)

            where_dense(pe, dense)


def constants():
    import numpy as np

    k = np.arange(128)
    tri = (k[:, None] < k[None, :]).astype(np.float32)
    reset = np.tile((k > 0).astype(np.float32), (128, GB))
    f32 = np.concatenate([tri, np.eye(128, dtype=np.float32), np.ones((128, 128), np.float32), reset,
                          np.zeros((128, 1), np.float32)], 1)
    e = np.arange(CAP)
    fp16 = np.concatenate([np.tile(e, (128, 1)), np.tile(e[:T] + 1, (128, 1)),
                           np.tile(e[T:] + 1, (128, GB)), np.tile(k + 1, (128, 1)),
                           (k + 1)[:, None]], 1).astype(np.float16)
    rows = np.arange(PARTS * ROWS) % ROWS
    want = np.array([[4 * b + t for b in range(GB)] for t in range(4)])
    sel = (rows[:, None, None] == want[None]).astype(np.float16)
    sel = np.repeat(sel.reshape(PARTS * ROWS, 4 * GB), 128, axis=1)
    return {"c_f32": f32, "c_fp16": fp16, "c_sel": sel}


def kernel(**inputs):
    import numpy as np
    import concourse.bacc as bacc
    from concourse.bass_utils import run_bass_kernel_spmd

    a = {k: np.asarray(v) for k, v in inputs.items()}

    def flat(v):
        return np.ascontiguousarray(v).reshape(128, NB * 128)

    arrays = {
        "x_n": flat(a["x"].transpose(1, 0, 2)), "x_t": flat(a["x"].transpose(2, 0, 1)),
        "adj_n": flat(a["adj"].transpose(1, 0, 2)), "adj_t": flat(a["adj"].transpose(2, 0, 1)),
        "att_w": a["L0_gnn_att_w"].reshape(2, 128).T, "att_b": a["L0_gnn_att_b"].reshape(1),
        "W1": a["L1_gnn_W1"].reshape(2, 128, 128).transpose(1, 0, 2).reshape(128, 256),
        "b1": a["L1_gnn_b1"].reshape(128, 1), "W2": a["L1_gnn_W2"], "b2": a["L1_gnn_b2"],
        "gamma": a["L1_gnn_gamma"], "beta": a["L1_gnn_beta"], **constants(),
    }
    nc = bacc.Bacc("TRN2", target_bir_lowering=False, num_devices=1)
    aps = {}
    for name, v in arrays.items():
        arrays[name] = v = np.ascontiguousarray(v)
        aps[name] = nc.dram_tensor(name, v.shape, mybir.dt.from_np(v.dtype), kind="ExternalInput").ap()
    out = nc.dram_tensor("out", (128, NB * 128), F32, kind="ExternalOutput").ap()
    two_graph_layers(nc, out=out, **aps)
    r = run_bass_kernel_spmd(nc, [arrays], core_ids=[0])
    return np.ascontiguousarray(r.results[0]["out"].reshape(128, NB, 128).transpose(1, 0, 2))
```

```python
from contextlib import ExitStack

import concourse.bass as bass
from concourse import mybir

NB = 64
N = 128
D = 128
GB = 4
NG = NB // GB
W = GB * N
CH = 4
T = CH * 128
TILES = GB + 1
CAP = T + 128
PARTS = 3
ROWS = 4 * GB
X2, BB, LL, RR = range(4)

MIN_NORM = 1e-15
CLIP = 1.0 - 1e-7
LN_EPS = 1e-5
LOG_MIN_NORM = -34.538776394910684
ROW_STEPS, COL_STEPS, DENSE_ROW_STEPS = 28, 14, 8
UQ_STEP, DE_STEP = 13, 21
TINY = 2.0 ** -60
SIG_MAX = 1e19

ALU = mybir.AluOpType
ACT = mybir.ActivationFunctionType
F32 = mybir.dt.float32
BF16 = mybir.dt.bfloat16
FP16 = mybir.dt.float16
I32 = mybir.dt.int32
AX_X = mybir.AxisListType.X

GROUP_STEPS = """loaded adj_loaded adjt_loaded xt_loaded xm2 lr sqx x2 x2m lpn pn pcl at1 at2 xcol lrc rowsb rowst_ps rowst d2 bj_ps
lg bjs esig esigc lse den nm denc lnn lnd ls lsc uu ucl l1 l2 qe q2e w0 dl w1 wt mm sw xmp sqm sws uqm lun un zz ez
ga tx hh bns bna vare lv rs x1s x1a x1t_ps x1t scan degs dega off offc mid vt bsq bdiff bad
held bc bm rbm rpn xmr mmr run e1 re th dec rd newton
fin1 fin2 fin3 fbns fbna fvare flv frs fout stored rows frows cols""".split()
BATCH_STEPS = "tab t0 r1 t1 t2b absd si vg ie ies sj hps ht yps z sq ss lnv rstd sit ops osb".split()
ONCE_STEPS = "const selb w2sum w2c b2c ones badr nall okn flagf flag".split()
DENSE_STEPS = "loaded x1 x1t_ps x1t hps hidden_ready h y z sq lv r w o turned rows bns var lv2 rs out stored".split()


def two_graph_layers(nc, x_n, x_t, adj_n, adj_t, att_w, att_b, W1, b1, W2, b2, gamma, beta,
                     c_f32, c_fp16, c_sel, out, groups=NG):
    with ExitStack() as ctx:
        def sb(name, shape, dt=F32):
            return ctx.enter_context(nc.sbuf_tensor(name, shape, dt))

        sem = {n: ctx.enter_context(nc.semaphore(f"s_{n}"))
                                 for n in GROUP_STEPS + ["e_" + b for b in BATCH_STEPS] + ONCE_STEPS
                                 + ["dense_" + d for d in DENSE_STEPS]
                                 }

        x_all = sb("x_all", [128, NB * D])
        x1_all = sb("x1_all", [128, NB * D])
        vt_all = sb("vt_all", [128, NB * N], FP16)
        deg_all = sb("deg_all", [128, NB])
        half_all = sb("half_all", [128, NB])
        mid_all = sb("mid_all", [128, NB])
        bad_all = sb("bad_all", [128, NG])

        cf = sb("cf", [128, 3 * 128 + 512 + 1])
        tri, ident, ones_f = cf[:, 0:128], cf[:, 128:256], cf[:, 256:384]
        reset = cf[:, 384:896]
        ch = sb("ch", [128, CAP + 2 * T + 128 + 1], FP16)
        iota_e = ch[:, 0:CAP]
        rank_main = ch[:, CAP:CAP + T]
        rank_tail = ch[:, CAP + T:CAP + 2 * T]
        iota_i1, col_i1 = ch[:, CAP + 2 * T:CAP + 2 * T + 128], ch[:, CAP + 2 * T + 128:CAP + 2 * T + 129]
        colb = sb("colb", [128, 1], BF16)
        identb = sb("identb", [128, 128], BF16)
        self_ = sb("self", [PARTS * ROWS, 4 * GB * 128], FP16)
        selb = sb("selb", [PARTS * ROWS, 4 * GB * 128], BF16)
        selv = selb[:, :].rearrange("k (t b n) -> k t b n", t=4, b=GB)
        wlr = sb("wlr", [128, 2])
        attb = sb("attb", [128, 1])
        w1c = sb("w1c", [128, 256])
        b1c = sb("b1c", [128, 1])
        w2 = sb("w2", [128, 128])
        w2s = sb("w2s", [128, 1])
        w2c = sb("w2c", [128, 128])
        b2b = sb("b2b", [128, 128])
        b2s = sb("b2s", [128, 1])
        b2c = sb("b2c", [128, 128])
        gab = sb("gab", [128, 128])
        beb = sb("beb", [128, 128])
        eps1 = sb("eps1", [128, 1])
        one1 = sb("one1", [128, 1])

        xts = sb("xts", [128, W])
        xm2 = sb("xm2", [128, W])
        adjt = sb("adjt", [128, W])
        adjs = sb("adjs", [128, W])
        sqx, bjs, esig, lse, den, nm, lnn, lnd, ls, uw, ucl, l1, l2, qe, q2e, w0, dl, w1, wt = (
            sb(n, [128, W]) for n in "sqx bjs esig lse den nm lnn lnd ls uw ucl l1 l2 qe q2e w0 dl w1 wt".split())
        xmp, sqm, tx, hh, x1s, x1t = (sb(n, [128, W]) for n in "xmp sqm tx hh x1s x1t".split())
        tiny = sb("tiny", [128, 80 * GB])
        tiny_names = """x2 bc bm hbm be rbm hx2 hbc hbm_ hbm2 hbe hrbm x2m lpn pn pcl at1 at2 rpn dat fac0 fac lcol
        xmr mmr c1 m1 m2 al ax bx xu t2 t3 t4 t5 t6 uq uqm lun un zz ez e1 re th run rho r2 s1 rxu tw0 tw nx de dec
        rd rr gg ga2 ga0 ga t7 t8 t9 vare lv rs ra rb rsn dg""".split()
        c = {n: tiny[:, GB * k:GB * (k + 1)] for k, n in enumerate(tiny_names)}
        fresh, held = tiny[:, 0:6 * GB], tiny[:, 6 * GB:12 * GB]
        h = dict(x2=c["hx2"], bc=c["hbc"], bm=c["hbm_"], hbm=c["hbm2"], be=c["hbe"], rbm=c["hrbm"])
        half_c = sb("half_c", [128, GB])
        vals = sb("vals", [128, ROWS])
        vv = vals[:, :].rearrange("p (b t) -> p t b", t=4)
        q1 = sb("q1", [128, ROWS])
        q2 = sb("q2", [128, ROWS])
        rowsb = sb("rowsb", [128, 128], BF16)
        rowst = sb("rowst", [PARTS * ROWS, 128], BF16)
        onex2 = sb("onex2", [128, 2 * GB])
        lrs = sb("lrs", [128, 2 * GB])
        sws = sb("sws", [128, 2 * GB])
        bns = sb("bns", [128, 6 * GB])
        mv = sb("mv", [128, 2 * GB])
        scan = sb("scan", [128, W])
        offc = sb("offc", [128, GB])
        bsq = sb("bsq", [128, W])
        bdiff = sb("bdiff", [128, W])

        tb = sb("tb", [128, GB, PARTS, 256], BF16)
        r1 = sb("r1", [128, 512])
        absd = sb("absd", [128, T], FP16)
        si = sb("si", [128, 3, T], BF16)
        sj = sb("sj", [128, 3, T], BF16)
        ies = sb("ies", [128, 3, CH])
        ht = sb("ht", [128, T])
        z = sb("z", [128, 3, T])
        sq = sb("sq", [128, T])
        ss = sb("ss", [128, 3, CH])
        lnv = sb("lnv", [128, 3, CH])
        rstd = sb("rstd", [128, 3, CH])
        sit = sb("sit", [128, 3, T])
        osb = sb("osb", [128, W])
        fin1 = sb("fin1", [128, W])
        fbns = sb("fbns", [128, 6 * GB])
        fmv = sb("fmv", [128, 2 * GB])
        ftiny = sb("ftiny", [128, 8 * GB])
        f = {n: ftiny[:, GB * k:GB * (k + 1)]
                               for k, n in enumerate("vare lv rs ra rb rc rsn".split())}
        fo = sb("fo", [128, W])
        okn = sb("okn", [128, NB])
        fl = sb("fl", [128, 8])
        flagi = sb("flagi", [128, 1], I32)

        g_x1, g_x1t, g_hi, g_hj = xts[:, 0:128], xts[:, 128:256], xts[:, 256:384], xts[:, 384:512]
        g_h, g_z, g_sq, g_o = xm2[:, 0:128], xm2[:, 128:256], xm2[:, 256:384], xm2[:, 384:512]
        g_adj, g_adjt, g_rows, g_out = adjs[:, 0:128], adjt[:, 0:128], sqx[:, 0:128], fo[:, 0:128]
        g_ss, g_lv, g_r, g_w, g_deg, g_var, g_lv2, g_rs = (fbns[:, k:k + 1] for k in range(8))
        g_tiny = dict(vare=g_var, rs=g_rs, ra=fbns[:, 8:9], rb=fbns[:, 9:10], rsn=fbns[:, 10:11])
        g_bns, g_mv = bns[:, 0:6], mv[:, 0:2]

        banks = [ctx.enter_context(nc.psum_tensor(f"bank{k}", [128, 512], F32)) for k in range(8)]
        vg_ps, h_ps, y_ps = (b[:, :] for b in banks[0:3])
        o_ps, ie_ps, off_ps = banks[3][:, 0:128], banks[3][:, 128:128 + CH], banks[3][:, 136:136 + GB]
        lg_ps = banks[4][:, :]
        d2_ps = banks[5][:, :]
        m_ps = banks[7][:, :]
        bj_ps = banks[6][:, :]
        lr_ps, rt_ps, sw_ps = banks[6][:, 0:8], banks[6][:, 64:128].bitcast(BF16), banks[6][:, 128:136]

        def grp(t, g, width=W):
            return t[:, bass.ds(g * width, width)]

        def bt(t, b, width=128):
            return t[:, bass.ds(b * width, width)]

        def cut(u):
            return slice(128 * u, 128 * (u + 1))

        def wide(a):
            return a.rearrange("p (b n) -> p b n", b=GB)

        def spread(col):
            return col.unsqueeze(2).to_broadcast([128, GB, 128])

        def settle(eng):
            eng.wait_ge(sem["ones"], 2)

        class Chain:

            def __init__(self, eng, sem_, steps):
                self.eng, self.sem, self.steps = eng, sem_, steps

            def start(self, g):
                self.base, self.k = g * self.steps, 0

            def __call__(self, ins, wait=True):
                self.k += 1
                ins.then_inc(self.sem, 1)
                if wait:
                    self.eng.wait_ge(self.sem, self.base + self.k)

            def end(self):
                assert self.k == self.steps, self.k

        def where_dense(eng, body):
            eng.wait_ge(sem["flag"], 1)
            found = eng.value_load(flagi[0:1, 0:1], min_val=0, max_val=1)
            with eng.If(found > 0):
                body()

        def slot(k):
            return 0 if k == 0 else 1 + (k - 1) % 2

        def reuse(g, k):
            if first(g) and k < 3:
                return None
            return TILES * g + k - (5, 3, 3, 2, 2)[k] + 1

        def first(g):
            return isinstance(g, int) and g == 0

        block = ctx.enter_context(nc.Block())

        def run_groups(eng, body):
            def turn(t):
                body(*(t - lag if 0 <= t - lag < groups else None for lag in range(4)))

            for t in range(4):
                turn(t)
            with eng.Fori(1, groups - 3) as g:
                body(g + 3, g + 2, g + 1, g)
            for t in range(groups, groups + 3):
                turn(t)

        @block.sync
        def _(sp):
            def load(dst, src):
                sp.dma_start(dst, src).then_inc(sem["const"], 16)

            load(cf[:, :], c_f32)
            load(ch[:, :], c_fp16)
            load(self_[:, :], c_sel)
            load(wlr[:, :], att_w)
            load(attb[:, :], att_b.partition_broadcast(128))
            load(w1c[:, :], W1)
            load(b1c[:, :], b1)
            load(w2[:, :], W2)
            load(b2b[:, :], b2.partition_broadcast(128))
            load(gab[:, :], gamma.partition_broadcast(128))
            load(beb[:, :], beta.partition_broadcast(128))

            def load_adj(g):
                if not first(g):
                    sp.wait_ge(sem["loaded"], 16 * g)
                    sp.wait_ge(sem["scan"], g)
                    sp.wait_ge(sem["vt"], g)
                    sp.wait_ge(sem["bdiff"], g)
                sp.dma_start(adjs[:, :], grp(adj_n, g)).then_inc(sem["adj_loaded"], 16)

            def load_x(g):
                if not first(g):
                    sp.wait_ge(sem["d2"], g)
                    sp.wait_ge(sem["lr"], g)
                    sp.wait_ge(sem["xm2"], g)
                sp.dma_start(xts[:, :], grp(x_t, g)).then_inc(sem["xt_loaded"], 16)
                sp.dma_start(grp(x_all, g), grp(x_n, g)).then_inc(sem["loaded"], 16)

            def load_adjt(g):
                if not first(g):
                    sp.wait_ge(sem["w1"], g)
                sp.dma_start(adjt[:, :], grp(adj_t, g)).then_inc(sem["adjt_loaded"], 16)

            def body(a, b, e, f):
                if a is not None:
                    load_adj(a)
                    load_x(a)
                    load_adjt(a)

            run_groups(sp, body)

            def dense():
                sp.wait_ge(sem["stored"], 16 * groups)
                sp.dma_start(g_out, bt(out, 0)).then_inc(sem["dense_stored"], 16)
                with sp.Fori(0, NB) as b:
                    sp.dma_start(g_adj, bt(adj_n, b)).then_inc(sem["dense_loaded"], 16)
                    sp.dma_start(g_adjt, bt(adj_t, b)).then_inc(sem["dense_loaded"], 16)
                    settle(sp)
                    sp.wait_ge(sem["dense_out"], b + 1)
                    sp.dma_start(bt(out, b), g_out).then_inc(sem["dense_stored"], 16)
                sp.wait_ge(sem["dense_stored"], 16 * NB + 16)

            where_dense(sp, dense)

        @block.gpsimd
        def _(pool):
            tt = nc.gpsimd.tensor_tensor
            ones_c = ones_f[:, 0:GB]
            cols, rows = Chain(pool, sem["cols"], COL_STEPS), Chain(pool, sem["rows"], ROW_STEPS)

            def badness(g):
                pool.wait_ge(sem["adj_loaded"], 16 * g + 16)
                tt(bsq[:, :], adjs[:, :], adjs[:, :], ALU.mult).then_inc(sem["bsq"], 1)
                pool.wait_ge(sem["bsq"], g + 1)
                if not first(g):
                    pool.wait_ge(sem["bad"], g)
                tt(bdiff[:, :], bsq[:, :], adjs[:, :], ALU.subtract).then_inc(sem["bdiff"], 1)

            def weights(g):
                pool.wait_ge(sem["qe"], g + 1)
                pool.wait_ge(sem["lse"], g + 1)
                tt(q2e[:, :], qe[:, :], lse[:, :], ALU.add).then_inc(sem["q2e"], 1)
                pool.wait_ge(sem["l1"], g + 1)
                pool.wait_ge(sem["l2"], g + 1)
                tt(dl[:, :], l1[:, :], l2[:, :], ALU.subtract).then_inc(sem["dl"], 1)
                settle(pool)
                pool.wait_ge(sem["dl"], g + 1)
                pool.wait_ge(sem["adjt_loaded"], 16 * g + 16)
                tt(w1[:, :], dl[:, :], adjt[:, :], ALU.mult).then_inc(sem["w1"], 1)
                pool.wait_ge(sem["w1"], g + 1)
                pool.wait_ge(sem["w0"], g + 1)
                if not first(g):
                    pool.wait_ge(sem["mm"], g)
                    pool.wait_ge(sem["sw"], g)
                tt(wt[:, :], w1[:, :], w0[:, :], ALU.mult).then_inc(sem["wt"], 1)

            def hold(g):
                if not first(g):
                    pool.wait_ge(sem["ga"], g)
                pool.wait_ge(sem["rbm"], g + 1)
                pool.wait_ge(sem["cols"], COL_STEPS * g + COL_STEPS)
                pool.wait_ge(sem["bm"], g + 1)
                if not first(g):
                    pool.wait_ge(sem["zz"], g)
                tt(held, fresh, ones_f[:, 0:6 * GB], ALU.mult).then_inc(sem["held"], 1)

            def cols_1(g):
                cols.start(g)
                pool.wait_ge(sem["x2"], g + 1)
                pool.wait_ge(sem["bc"], g + 1)
                pool.wait_ge(sem["const"], 16 * 11)
                pool.wait_ge(sem["ones"], 2)
                if not first(g):
                    pool.wait_ge(sem["held"], g)
                cols(tt(vv[:, BB, :], c["bc"], ones_c, ALU.mult), wait=False)
                cols(tt(vv[:, X2, :], c["x2"], ones_c, ALU.mult), wait=False)
                if not first(g):
                    pool.wait_ge(sem["sw"], g)
                tt(onex2[:, 1:2 * GB:2], c["x2"], ones_c, ALU.mult).then_inc(sem["xcol"], 1)
                pool.wait_ge(sem["bm"], g + 1)
                cols(tt(c["hbm"], c["bm"], half_c[:, :], ALU.mult))
                cols(tt(c["be"], c["hbm"], c["bc"], ALU.mult), wait=False)

            def cols_2(g):
                pool.wait_ge(sem["at1"], g + 1)
                pool.wait_ge(sem["at2"], g + 1)
                cols(tt(c["dat"], c["at1"], c["at2"], ALU.subtract))
                pool.wait_ge(sem["rpn"], g + 1)
                cols(tt(c["fac0"], c["dat"], c["rpn"], ALU.mult))
                cols(tt(c["fac"], c["fac0"], half_c[:, :], ALU.mult))
                pool.wait_ge(sem["lrc"], g + 1)
                cols(tt(vv[:, RR, :], lrs[:, 1:2 * GB:2], c["fac"], ALU.mult), wait=False)
                cols(tt(c["lcol"], lrs[:, 0:2 * GB:2], c["fac"], ALU.mult))
                cols(tt(vv[:, LL, :], c["lcol"], attb[:, :].to_broadcast([128, GB]), ALU.add))

            def split_rows(g):
                if not first(g):
                    pool.wait_ge(sem["rowst_ps"], g)
                ones_r = ones_f[:, 0:ROWS]
                cols(tt(rowsb[:, 0:ROWS], vals[:, :], ones_r, ALU.mult))
                cols(tt(q1[:, :], vals[:, :], rowsb[:, 0:ROWS], ALU.subtract))
                cols(tt(rowsb[:, ROWS:2 * ROWS], q1[:, :], ones_r, ALU.mult))
                cols(tt(q2[:, :], q1[:, :], rowsb[:, ROWS:2 * ROWS], ALU.subtract))
                tt(rowsb[:, 2 * ROWS:3 * ROWS], q2[:, :], ones_r, ALU.mult).then_inc(sem["rowsb"], 1)
                pool.wait_ge(sem["rowsb"], g + 1)
                cols.end()

            def rows_1(g):
                rows.start(g)
                pool.wait_ge(sem["held"], g + 1)
                pool.wait_ge(sem["sws"], g + 1)
                rows(tt(c["c1"], sws[:, 0:2 * GB:2], sws[:, 1:2 * GB:2], ALU.add))
                rows(tt(c["m1"], h["hbm"], c["c1"], ALU.mult), wait=False)
                pool.wait_ge(sem["xmr"], g + 1)
                rows(tt(c["bx"], h["be"], c["xmr"], ALU.mult), wait=False)
                rows(tt(c["m2"], h["bm"], c["xmr"], ALU.mult))
                rows(tt(c["al"], c["m2"], c["m1"], ALU.subtract))
                rows(tt(c["ax"], c["al"], h["x2"], ALU.mult))
                rows(tt(c["xu"], c["ax"], c["bx"], ALU.add))
                rows(tt(c["t2"], c["al"], c["xu"], ALU.mult), wait=False)
                rows(tt(c["t3"], c["al"], c["xmr"], ALU.mult), wait=False)
                pool.wait_ge(sem["mmr"], g + 1)
                rows(tt(c["t4"], h["be"], c["mmr"], ALU.mult))
                rows(tt(c["t5"], c["t3"], c["t4"], ALU.add))
                rows(tt(c["t6"], h["be"], c["t5"], ALU.mult))
                rows(tt(c["uq"], c["t2"], c["t6"], ALU.add))

            def rows_2(g):
                pool.wait_ge(sem["un"], g + 1)
                tt(c["zz"], c["un"], h["rbm"], ALU.mult).then_inc(sem["zz"], 1)

            def rows_3(g):
                pool.wait_ge(sem["run"], g + 1)
                pool.wait_ge(sem["th"], g + 1)
                rows(tt(c["rho"], c["th"], c["run"], ALU.mult))
                rows(tt(c["rxu"], c["rho"], c["xu"], ALU.mult), wait=False)
                rows(tt(c["r2"], c["rho"], c["rho"], ALU.mult))
                rows(tt(c["tw0"], c["rxu"], c["rxu"], ALU.add), wait=False)
                rows(tt(c["s1"], c["r2"], c["uqm"], ALU.mult))
                rows(tt(c["tw"], c["tw0"], ones_c, ALU.add), wait=False)
                rows(tt(c["t7"], h["x2"], c["s1"], ALU.mult))
                rows(tt(c["de"], c["t7"], c["tw"], ALU.add), wait=False)
                rows(tt(c["nx"], c["tw"], c["s1"], ALU.add))

            def rows_4(g):
                rows(tt(c["gg"], c["rho"], h["bc"], ALU.mult), wait=False)
                pool.wait_ge(sem["rd"], g + 1)
                rows(tt(c["t9"], c["rd"], c["nx"], ALU.mult))
                rows(tt(c["rr"], c["gg"], c["rd"], ALU.mult))
                rows(tt(c["t8"], c["rr"], c["al"], ALU.mult), wait=False)
                rows(tt(c["ga2"], c["rr"], h["be"], ALU.mult))
                rows(tt(c["ga0"], c["t8"], c["t9"], ALU.add))
                tt(c["ga"], c["ga0"], ones_c, ALU.add).then_inc(sem["ga"], 1)
                rows.end()

            def h_part(g):
                settle(pool)
                pool.wait_ge(sem["ga"], g + 1)
                if not first(g):
                    pool.wait_ge(sem["hh"], g)
                tt(wide(tx[:, :]), wide(grp(x_all, g)), spread(c["ga"]), ALU.mult).then_inc(sem["tx"], 1)

            def keep_x1(g):
                settle(pool)
                pool.wait_ge(sem["x1s"], g + 1)
                nc.gpsimd.tensor_copy(grp(x1_all, g), x1s[:, :]).then_inc(sem["x1a"], 1)

            def finish(g):
                settle(pool)
                if not first(g):
                    pool.wait_ge(sem["fbns"], g)
                    pool.wait_ge(sem["fout"], g)
                pool.wait_ge(sem["dega"], 2 * g + 2)
                pool.wait_ge(sem["const"], 16 * 11)
                tt(wide(fin1[:, :]), beb[:, :].unsqueeze(1).to_broadcast([128, GB, 128]),
                   spread(bt(deg_all, g, GB)), ALU.mult).then_inc(sem["fin1"], 1)
                pool.wait_ge(sem["fin1"], g + 1)
                pool.wait_ge(sem["e_osb"], GB * g + GB)
                tt(fin1[:, :], fin1[:, :], osb[:, :], ALU.add).then_inc(sem["fin2"], 1)
                settle(pool)
                pool.wait_ge(sem["fin2"], g + 1)
                pool.wait_ge(sem["x1a"], g + 1)
                tt(fin1[:, :], fin1[:, :], grp(x1_all, g), ALU.add).then_inc(sem["fin3"], 1)

            def body(a, b, e, f):
                if b is not None:
                    hold(b)
                if a is not None:
                    cols_1(a)
                    cols_2(a)
                    split_rows(a)
                if b is not None:
                    rows_1(b)
                    rows_2(b)
                    rows_3(b)
                    rows_4(b)
                    h_part(b)
                if a is not None:
                    badness(a)
                if b is not None:
                    keep_x1(b)
                if a is not None:
                    weights(a)
                if e is not None:
                    finish(e)

            run_groups(pool, body)

        @block.scalar
        def _(act):
            fn = nc.scalar.activation

            nc.scalar.preload_act_table_set("natural_log_exp_and_others")
            act.wait_ge(sem["const"], 16 * 11)
            act.wait_ge(sem["ones"], 1)
            fn(selb[:, :], self_[:, :], ACT.Copy).then_inc(sem["selb"], 1)
            fn(identb[:, :], ident, ACT.Copy).then_inc(sem["selb"], 1)
            fn(colb[:, :], col_i1, ACT.Copy).then_inc(sem["selb"], 1)

            def l0_x(g):
                act.wait_ge(sem["xt_loaded"], 16 * g + 16)
                if not first(g):
                    act.wait_ge(sem["d2"], g)
                fn(xm2[:, :], xts[:, :], ACT.Copy, scale=-2.0).then_inc(sem["xm2"], 1)
                settle(act)
                act.wait_ge(sem["loaded"], 16 * g + 16)
                if not first(g):
                    act.wait_ge(sem["x2"], g)
                fn(sqx[:, :], grp(x_all, g), ACT.Square).then_inc(sem["sqx"], 1)

            def l0_lr(g):
                act.wait_ge(sem["lr"], g + 1)
                if not first(g):
                    act.wait_ge(sem["cols"], COL_STEPS * g)
                fn(lrs[:, :], lr_ps, ACT.Copy).then_inc(sem["lrc"], 1)

            def l0_norm(g):
                act.wait_ge(sem["x2m"], g + 1)
                fn(c["lpn"], c["x2m"], ACT.Ln).then_inc(sem["lpn"], 1)
                act.wait_ge(sem["lpn"], g + 1)
                fn(c["pn"], c["lpn"], ACT.Exp, scale=0.5).then_inc(sem["pn"], 1)

            def l0_atanh(g):
                act.wait_ge(sem["pcl"], g + 1)
                fn(c["at1"], c["pcl"], ACT.Ln, bias=one1[:, :]).then_inc(sem["at1"], 1)
                fn(c["at2"], c["pcl"], ACT.Ln, bias=one1[:, :], scale=-1.0).then_inc(sem["at2"], 1)

            def l0_rows(g):
                act.wait_ge(sem["rowst_ps"], g + 1)
                if not first(g):
                    act.wait_ge(sem["d2"], g)
                    act.wait_ge(sem["bj_ps"], g)
                    act.wait_ge(sem["lg"], g)
                fn(rowst[:, :], rt_ps[0:PARTS * ROWS, :], ACT.Copy).then_inc(sem["rowst"], 1)

            def l0_bc(g):
                act.wait_ge(sem["bj_ps"], g + 1)
                if not first(g):
                    act.wait_ge(sem["den"], g)
                fn(bjs[:, :], bj_ps, ACT.Copy).then_inc(sem["bjs"], 1)

            def l0_esig(g):
                act.wait_ge(sem["lg"], g + 1)
                if not first(g):
                    act.wait_ge(sem["lse"], g)
                fn(esig[:, :], lg_ps, ACT.Exp, scale=-1.0).then_inc(sem["esig"], 1)

            def l0_lse(g):
                act.wait_ge(sem["esigc"], g + 1)
                if not first(g):
                    act.wait_ge(sem["q2e"], g)
                fn(lse[:, :], esig[:, :], ACT.Ln, bias=one1[:, :]).then_inc(sem["lse"], 1)

            def l0_logs(g):
                act.wait_ge(sem["nm"], g + 1)
                fn(lnn[:, :], nm[:, :], ACT.Ln).then_inc(sem["lnn"], 1)
                act.wait_ge(sem["denc"], g + 1)
                fn(lnd[:, :], den[:, :], ACT.Ln).then_inc(sem["lnd"], 1)

            def l0_u(g):
                act.wait_ge(sem["lsc"], g + 1)
                fn(uw[:, :], ls[:, :], ACT.Exp, scale=0.5).then_inc(sem["uu"], 1)

            def l0_at(g):
                act.wait_ge(sem["ucl"], g + 1)
                if not first(g):
                    act.wait_ge(sem["dl"], g)
                fn(l1[:, :], ucl[:, :], ACT.Ln, bias=one1[:, :]).then_inc(sem["l1"], 1)
                fn(l2[:, :], ucl[:, :], ACT.Ln, bias=one1[:, :], scale=-1.0).then_inc(sem["l2"], 1)

            def l0_w0(g):
                act.wait_ge(sem["q2e"], g + 1)
                if not first(g):
                    act.wait_ge(sem["wt"], g)
                fn(w0[:, :], q2e[:, :], ACT.Exp, scale=-1.0).then_inc(sem["w0"], 1)

            def l0_m(g):
                act.wait_ge(sem["sw"], g + 1)
                if not first(g):
                    act.wait_ge(sem["rows"], ROW_STEPS * g - ROW_STEPS + 1)
                fn(sws[:, :], sw_ps, ACT.Copy).then_inc(sem["sws"], 1)
                act.wait_ge(sem["xmp"], g + 1)
                if not first(g):
                    act.wait_ge(sem["mmr"], g)
                fn(sqm[:, :], m_ps, ACT.Square).then_inc(sem["sqm"], 1)

            def l0_un(g):
                act.wait_ge(sem["uqm"], g + 1)
                fn(c["lun"], c["uqm"], ACT.Ln).then_inc(sem["lun"], 1)
                act.wait_ge(sem["lun"], g + 1)
                fn(c["un"], c["lun"], ACT.Exp, scale=0.5).then_inc(sem["un"], 1)

            def l0_ez(g):
                act.wait_ge(sem["zz"], g + 1)
                fn(c["ez"], c["zz"], ACT.Exp, scale=2.0).then_inc(sem["ez"], 1)

            def l0_rs(g):
                act.wait_ge(sem["vare"], g + 1)
                fn(c["lv"], c["vare"], ACT.Ln).then_inc(sem["lv"], 1)
                act.wait_ge(sem["lv"], g + 1)
                fn(c["rs"], c["lv"], ACT.Exp, scale=-0.5).then_inc(sem["rs"], 1)

            def l0_x1t(g):
                act.wait_ge(sem["x1t_ps"], g + 1)
                if not first(g):
                    act.wait_ge(sem["e_tab"], 2 * g)
                fn(x1t[:, :], lg_ps, ACT.Copy).then_inc(sem["x1t"], 1)

            def bad(g):
                settle(act)
                act.wait_ge(sem["bdiff"], g + 1)
                fn(bdiff[:, :], bdiff[:, :], ACT.Abs, accum_out=bt(bad_all, g, 1)).then_inc(sem["bad"], 1)

            def split0(g, half):
                act.wait_ge(sem["e_tab"], 2 * g + half + 1)
                if not first(g):
                    act.wait_ge(sem["e_hps"], TILES * g)
                fn(tb[:, 2 * half:2 * half + 2, 0, :], lg_ps.rearrange("p (b k) -> p b k", b=2),
                   ACT.Copy).then_inc(sem["e_t0"], 1)

            def split1(g, half):
                act.wait_ge(sem["e_r1"], 2 * g + half + 1)
                fn(tb[:, 2 * half:2 * half + 2, 1, :], r1[:, :].rearrange("p (b k) -> p b k", b=2),
                   ACT.Copy).then_inc(sem["e_t1"], 1)

            def distance(g, k):
                q = TILES * g + k
                if not isinstance(q, int):
                    q = act.to_reg(q)
                settle(act)
                act.wait_ge(sem["mid"], g + 1)
                if not (first(g) and k == 0):
                    act.wait_ge(sem["e_si"], q)
                if k == 0:
                    for u in range(GB):
                        last = fn(absd[:, cut(u)], iota_e[:, T:CAP], ACT.Abs, bias=bt(mid_all, GB * g + u, 1), scale=-1.0)
                else:
                    last = fn(absd[:, :], iota_e[:, 0:T], ACT.Abs, bias=bt(mid_all, GB * g + k - 1, 1), scale=-1.0)
                last.then_inc(sem["e_absd"], 1)

            def relu(g, k):
                q = TILES * g + k
                act.wait_ge(sem["e_hps"], q + 1)
                if not (first(g) and k == 0):
                    act.wait_ge(sem["e_yps"], q)
                fn(ht[:, :], h_ps, ACT.Relu, bias=b1c[:, :]).then_inc(sem["e_ht"], 1)

            def square(g, k):
                q = TILES * g + k
                act.wait_ge(sem["e_z"], q + 1)
                if not (first(g) and k == 0):
                    act.wait_ge(sem["e_ss"], q)
                fn(sq[:, :], z[:, slot(k), :], ACT.Square).then_inc(sem["e_sq"], 1)

            def inv_std(g, k):
                q, s = TILES * g + k, slot(k)
                act.wait_ge(sem["e_ss"], q + 1)
                fn(lnv[:, s, :], ss[:, s, :], ACT.Ln, scale=1.0 / D, bias=eps1[:, :]).then_inc(sem["e_lnv"], 1)
                act.wait_ge(sem["e_lnv"], q + 1)
                if reuse(g, k) is not None:
                    act.wait_ge(sem["e_sit"], reuse(g, k))
                fn(rstd[:, s, :], lnv[:, s, :], ACT.Exp, scale=-0.5).then_inc(sem["e_rstd"], 1)

            def finish(g):
                act.wait_ge(sem["fvare"], g + 1)
                fn(f["lv"], f["vare"], ACT.Ln).then_inc(sem["flv"], 1)
                act.wait_ge(sem["flv"], g + 1)
                fn(f["rs"], f["lv"], ACT.Exp, scale=-0.5).then_inc(sem["frs"], 1)

            def store(g):
                act.wait_ge(sem["fout"], g + 1)
                act.dma_start(grp(out, g), fo[:, :]).then_inc(sem["stored"], 16)

            def body(a, b, e, f):
                if e is not None:
                    distance(e, 0)
                if a is not None:
                    l0_x(a)
                if b is not None:
                    l0_m(b)
                if a is not None:
                    l0_norm(a)
                    l0_lr(a)
                if e is not None:
                    distance(e, 1)
                if a is not None:
                    l0_atanh(a)
                if e is not None:
                    relu(e, 0)
                    distance(e, 2)
                    square(e, 0)
                if b is not None:
                    l0_un(b)
                if a is not None:
                    l0_rows(a)
                if e is not None:
                    inv_std(e, 0)
                if b is not None:
                    l0_ez(b)
                if e is not None:
                    relu(e, 1)
                    distance(e, 3)
                if a is not None:
                    l0_bc(a)
                if e is not None:
                    square(e, 1)
                if a is not None:
                    l0_esig(a)
                if f is not None:
                    finish(f)
                if e is not None:
                    inv_std(e, 1)
                if e is not None:
                    relu(e, 2)
                    distance(e, 4)
                if a is not None:
                    l0_lse(a)
                if e is not None:
                    square(e, 2)
                if a is not None:
                    l0_logs(a)
                if f is not None:
                    store(f)
                if e is not None:
                    inv_std(e, 2)
                if e is not None:
                    relu(e, 3)
                if a is not None:
                    l0_u(a)
                if e is not None:
                    square(e, 3)
                if b is not None:
                    l0_rs(b)
                if e is not None:
                    inv_std(e, 3)
                if a is not None:
                    l0_at(a)
                if e is not None:
                    relu(e, 4)
                if a is not None:
                    bad(a)
                if b is not None:
                    l0_x1t(b)
                if e is not None:
                    square(e, 4)
                if b is not None:
                    split0(b, 0)
                if e is not None:
                    inv_std(e, 4)
                if b is not None:
                    split1(b, 0)
                    split0(b, 1)
                if a is not None:
                    l0_w0(a)
                if b is not None:
                    split1(b, 1)

            run_groups(act, body)
            act.wait_ge(sem["stored"], 16 * groups)

            def dense():
                with act.Fori(0, NB) as b:
                    act.wait_ge(sem["dense_loaded"], 32 * b + 32)
                    fn(g_x1, bt(x1_all, b), ACT.Copy).then_inc(sem["dense_x1"], 1)
                    act.wait_ge(sem["dense_x1t_ps"], b + 1)
                    fn(g_x1t, lg_ps[:, 0:128], ACT.Copy).then_inc(sem["dense_x1t"], 1)
                    act.wait_ge(sem["dense_hps"], b + 1)
                    fn(g_hi, h_ps[:, 0:128], ACT.Identity, bias=b1c[:, :]).then_inc(sem["dense_hidden_ready"], 1)
                    fn(g_hj, h_ps[:, 128:256], ACT.Copy).then_inc(sem["dense_hidden_ready"], 1)
                    with act.Fori(0, N) as i:
                        q = N * b + i
                        act.wait_ge(sem["dense_z"], q + 1)
                        fn(g_sq, g_z, ACT.Square, accum_out=g_ss).then_inc(sem["dense_sq"], 1)
                        act.wait_ge(sem["dense_sq"], q + 1)
                        fn(g_lv, g_ss, ACT.Ln, scale=1.0 / D, bias=eps1[:, :]).then_inc(sem["dense_lv"], 1)
                        act.wait_ge(sem["dense_lv"], q + 1)
                        fn(g_r, g_lv, ACT.Exp, scale=-0.5).then_inc(sem["dense_r"], 1)
                        settle(act)
                        act.wait_ge(sem["dense_o"], q + 1)
                        fn(g_o[:, bass.ds(i, 1)], o_ps[:, 0:1], ACT.Copy).then_inc(sem["dense_hidden_ready"], 1)
                    act.wait_ge(sem["dense_var"], b + 1)
                    fn(g_lv2, g_var, ACT.Ln).then_inc(sem["dense_lv2"], 1)
                    act.wait_ge(sem["dense_lv2"], b + 1)
                    fn(g_rs, g_lv2, ACT.Exp, scale=-0.5).then_inc(sem["dense_rs"], 1)

            where_dense(act, dense)

        @block.vector
        def _(dve):
            v = nc.vector
            tt, ts, stt = v.tensor_tensor, v.tensor_scalar, v.scalar_tensor_tensor

            v.memset(one1[:, :], 1.0).then_inc(sem["ones"], 1)
            v.memset(half_c[:, :], 0.5)
            v.memset(eps1[:, :], LN_EPS)
            v.memset(rowsb[:, :], 0.0)
            v.memset(onex2[:, :], 1.0).then_inc(sem["ones"], 1)
            dve.wait_ge(sem["const"], 16 * 11)
            dve.wait_ge(sem["ones"], 2)
            v.tensor_reduce(w2s[:, :], w2[:, :], AX_X, ALU.add).then_inc(sem["w2sum"], 1)
            v.tensor_reduce(b2s[:, :], b2b[:, :], AX_X, ALU.add).then_inc(sem["b2c"], 1)
            dve.wait_ge(sem["w2sum"], 1)
            ts(w2s[:, :], w2s[:, :], -1.0 / D, None, ALU.mult).then_inc(sem["w2sum"], 1)
            dve.wait_ge(sem["b2c"], 1)
            ts(b2s[:, :], b2s[:, :], -1.0 / D, None, ALU.mult).then_inc(sem["b2c"], 1)
            dve.wait_ge(sem["w2sum"], 2)
            ts(w2c[:, :], w2[:, :], w2s[:, :], None, ALU.add).then_inc(sem["w2c"], 1)
            dve.wait_ge(sem["b2c"], 2)
            ts(b2c[:, :], b2b[:, :], b2s[:, :], None, ALU.add).then_inc(sem["b2c"], 1)
            dve.wait_ge(sem["b2c"], 3)

            rows, frows = Chain(dve, sem["newton"], 3), Chain(dve, sem["frows"], 3)

            def x_sq(g):
                dve.wait_ge(sem["sqx"], g + 1)
                if not first(g):
                    dve.wait_ge(sem["held"], g)
                    dve.wait_ge(sem["cols"], COL_STEPS * g)
                v.tensor_reduce(c["x2"], wide(sqx[:, :]), AX_X, ALU.add).then_inc(sem["x2"], 1)
                dve.wait_ge(sem["x2"], g + 1)
                ts(c["x2m"], c["x2"], MIN_NORM, None, ALU.max).then_inc(sem["x2m"], 1)
                ts(c["bc"], c["x2"], -1.0, 1.0, ALU.mult, ALU.add).then_inc(sem["bc"], 1)
                dve.wait_ge(sem["bc"], g + 1)
                if not first(g):
                    dve.wait_ge(sem["rbm"], g)
                ts(c["bm"], c["bc"], MIN_NORM, None, ALU.max).then_inc(sem["bm"], 1)

            def reciprocals(g):
                dve.wait_ge(sem["bm"], g + 1)
                v.reciprocal(c["rbm"], c["bm"]).then_inc(sem["rbm"], 1)
                dve.wait_ge(sem["pn"], g + 1)
                ts(c["pcl"], c["pn"], CLIP, None, ALU.min).then_inc(sem["pcl"], 1)
                v.reciprocal(c["rpn"], c["pn"]).then_inc(sem["rpn"], 1)

            def clip_esig(g):
                dve.wait_ge(sem["esig"], g + 1)
                ts(esig[:, :], esig[:, :], SIG_MAX, None, ALU.min).then_inc(sem["esigc"], 1)

            def pairs_a(g):
                dve.wait_ge(sem["d2"], g + 1)
                if not first(g):
                    dve.wait_ge(sem["lnn"], g)
                    dve.wait_ge(sem["lnd"], g)
                ts(nm[:, :], d2_ps, TINY, None, ALU.max).then_inc(sem["nm"], 1)
                dve.wait_ge(sem["bjs"], g + 1)
                for u in range(GB):
                    last = stt(den[:, cut(u)], bjs[:, cut(u)], c["bc"][:, u:u + 1], d2_ps[:, cut(u)], ALU.mult, ALU.add)
                last.then_inc(sem["den"], 1)
                dve.wait_ge(sem["den"], g + 1)
                ts(den[:, :], den[:, :], MIN_NORM, None, ALU.max).then_inc(sem["denc"], 1)

            def pairs_b(g):
                dve.wait_ge(sem["lnn"], g + 1)
                dve.wait_ge(sem["lnd"], g + 1)
                tt(ls[:, :], lnn[:, :], lnd[:, :], ALU.subtract).then_inc(sem["ls"], 1)
                dve.wait_ge(sem["ls"], g + 1)
                ts(ls[:, :], ls[:, :], LOG_MIN_NORM, None, ALU.max).then_inc(sem["lsc"], 1)
                dve.wait_ge(sem["lsc"], g + 1)
                if not first(g):
                    dve.wait_ge(sem["q2e"], g)
                stt(qe[:, :], ls[:, :], 0.5, lnd[:, :], ALU.mult, ALU.add).then_inc(sem["qe"], 1)

            def clip_u(g):
                dve.wait_ge(sem["uu"], g + 1)
                if not first(g):
                    dve.wait_ge(sem["l1"], g)
                    dve.wait_ge(sem["l2"], g)
                ts(ucl[:, :], uw[:, :], CLIP, None, ALU.min).then_inc(sem["ucl"], 1)

            def dot_x(g):
                dve.wait_ge(sem["mm"], g + 1)
                tt(xmp[:, :], m_ps, grp(x_all, g), ALU.mult).then_inc(sem["xmp"], 1)
                dve.wait_ge(sem["xmp"], g + 1)
                if not first(g):
                    dve.wait_ge(sem["rows"], ROW_STEPS * g)
                v.tensor_reduce(c["xmr"], wide(xmp[:, :]), AX_X, ALU.add).then_inc(sem["xmr"], 1)

            def dot_m(g):
                dve.wait_ge(sem["sqm"], g + 1)
                v.tensor_reduce(c["mmr"], wide(sqm[:, :]), AX_X, ALU.add).then_inc(sem["mmr"], 1)

            def clip_uq(g):
                dve.wait_ge(sem["rows"], ROW_STEPS * g + UQ_STEP)
                ts(c["uqm"], c["uq"], MIN_NORM, None, ALU.max).then_inc(sem["uqm"], 1)

            def recip_un(g):
                dve.wait_ge(sem["un"], g + 1)
                v.reciprocal(c["run"], c["un"]).then_inc(sem["run"], 1)

            def tanh(g):
                dve.wait_ge(sem["ez"], g + 1)
                ts(c["e1"], c["ez"], 1.0, None, ALU.add).then_inc(sem["e1"], 1)
                dve.wait_ge(sem["e1"], g + 1)
                v.reciprocal(c["re"], c["e1"]).then_inc(sem["re"], 1)
                dve.wait_ge(sem["re"], g + 1)
                ts(c["th"], c["re"], -2.0, 1.0, ALU.mult, ALU.add).then_inc(sem["th"], 1)

            def recip_de(g):
                dve.wait_ge(sem["rows"], ROW_STEPS * g + DE_STEP)
                ts(c["dec"], c["de"], MIN_NORM, None, ALU.max).then_inc(sem["dec"], 1)
                dve.wait_ge(sem["dec"], g + 1)
                v.reciprocal(c["rd"], c["dec"]).then_inc(sem["rd"], 1)

            def newton(w, chain):
                chain(tt(w["ra"], w["rs"], w["rs"], ALU.mult))
                chain(stt(w["rb"], w["ra"], -0.5, w["vare"], ALU.mult, ALU.mult))
                chain(stt(w["rsn"], w["rb"], 1.5, w["rs"], ALU.add, ALU.mult))
                chain.end()

            def norm0_a(g):
                dve.wait_ge(sem["tx"], g + 1)
                dve.wait_ge(sem["sqm"], g + 1)
                for u in range(GB):
                    last = stt(hh[:, cut(u)], m_ps[:, cut(u)], c["ga2"][:, u:u + 1], tx[:, cut(u)], ALU.mult, ALU.add)
                last.then_inc(sem["hh"], 1)
                dve.wait_ge(sem["hh"], g + 1)
                for u in range(GB):
                    last = v.bn_stats(bns[:, 6 * u:6 * u + 6], hh[:, cut(u)])
                last.then_inc(sem["bns"], 1)
                settle(dve)
                dve.wait_ge(sem["bns"], g + 1)
                for u in range(GB):
                    last = v.bn_aggr(mv[:, 2 * u:2 * u + 2], bns[:, 6 * u:6 * u + 6])
                last.then_inc(sem["bna"], 1)
                dve.wait_ge(sem["bna"], g + 1)
                ts(c["vare"], mv[:, 1:2 * GB:2], LN_EPS, None, ALU.add).then_inc(sem["vare"], 1)

            def norm0_b(g):
                rows.start(g)
                dve.wait_ge(sem["rs"], g + 1)
                newton(c, rows)
                if not first(g):
                    dve.wait_ge(sem["x1t_ps"], g)
                    dve.wait_ge(sem["x1a"], g)
                for u in range(GB):
                    last = ts(x1s[:, cut(u)], hh[:, cut(u)], mv[:, 2 * u:2 * u + 1], c["rsn"][:, u:u + 1],
                              ALU.subtract, ALU.mult)
                last.then_inc(sem["x1s"], 1)

            def ranks_a(g):
                dve.wait_ge(sem["adj_loaded"], 16 * g + 16)
                v.tensor_tensor_scan(scan[:, :], reset, adjs[:, :], 0.0, ALU.mult, ALU.add).then_inc(sem["scan"], 1)
                dve.wait_ge(sem["scan"], g + 1)
                if not first(g):
                    dve.wait_ge(sem["off"], g)
                ts(c["dg"], scan[:, 127:W:128], 1.0, None, ALU.mult).then_inc(sem["degs"], 1)
                dve.wait_ge(sem["degs"], g + 1)
                ts(bt(deg_all, g, GB), c["dg"], 1.0, None, ALU.mult).then_inc(sem["dega"], 1)
                ts(bt(half_all, g, GB), c["dg"], 0.5, -0.5, ALU.mult, ALU.add).then_inc(sem["dega"], 1)

            def ranks_b(g):
                dve.wait_ge(sem["off"], g + 1)
                ts(offc[:, :], off_ps, 1.0, None, ALU.mult).then_inc(sem["offc"], 1)
                dve.wait_ge(sem["offc"], g + 1)
                dve.wait_ge(sem["dega"], 2 * g + 2)
                tt(bt(mid_all, g, GB), offc[:, :], bt(half_all, g, GB), ALU.add).then_inc(sem["mid"], 1)
                for u in range(GB):
                    last = stt(bt(vt_all, GB * g + u), scan[:, cut(u)], offc[:, u:u + 1], adjs[:, cut(u)],
                               ALU.add, ALU.mult)
                last.then_inc(sem["vt"], 1)
                dve.wait_ge(sem["mid"], g + 1)

            def split_r1(g, half):
                dve.wait_ge(sem["e_t0"], 2 * g + half + 1)
                if not (first(g) and half == 0):
                    dve.wait_ge(sem["e_t1"], 2 * g + half)
                    dve.wait_ge(sem["e_t2b"], 2 * g + half)
                tt(r1[:, :].rearrange("p (b k) -> p b k", b=2), lg_ps.rearrange("p (b k) -> p b k", b=2),
                   tb[:, 2 * half:2 * half + 2, 0, :], ALU.subtract).then_inc(sem["e_r1"], 1)

            def split_t2(g, half):
                dve.wait_ge(sem["e_t1"], 2 * g + half + 1)
                tt(tb[:, 2 * half:2 * half + 2, 2, :], r1[:, :].rearrange("p (b k) -> p b k", b=2),
                   tb[:, 2 * half:2 * half + 2, 1, :], ALU.subtract).then_inc(sem["e_t2b"], 1)

            def row_hot(g, k):
                q, s = TILES * g + k, slot(k)
                dve.wait_ge(sem["e_absd"], q + 1)
                if reuse(g, k) is not None:
                    dve.wait_ge(sem["e_hps"], reuse(g, k))
                    dve.wait_ge(sem["e_ie"], reuse(g, k))
                if k == 0:
                    for u in range(GB):
                        last = ts(si[:, s, cut(u)], absd[:, cut(u)], bt(half_all, GB * g + u, 1), None, ALU.is_le)
                else:
                    last = ts(si[:, s, :], absd[:, :], bt(half_all, GB * g + k - 1, 1), None, ALU.is_le)
                last.then_inc(sem["e_si"], 1)

            def col_hot(g, k):
                q, s = TILES * g + k, slot(k)
                dve.wait_ge(sem["e_vg"], q + 1)
                if reuse(g, k) is not None:
                    dve.wait_ge(sem["e_hps"], reuse(g, k))
                tt(sj[:, s, :], vg_ps, rank_tail if k == 0 else rank_main, ALU.is_equal).then_inc(sem["e_sj"], 1)

            def ie_copy(g, k):
                q, s = TILES * g + k, slot(k)
                dve.wait_ge(sem["e_ie"], q + 1)
                if reuse(g, k) is not None:
                    dve.wait_ge(sem["e_sit"], reuse(g, k))
                ts(ies[:, s, :], ie_ps, 1.0, None, ALU.mult).then_inc(sem["e_ies"], 1)

            def add_b2(g, k):
                q, s = TILES * g + k, slot(k)
                dve.wait_ge(sem["e_yps"], q + 1)
                if reuse(g, k) is not None:
                    dve.wait_ge(sem["e_ops"], GB * g if k == 0 else GB * g + k - 1 - (0, 2, 2, 2, 2)[k] + 1)
                    dve.wait_ge(sem["e_sq"], reuse(g, k))
                tt(z[:, s, :].rearrange("p (c l) -> p c l", c=CH), y_ps.rearrange("p (c l) -> p c l", c=CH),
                   b2c[:, :].unsqueeze(1).to_broadcast([128, CH, 128]), ALU.add).then_inc(sem["e_z"], 1)

            def sum_sq(g, k):
                q, s = TILES * g + k, slot(k)
                dve.wait_ge(sem["e_sq"], q + 1)
                if reuse(g, k) is not None:
                    dve.wait_ge(sem["e_lnv"], reuse(g, k))
                v.tensor_reduce(ss[:, s, :], sq[:, :].rearrange("p (c l) -> p c l", c=CH), AX_X,
                                ALU.add).then_inc(sem["e_ss"], 1)

            def row_hot_t(g, k):
                q, s = TILES * g + k, slot(k)
                dve.wait_ge(sem["e_rstd"], q + 1)
                dve.wait_ge(sem["e_ies"], q + 1)
                if reuse(g, k) is not None:
                    dve.wait_ge(sem["e_ops"], GB * g if k == 0 else GB * g + k - 1 - (0, 2, 2, 2, 2)[k] + 1)
                for n in range(CH):
                    last = ts(sit[:, s, cut(n)], iota_i1, ies[:, s, n:n + 1], rstd[:, s, n:n + 1],
                              ALU.is_equal, ALU.mult)
                last.then_inc(sem["e_sit"], 1)

            def gamma_out(g, u):
                dve.wait_ge(sem["e_ops"], GB * g + u + 1)
                if not first(g):
                    dve.wait_ge(sem["fin2"], g)
                tt(osb[:, cut(u)], o_ps, gab[:, :], ALU.mult).then_inc(sem["e_osb"], 1)

            def finish_a(g):
                dve.wait_ge(sem["fin3"], g + 1)
                for u in range(GB):
                    last = v.bn_stats(fbns[:, 6 * u:6 * u + 6], fin1[:, cut(u)])
                last.then_inc(sem["fbns"], 1)
                settle(dve)
                dve.wait_ge(sem["fbns"], g + 1)
                for u in range(GB):
                    last = v.bn_aggr(fmv[:, 2 * u:2 * u + 2], fbns[:, 6 * u:6 * u + 6])
                last.then_inc(sem["fbna"], 1)
                dve.wait_ge(sem["fbna"], g + 1)
                ts(f["vare"], fmv[:, 1:2 * GB:2], LN_EPS, None, ALU.add).then_inc(sem["fvare"], 1)

            def finish_b(g):
                frows.start(g)
                dve.wait_ge(sem["frs"], g + 1)
                newton(f, frows)
                if not first(g):
                    dve.wait_ge(sem["stored"], 16 * g)
                for u in range(GB):
                    last = ts(fo[:, cut(u)], fin1[:, cut(u)], fmv[:, 2 * u:2 * u + 1], f["rsn"][:, u:u + 1],
                              ALU.subtract, ALU.mult)
                last.then_inc(sem["fout"], 1)

            def body(a, b, e, f):
                if e is not None:
                    row_hot(e, 0)
                    ie_copy(e, 0)
                    col_hot(e, 0)
                if a is not None:
                    x_sq(a)
                if b is not None:
                    dot_x(b)
                if a is not None:
                    ranks_a(a)
                    reciprocals(a)
                if b is not None:
                    dot_m(b)
                if a is not None:
                    ranks_b(a)
                if e is not None:
                    row_hot(e, 1)
                    ie_copy(e, 1)
                    col_hot(e, 1)
                if b is not None:
                    clip_uq(b)
                if e is not None:
                    add_b2(e, 0)
                    row_hot(e, 2)
                    sum_sq(e, 0)
                if b is not None:
                    recip_un(b)
                if e is not None:
                    row_hot_t(e, 0)
                if b is not None:
                    tanh(b)
                if e is not None:
                    ie_copy(e, 2)
                    col_hot(e, 2)
                if f is not None:
                    finish_a(f)
                if e is not None:
                    add_b2(e, 1)
                    row_hot(e, 3)
                if a is not None:
                    clip_esig(a)
                if e is not None:
                    sum_sq(e, 1)
                if b is not None:
                    recip_de(b)
                if e is not None:
                    row_hot_t(e, 1)
                    ie_copy(e, 3)
                    col_hot(e, 3)
                if f is not None:
                    finish_b(f)
                if e is not None:
                    add_b2(e, 2)
                    row_hot(e, 4)
                if a is not None:
                    pairs_a(a)
                if e is not None:
                    sum_sq(e, 2)
                if e is not None:
                    gamma_out(e, 0)
                    row_hot_t(e, 2)
                    ie_copy(e, 4)
                    col_hot(e, 4)
                if a is not None:
                    pairs_b(a)
                if e is not None:
                    add_b2(e, 3)
                if b is not None:
                    norm0_a(b)
                if e is not None:
                    sum_sq(e, 3)
                if a is not None:
                    clip_u(a)
                if e is not None:
                    gamma_out(e, 1)
                    row_hot_t(e, 3)
                if b is not None:
                    norm0_b(b)
                if e is not None:
                    add_b2(e, 4)
                    gamma_out(e, 2)
                    sum_sq(e, 4)
                if b is not None:
                    split_r1(b, 0)
                    split_t2(b, 0)
                if e is not None:
                    row_hot_t(e, 4)
                if b is not None:
                    split_r1(b, 1)
                    split_t2(b, 1)
                if e is not None:
                    gamma_out(e, 3)

            run_groups(dve, body)

            dve.wait_ge(sem["bad"], groups)
            v.tensor_reduce(fl[:, 0:1], bad_all[:, 0:groups], AX_X, ALU.add).then_inc(sem["badr"], 1)
            dve.wait_ge(sem["nall"], 2)
            ts(okn[:, 0:GB * groups], y_ps[:, 0:GB * groups], float(CAP), None, ALU.is_le).then_inc(sem["okn"], 1)
            ts(fl[:, 1:2], y_ps[:, 128:129], 0.0, None, ALU.is_le).then_inc(sem["okn"], 1)
            dve.wait_ge(sem["okn"], 2)
            v.tensor_reduce(fl[:, 2:3], okn[:, 0:GB * groups], AX_X, ALU.min).then_inc(sem["okn"], 1)
            dve.wait_ge(sem["okn"], 3)
            tt(fl[:, 3:4], fl[:, 1:2], fl[:, 2:3], ALU.mult).then_inc(sem["flagf"], 1)
            dve.wait_ge(sem["flagf"], 1)
            dve.wait_ge(sem["e_osb"], GB * groups)
            ts(flagi[:, :], fl[:, 3:4], -1.0, 1.0, ALU.mult, ALU.add).then_inc(sem["flag"], 1)

            def dense():
                drows = Chain(dve, sem["dense_rows"], DENSE_ROW_STEPS)
                with dve.Fori(0, NB) as b:
                    with dve.Fori(0, N) as i:
                        q = N * b + i
                        settle(dve)
                        dve.wait_ge(sem["dense_hidden_ready"], (N + 2) * b + i + 2)
                        ts(g_h, g_hj, g_hi[:, bass.ds(i, 1)], 0.0, ALU.add, ALU.max).then_inc(sem["dense_h"], 1)
                        dve.wait_ge(sem["dense_y"], q + 1)
                        tt(g_z, y_ps[:, 0:128], b2c[:, :], ALU.add).then_inc(sem["dense_z"], 1)
                        settle(dve)
                        dve.wait_ge(sem["dense_r"], q + 1)
                        tt(g_w, g_r, g_adjt[:, bass.ds(i, 1)], ALU.mult).then_inc(sem["dense_w"], 1)
                    drows.start(b)
                    dve.wait_ge(sem["dense_turned"], b + 1)
                    drows(tt(g_rows, lg_ps[:, 0:128], gab[:, :], ALU.mult))
                    drows(v.tensor_reduce(g_deg, g_adj, AX_X, ALU.add))
                    drows(stt(g_rows, beb[:, :], g_deg, g_rows, ALU.mult, ALU.add))
                    drows(tt(g_rows, g_rows, g_x1, ALU.add))
                    v.bn_stats(g_bns, g_rows).then_inc(sem["dense_bns"], 1)
                    settle(dve)
                    dve.wait_ge(sem["dense_bns"], b + 1)
                    v.bn_aggr(g_mv, g_bns).then_inc(sem["dense_rows"], 1)
                    drows.k += 1
                    dve.wait_ge(sem["dense_rows"], drows.base + drows.k)
                    ts(g_var, g_mv[:, 1:2], LN_EPS, None, ALU.add).then_inc(sem["dense_var"], 1)
                    dve.wait_ge(sem["dense_rs"], b + 1)
                    newton(g_tiny, drows)
                    dve.wait_ge(sem["dense_stored"], 16 * b + 16)
                    ts(g_out, g_rows, g_mv[:, 0:1], g_tiny["rsn"], ALU.subtract, ALU.mult).then_inc(sem["dense_out"], 1)

            where_dense(dve, dense)

        @block.tensor
        def _(pe):
            mm = nc.tensor.matmul

            pe.wait_ge(sem["const"], 16 * 11)
            pe.wait_ge(sem["selb"], 3)
            pe.wait_ge(sem["w2c"], 1)

            def logits_raw(g):
                pe.wait_ge(sem["xt_loaded"], 16 * g + 16)
                if not first(g):
                    pe.wait_ge(sem["sws"], g)
                for u in range(GB):
                    last = mm(lr_ps[:, 2 * u:2 * u + 2], xts[:, cut(u)], wlr[:, :], start=True, stop=True)
                last.then_inc(sem["lr"], 1)

            def turn_rows(g):
                pe.wait_ge(sem["rowsb"], g + 1)
                pe.wait_ge(sem["lrc"], g + 1)
                nc.tensor.transpose(rt_ps, rowsb[:, :], identb[:, :]).then_inc(sem["rowst_ps"], 1)

            def spread_rows(g):
                pe.wait_ge(sem["rowst"], g + 1)
                for u in range(GB):
                    last = mm(bj_ps[:, cut(u)], selv[:, BB, u, :], rowst[:, :], start=True, stop=True)
                last.then_inc(sem["bj_ps"], 1)
                if not first(g):
                    pe.wait_ge(sem["esig"], g)
                if not (isinstance(g, int) and g < 2):
                    pe.wait_ge(sem["e_r1"], 2 * g - 2)
                for u in range(GB):
                    mm(lg_ps[:, cut(u)], rowst[:, :], selv[:, RR, u, :], start=True, stop=False)
                    last = mm(lg_ps[:, cut(u)], selv[:, LL, u, :], rowst[:, :], start=False, stop=True)
                last.then_inc(sem["lg"], 1)

            def gram(g):
                pe.wait_ge(sem["xm2"], g + 1)
                if not first(g):
                    pe.wait_ge(sem["nm"], g)
                    pe.wait_ge(sem["den"], g)
                for u in range(GB):
                    d2 = d2_ps[:, cut(u)]
                    mm(d2, xts[:, cut(u)], xm2[:, cut(u)], start=True, stop=False)
                    mm(d2, rowst[:, :], selv[:, X2, u, :], start=False, stop=False)
                    last = mm(d2, selv[:, X2, u, :], rowst[:, :], start=False, stop=True)
                last.then_inc(sem["d2"], 1)

            def with_x(g):
                pe.wait_ge(sem["wt"], g + 1)
                if not first(g):
                    pe.wait_ge(sem["hh"], g)
                pe.wait_ge(sem["bjs"], g + 1)
                pe.wait_ge(sem["xcol"], g + 1)
                for u in range(GB):
                    last = mm(sw_ps[:, 2 * u:2 * u + 2], wt[:, cut(u)], onex2[:, 2 * u:2 * u + 2], start=True, stop=True)
                last.then_inc(sem["sw"], 1)
                for u in range(GB):
                    last = mm(m_ps[:, cut(u)], wt[:, cut(u)], bt(x_all, GB * g + u), start=True, stop=True)
                last.then_inc(sem["mm"], 1)

            def turn_x1(g, a):
                pe.wait_ge(sem["x1s"], g + 1)
                pe.wait_ge(sem["esig"], groups if a is None else a + 1)
                if not first(g):
                    pe.wait_ge(sem["e_r1"], 2 * g)
                for u in range(GB):
                    last = nc.tensor.transpose(lg_ps[:, cut(u)], x1s[:, cut(u)], ident)
                last.then_inc(sem["x1t_ps"], 1)

            def offsets(g, e):
                pe.wait_ge(sem["degs"], g + 1)
                if not first(g):
                    pe.wait_ge(sem["offc"], g)
                if e is not None:
                    pe.wait_ge(sem["e_ies"], TILES * e + 1)
                    if not first(e):
                        pe.wait_ge(sem["e_osb"], GB * e)
                mm(off_ps, tri, c["dg"], start=True, stop=True).then_inc(sem["off"], 1)

            def tables(g, half):
                pe.wait_ge(sem["x1t"], g + 1)
                if half == 1:
                    pe.wait_ge(sem["e_r1"], 2 * g + 1)
                for u in range(2):
                    last = mm(lg_ps[:, 256 * u:256 * u + 256], x1t[:, cut(2 * half + u)], w1c[:, :], start=True, stop=True)
                last.then_inc(sem["e_tab"], 1)

            def row_ranks(g, k):
                q, s = TILES * g + k, slot(k)
                pe.wait_ge(sem["e_si"], q + 1)
                pe.wait_ge(sem["vt"], g + 1)
                if not (first(g) and k == 0):
                    pe.wait_ge(sem["e_sj"], q)
                if k == 0:
                    for u in range(GB):
                        last = mm(vg_ps[:, cut(u)], bt(vt_all, GB * g + u), si[:, s, cut(u)], start=True, stop=True)
                else:
                    last = mm(vg_ps, bt(vt_all, GB * g + k - 1), si[:, s, :], start=True, stop=True)
                last.then_inc(sem["e_vg"], 1)

            def row_numbers(g, k, a):
                q, s = TILES * g + k, slot(k)
                pe.wait_ge(sem["e_si"], q + 1)
                pe.wait_ge(sem["offc"], groups if a is None else a + (k > 0))
                if not (first(g) and k == 0):
                    pe.wait_ge(sem["e_ies"], q)
                if k > 3:
                    pe.wait_ge(sem["e_osb"], GB * g + k - 3)
                elif not first(g):
                    pe.wait_ge(sem["e_osb"], GB * g)
                for n in range(CH):
                    last = mm(ie_ps[:, n:n + 1], si[:, s, cut(n)], colb[:, :], start=True, stop=True)
                last.then_inc(sem["e_ie"], 1)

            def gather(g, k):
                q, s = TILES * g + k, slot(k)
                pe.wait_ge(sem["e_sj"], q + 1)
                pe.wait_ge(sem["e_t2b"], 2 * g + 2)
                if not (first(g) and k == 0):
                    pe.wait_ge(sem["e_ht"], q)
                spans = [(u, cut(u)) for u in range(GB)] if k == 0 else [(k - 1, slice(0, T))]
                for u, cols_ in spans:
                    for n in range(PARTS):
                        mm(h_ps[:, cols_], tb[:, u, n, 0:128], si[:, s, cols_], start=(n == 0), stop=False)
                        last = mm(h_ps[:, cols_], tb[:, u, n, 128:256], sj[:, s, cols_],
                                  start=False, stop=(n == PARTS - 1))
                last.then_inc(sem["e_hps"], 1)

            def second(g, k):
                q = TILES * g + k
                pe.wait_ge(sem["e_ht"], q + 1)
                if not (first(g) and k == 0):
                    pe.wait_ge(sem["e_z"], q)
                for n in range(CH):
                    last = mm(y_ps[:, cut(n)], ht[:, cut(n)], w2c[:, :], start=True, stop=True)
                last.then_inc(sem["e_yps"], 1)

            def add_rows(g, k):
                q, s = TILES * g + k, slot(k)
                pe.wait_ge(sem["e_sit"], q + 1)
                pe.wait_ge(sem["e_z"], q + 1)
                pe.wait_ge(sem["e_ies"], TILES * g + min(k + 2, TILES - 1) + 1)
                if not (first(g) and k == 1):
                    pe.wait_ge(sem["e_osb"], GB * g + k - 1)
                mm(o_ps, sit[:, 0, cut(k - 1)], z[:, 0, cut(k - 1)], start=True, stop=False)
                for n in range(CH):
                    last = mm(o_ps, sit[:, s, cut(n)], z[:, s, cut(n)], start=False, stop=(n == CH - 1))
                last.then_inc(sem["e_ops"], 1)

            def body(a, b, e, f):
                if b is not None:
                    with_x(b)
                if e is not None:
                    row_ranks(e, 0)
                    row_numbers(e, 0, a)
                if a is not None:
                    logits_raw(a)
                    offsets(a, e)
                if e is not None:
                    gather(e, 0)
                    row_ranks(e, 1)
                    row_numbers(e, 1, a)
                if a is not None:
                    turn_rows(a)
                if e is not None:
                    second(e, 0)
                if e is not None:
                    gather(e, 1)
                    row_ranks(e, 2)
                    row_numbers(e, 2, a)
                if a is not None:
                    spread_rows(a)
                if e is not None:
                    second(e, 1)
                if a is not None:
                    gram(a)
                if e is not None:
                    gather(e, 2)
                    row_ranks(e, 3)
                    row_numbers(e, 3, a)
                    second(e, 2)
                    add_rows(e, 1)
                if e is not None:
                    gather(e, 3)
                    row_ranks(e, 4)
                    row_numbers(e, 4, a)
                    second(e, 3)
                    add_rows(e, 2)
                if e is not None:
                    gather(e, 4)
                    second(e, 4)
                if b is not None:
                    turn_x1(b, a)
                if e is not None:
                    add_rows(e, 3)
                if b is not None:
                    tables(b, 0)
                if e is not None:
                    add_rows(e, 4)
                if b is not None:
                    tables(b, 1)

            run_groups(pe, body)
            pe.wait_ge(sem["dega"], 2 * groups)
            pe.wait_ge(sem["badr"], 1)
            mm(y_ps[:, 0:GB * groups], ones_f, deg_all[:, 0:GB * groups], start=True, stop=True).then_inc(sem["nall"], 1)
            mm(y_ps[:, 128:129], ones_f, fl[:, 0:1], start=True, stop=True).then_inc(sem["nall"], 1)

            def dense():
                with pe.Fori(0, NB) as b:
                    pe.wait_ge(sem["dense_x1"], b + 1)
                    nc.tensor.transpose(lg_ps[:, 0:128], g_x1, ident).then_inc(sem["dense_x1t_ps"], 1)
                    pe.wait_ge(sem["dense_x1t"], b + 1)
                    mm(h_ps[:, 0:128], w1c[:, 0:128], g_x1t, start=True, stop=True)
                    mm(h_ps[:, 128:256], w1c[:, 128:256], g_x1t, start=True, stop=True).then_inc(sem["dense_hps"], 1)
                    with pe.Fori(0, N) as i:
                        q = N * b + i
                        pe.wait_ge(sem["dense_h"], q + 1)
                        mm(y_ps[:, 0:128], g_h, w2c[:, :], start=True, stop=True).then_inc(sem["dense_y"], 1)
                        pe.wait_ge(sem["dense_w"], q + 1)
                        mm(o_ps[:, 0:1], g_z, g_w, start=True, stop=True).then_inc(sem["dense_o"], 1)
                    pe.wait_ge(sem["dense_hidden_ready"], (N + 2) * b + N + 2)
                    nc.tensor.transpose(lg_ps[:, 0:128], g_o, ident).then_inc(sem["dense_turned"], 1)

            where_dense(pe, dense)


def constants():
    import numpy as np

    k = np.arange(128)
    tri = (k[:, None] < k[None, :]).astype(np.float32)
    reset = np.tile((k > 0).astype(np.float32), (128, GB))
    f32 = np.concatenate([tri, np.eye(128, dtype=np.float32), np.ones((128, 128), np.float32), reset,
                          np.zeros((128, 1), np.float32)], 1)
    e = np.arange(CAP)
    fp16 = np.concatenate([np.tile(e, (128, 1)), np.tile(e[:T] + 1, (128, 1)),
                           np.tile(e[T:] + 1, (128, GB)), np.tile(k + 1, (128, 1)),
                           (k + 1)[:, None]], 1).astype(np.float16)
    rows = np.arange(PARTS * ROWS) % ROWS
    want = np.array([[4 * b + t for b in range(GB)] for t in range(4)])
    sel = (rows[:, None, None] == want[None]).astype(np.float16)
    sel = np.repeat(sel.reshape(PARTS * ROWS, 4 * GB), 128, axis=1)
    return {"c_f32": f32, "c_fp16": fp16, "c_sel": sel}


def kernel(**inputs):
    import numpy as np
    import concourse.bacc as bacc
    from concourse.bass_utils import run_bass_kernel_spmd

    a = {k: np.asarray(v) for k, v in inputs.items()}

    def flat(v):
        return np.ascontiguousarray(v).reshape(128, NB * 128)

    arrays = {
        "x_n": flat(a["x"].transpose(1, 0, 2)), "x_t": flat(a["x"].transpose(2, 0, 1)),
        "adj_n": flat(a["adj"].transpose(1, 0, 2)), "adj_t": flat(a["adj"].transpose(2, 0, 1)),
        "att_w": a["L0_gnn_att_w"].reshape(2, 128).T, "att_b": a["L0_gnn_att_b"].reshape(1),
        "W1": a["L1_gnn_W1"].reshape(2, 128, 128).transpose(1, 0, 2).reshape(128, 256),
        "b1": a["L1_gnn_b1"].reshape(128, 1), "W2": a["L1_gnn_W2"], "b2": a["L1_gnn_b2"],
        "gamma": a["L1_gnn_gamma"], "beta": a["L1_gnn_beta"], **constants(),
    }
    nc = bacc.Bacc("TRN2", target_bir_lowering=False, num_devices=1)
    aps = {}
    for name, v in arrays.items():
        arrays[name] = v = np.ascontiguousarray(v)
        aps[name] = nc.dram_tensor(name, v.shape, mybir.dt.from_np(v.dtype), kind="ExternalInput").ap()
    out = nc.dram_tensor("out", (128, NB * 128), F32, kind="ExternalOutput").ap()
    two_graph_layers(nc, out=out, **aps)
    r = run_bass_kernel_spmd(nc, [arrays], core_ids=[0])
    return np.ascontiguousarray(r.results[0]["out"].reshape(128, NB, 128).transpose(1, 0, 2))
```

```python
from contextlib import ExitStack

import concourse.bass as bass
from concourse import mybir

NB = 64
N = 128
D = 128
GB = 4
NG = NB // GB
W = GB * N
CH = 4
T = CH * 128
TILES = GB + 1
CAP = T + 128
PARTS = 3
ROWS = 4 * GB
X2, BB, LL, RR = range(4)

MIN_NORM = 1e-15
CLIP = 1.0 - 1e-7
LN_EPS = 1e-5
LOG_MIN_NORM = -34.538776394910684
ROW_STEPS, COL_STEPS, DENSE_ROW_STEPS = 28, 14, 8
UQ_STEP, DE_STEP = 13, 21
TINY = 2.0 ** -60
SIG_MAX = 1e19

ALU = mybir.AluOpType
ACT = mybir.ActivationFunctionType
F32 = mybir.dt.float32
BF16 = mybir.dt.bfloat16
FP16 = mybir.dt.float16
I32 = mybir.dt.int32
AX_X = mybir.AxisListType.X

GROUP_STEPS = """loaded adj_loaded adjt_loaded xt_loaded xm2 lr sqx x2 x2m lpn pn pcl at1 at2 xcol lrc rowsb rowst_ps rowst d2 bj_ps
lg bjs esig esigc lse den nm denc lnn lnd ls lsc uu ucl l1 l2 qe q2e w0 dl w1 wt mm sw xmp sqm sws uqm lun un zz ez
ga tx hh bns bna vare lv rs x1s x1a x1t_ps x1t scan degs dega off offc mid rank vt bsq bdiff bad
held bc bm rbm rpn xmr mmr run th dec rd newton
fin1 fin2 fin3 fbns fbna fvare flv frs fout stored rows frows cols""".split()
BATCH_STEPS = "tab t0 r1 t1 t2b absd si vg ie ies sj hps ht yps z ss lnv rstd sit ops osb".split()
ONCE_STEPS = "const selb w2sum w2c b2c ones badr nall okn flagf flag".split()
DENSE_STEPS = "loaded x1 x1t_ps x1t hps hidden_ready h y z sq lv r w o turned rows bns var lv2 rs out stored".split()


def two_graph_layers(nc, x_n, x_t, adj_n, adj_t, att_w, att_b, W1, b1, W2, b2, gamma, beta,
                     c_f32, c_fp16, c_sel, out, groups=NG):
    with ExitStack() as ctx:
        def sb(name, shape, dt=F32):
            return ctx.enter_context(nc.sbuf_tensor(name, shape, dt))

        sem = {n: ctx.enter_context(nc.semaphore(f"s_{n}"))
                                 for n in GROUP_STEPS + ["e_" + b for b in BATCH_STEPS] + ONCE_STEPS
                                 + ["dense_" + d for d in DENSE_STEPS]
                                 }

        x_all = sb("x_all", [128, NB * D])
        x1_all = sb("x1_all", [128, NB * D])
        vt_all = sb("vt_all", [128, NB * N], FP16)
        deg_all = sb("deg_all", [128, NB])
        half_all = sb("half_all", [128, NB])
        mid_all = sb("mid_all", [128, NB])
        bad_all = sb("bad_all", [128, NG])

        cf = sb("cf", [128, 3 * 128 + 512 + 1])
        tri, ident, ones_f = cf[:, 0:128], cf[:, 128:256], cf[:, 256:384]
        reset = cf[:, 384:896]
        ch = sb("ch", [128, CAP + 2 * T + 128 + 1], FP16)
        iota_e = ch[:, 0:CAP]
        rank_main = ch[:, CAP:CAP + T]
        rank_tail = ch[:, CAP + T:CAP + 2 * T]
        iota_i1, col_i1 = ch[:, CAP + 2 * T:CAP + 2 * T + 128], ch[:, CAP + 2 * T + 128:CAP + 2 * T + 129]
        colb = sb("colb", [128, 1], BF16)
        identb = sb("identb", [128, 128], BF16)
        selb = sb("selb", [PARTS * ROWS, 4 * GB * 128], BF16)
        selv = selb[:, :].rearrange("k (t b n) -> k t b n", t=4, b=GB)
        wlr = sb("wlr", [128, 2])
        attb = sb("attb", [128, 1])
        w1c = sb("w1c", [128, 256])
        b1c = sb("b1c", [128, 1])
        w2 = sb("w2", [128, 128])
        w2s = sb("w2s", [128, 1])
        w2c = sb("w2c", [128, 128])
        b2b = sb("b2b", [128, 128])
        b2s = sb("b2s", [128, 1])
        b2c = sb("b2c", [128, 128])
        gab = sb("gab", [128, 128])
        beb = sb("beb", [128, 128])
        b2r = sb("b2r", [128, 128])
        b2p = sb("b2p", [128, PARTS, 128], BF16)
        b2k = sb("b2k", [128, 128], BF16)
        onesb = sb("onesb", [PARTS, 128], BF16)
        eps1 = sb("eps1", [128, 1])
        one1 = sb("one1", [128, 1])

        xts = sb("xts", [128, W])
        xm2 = sb("xm2", [128, W])
        adjt = sb("adjt", [128, W])
        adjs = sb("adjs", [128, W])
        sqx, bjs, esig, lse, den, nm, lnn, lnd, ls, uw, ucl, l1, l2, qe, q2e, w0, dl, w1, wt = (
            sb(n, [128, W]) for n in "sqx bjs esig lse den nm lnn lnd ls uw ucl l1 l2 qe q2e w0 dl w1 wt".split())
        xmp, sqm, tx, hh, x1s, x1t = (sb(n, [128, W]) for n in "xmp sqm tx hh x1s x1t".split())
        tiny = sb("tiny", [128, 80 * GB])
        tiny_names = """x2 bc bm hbm be rbm hx2 hbc hbm_ hbm2 hbe hrbm x2m lpn pn pcl at1 at2 rpn dat fac0 fac lcol
        xmr mmr c1 m1 m2 al ax bx xu t2 t3 t4 t5 t6 uq uqm lun un zz ez e1 re th run rho r2 s1 rxu tw0 tw nx de dec
        rd rr gg ga2 ga0 ga t7 t8 t9 vare lv rs ra rb rsn dg""".split()
        c = {n: tiny[:, GB * k:GB * (k + 1)] for k, n in enumerate(tiny_names)}
        fresh, held = tiny[:, 0:6 * GB], tiny[:, 6 * GB:12 * GB]
        h = dict(x2=c["hx2"], bc=c["hbc"], bm=c["hbm_"], hbm=c["hbm2"], be=c["hbe"], rbm=c["hrbm"])
        half_c = sb("half_c", [128, GB])
        vals = sb("vals", [128, ROWS])
        vv = vals[:, :].rearrange("p (b t) -> p t b", t=4)
        q1 = sb("q1", [128, ROWS])
        q2 = sb("q2", [128, ROWS])
        rowsb = sb("rowsb", [128, 128], BF16)
        rowst = sb("rowst", [PARTS * ROWS, 128], BF16)
        onex2 = sb("onex2", [128, 2 * GB])
        lrs = sb("lrs", [128, 2 * GB])
        sws = sb("sws", [128, 2 * GB])
        bns = sb("bns", [128, 6 * GB])
        mv = sb("mv", [128, 2 * GB])
        scan = sb("scan", [128, W])
        rank = sb("rank", [128, W])
        offc = sb("offc", [128, GB])
        bsq = sb("bsq", [128, W])

        tb = sb("tb", [128, GB, PARTS, 256], BF16)
        r1 = sb("r1", [128, 2, 512])
        absd = sb("absd", [128, T], FP16)
        si = sb("si", [128, 3, T], BF16)
        sj = sb("sj", [128, 3, T], BF16)
        ies = sb("ies", [128, 3, CH])
        ht = sb("ht", [128, T])
        z = sb("z", [128, 3, T])
        self_ = z[0:PARTS * ROWS, 0:2, :].rearrange("k s t -> k (s t)").bitcast(FP16)
        sq = sb("sq", [128, T])
        ss = sb("ss", [128, 3, CH])
        lnv = sb("lnv", [128, 3, CH])
        rstd = sb("rstd", [128, 3, CH])
        sit = sb("sit", [128, 3, T])
        osb = sb("osb", [128, W])
        fin1 = sb("fin1", [128, W])
        fbns = sb("fbns", [128, 6 * GB])
        fmv = sb("fmv", [128, 2 * GB])
        ftiny = sb("ftiny", [128, 8 * GB])
        f = {n: ftiny[:, GB * k:GB * (k + 1)]
                               for k, n in enumerate("vare lv rs ra rb rc rsn".split())}
        fo = sb("fo", [128, W])
        okn = sb("okn", [128, NB])
        fl = sb("fl", [128, 8])
        flagi = sb("flagi", [128, 1], I32)

        g_x1, g_x1t, g_hi, g_hj = xts[:, 0:128], xts[:, 128:256], xts[:, 256:384], xts[:, 384:512]
        g_h, g_z, g_sq, g_o = xm2[:, 0:128], xm2[:, 128:256], xm2[:, 256:384], xm2[:, 384:512]
        g_adj, g_adjt, g_rows, g_out = adjs[:, 0:128], adjt[:, 0:128], sqx[:, 0:128], fo[:, 0:128]
        g_ss, g_lv, g_r, g_w, g_deg, g_var, g_lv2, g_rs = (fbns[:, k:k + 1] for k in range(8))
        g_tiny = dict(vare=g_var, rs=g_rs, ra=fbns[:, 8:9], rb=fbns[:, 9:10], rsn=fbns[:, 10:11])
        g_bns, g_mv = bns[:, 0:6], mv[:, 0:2]

        banks = [ctx.enter_context(nc.psum_tensor(f"bank{k}", [128, 512], F32)) for k in range(8)]
        vg_ps, h_ps, y_ps = (b[:, :] for b in banks[0:3])
        o_ps, ie_ps, off_ps = banks[3][:, 0:128], banks[3][:, 128:128 + 2 * CH], banks[3][:, 136:136 + GB]
        lg_ps = banks[4][:, :]
        d2_ps = banks[5][:, :]
        m_ps = banks[7][:, :]
        tab_ps = [banks[4][:, :], banks[7][:, :]]
        bj_ps = banks[6][:, :]
        lr_ps = banks[3][:, 144:152]
        rt_ps, sw_ps = banks[6][:, 64:128].bitcast(BF16), banks[6][:, 128:136]

        def grp(t, g, width=W):
            return t[:, bass.ds(g * width, width)]

        def bt(t, b, width=128):
            return t[:, bass.ds(b * width, width)]

        def cut(u):
            return slice(128 * u, 128 * (u + 1))

        def wide(a):
            return a.rearrange("p (b n) -> p b n", b=GB)

        def spread(col):
            return col.unsqueeze(2).to_broadcast([128, GB, 128])

        def settle(eng):
            eng.wait_ge(sem["ones"], 2)

        class Chain:

            def __init__(self, eng, sem_, steps):
                self.eng, self.sem, self.steps = eng, sem_, steps

            def start(self, g):
                self.base, self.k = g * self.steps, 0

            def __call__(self, ins, wait=True):
                self.k += 1
                ins.then_inc(self.sem, 1)
                if wait:
                    self.eng.wait_ge(self.sem, self.base + self.k)

            def end(self):
                assert self.k == self.steps, self.k

        def where_dense(eng, body):
            eng.wait_ge(sem["flag"], 1)
            found = eng.value_load(flagi[0:1, 0:1], min_val=0, max_val=1)
            with eng.If(found > 0):
                body()

        def slot(k):
            return 0 if k == 0 else 1 + (k - 1) % 2

        def reuse(g, k):
            if first(g) and k < 3:
                return None
            return TILES * g + k - (5, 3, 3, 2, 2)[k] + 1

        def first(g):
            return isinstance(g, int) and g == 0

        block = ctx.enter_context(nc.Block())

        def run_groups(eng, body):
            def turn(t):
                body(*(t - lag if 0 <= t - lag < groups else None for lag in range(4)))

            for t in range(4):
                turn(t)
            with eng.Fori(1, groups - 3) as g:
                body(g + 3, g + 2, g + 1, g)
            for t in range(groups, groups + 3):
                turn(t)

        @block.sync
        def _(sp):
            def load(dst, src):
                sp.dma_start(dst, src).then_inc(sem["const"], 16)

            load(cf[:, :], c_f32)
            load(ch[:, :], c_fp16)
            load(self_, c_sel)
            load(wlr[:, :], att_w)
            load(attb[:, :], att_b.partition_broadcast(128))
            load(w1c[:, :], W1)
            load(b1c[:, :], b1)
            load(w2[:, :], W2)
            load(b2b[:, :], b2.partition_broadcast(128))
            load(gab[:, :], gamma.partition_broadcast(128))
            load(beb[:, :], beta.partition_broadcast(128))

            def load_adj(g):
                if not first(g):
                    sp.wait_ge(sem["loaded"], 16 * g)
                    sp.wait_ge(sem["scan"], g)
                    sp.wait_ge(sem["vt"], g)
                    sp.wait_ge(sem["bdiff"], g)
                sp.dma_start(adjs[:, :], grp(adj_n, g)).then_inc(sem["adj_loaded"], 16)

            def load_x(g):
                if not first(g):
                    sp.wait_ge(sem["d2"], g)
                    sp.wait_ge(sem["lr"], g)
                    sp.wait_ge(sem["xm2"], g)
                sp.dma_start(xts[:, :], grp(x_t, g)).then_inc(sem["xt_loaded"], 16)
                sp.dma_start(grp(x_all, g), grp(x_n, g)).then_inc(sem["loaded"], 16)

            def load_adjt(g):
                if not first(g):
                    sp.wait_ge(sem["w1"], g)
                sp.dma_start(adjt[:, :], grp(adj_t, g)).then_inc(sem["adjt_loaded"], 16)

            def body(a, b, e, f):
                if a is not None:
                    load_adj(a)
                    load_x(a)
                    load_adjt(a)

            run_groups(sp, body)

            def dense():
                sp.wait_ge(sem["stored"], 16 * groups)
                sp.dma_start(g_out, bt(out, 0)).then_inc(sem["dense_stored"], 16)
                with sp.Fori(0, NB) as b:
                    sp.dma_start(g_adj, bt(adj_n, b)).then_inc(sem["dense_loaded"], 16)
                    sp.dma_start(g_adjt, bt(adj_t, b)).then_inc(sem["dense_loaded"], 16)
                    settle(sp)
                    sp.wait_ge(sem["dense_out"], b + 1)
                    sp.dma_start(bt(out, b), g_out).then_inc(sem["dense_stored"], 16)
                sp.wait_ge(sem["dense_stored"], 16 * NB + 16)

            where_dense(sp, dense)

        @block.gpsimd
        def _(pool):
            tt = nc.gpsimd.tensor_tensor
            ones_c = ones_f[:, 0:GB]
            cols, rows = Chain(pool, sem["cols"], COL_STEPS), Chain(pool, sem["rows"], ROW_STEPS)

            def badness(g):
                pool.wait_ge(sem["adj_loaded"], 16 * g + 16)
                if not first(g):
                    pool.wait_ge(sem["bad"], g)
                tt(bsq[:, :], adjs[:, :], adjs[:, :], ALU.mult).then_inc(sem["bsq"], 1)
                pool.wait_ge(sem["bsq"], g + 1)
                tt(bsq[:, :], bsq[:, :], adjs[:, :], ALU.subtract).then_inc(sem["bdiff"], 1)

            def rank_edges(g):
                settle(pool)
                pool.wait_ge(sem["scan"], g + 1)
                pool.wait_ge(sem["offc"], g + 1)
                if not first(g):
                    pool.wait_ge(sem["vt"], g)
                tt(wide(rank[:, :]), wide(scan[:, :]), spread(offc[:, :]), ALU.add).then_inc(sem["rank"], 1)

            def mask_ranks(g):
                settle(pool)
                pool.wait_ge(sem["rank"], g + 1)
                tt(grp(vt_all, g), rank[:, :], adjs[:, :], ALU.mult).then_inc(sem["vt"], 1)

            def weights_1(g):
                pool.wait_ge(sem["lnd"], g + 1)
                pool.wait_ge(sem["lse"], g + 1)
                if not first(g):
                    pool.wait_ge(sem["qe"], g)
                tt(q2e[:, :], lnd[:, :], lse[:, :], ALU.add).then_inc(sem["q2e"], 1)

            def weights_2(g):
                settle(pool)
                pool.wait_ge(sem["w0"], g + 1)
                pool.wait_ge(sem["adjt_loaded"], 16 * g + 16)
                tt(w1[:, :], w0[:, :], adjt[:, :], ALU.mult).then_inc(sem["w1"], 1)

            def weights_3(g):
                pool.wait_ge(sem["l1"], g + 1)
                pool.wait_ge(sem["l2"], g + 1)
                tt(dl[:, :], l1[:, :], l2[:, :], ALU.subtract).then_inc(sem["dl"], 1)

            def weights_4(g):
                pool.wait_ge(sem["w1"], g + 1)
                pool.wait_ge(sem["dl"], g + 1)
                if not first(g):
                    pool.wait_ge(sem["mm"], g)
                    pool.wait_ge(sem["sw"], g)
                tt(wt[:, :], w1[:, :], dl[:, :], ALU.mult).then_inc(sem["wt"], 1)

            def hold(g):
                if not first(g):
                    pool.wait_ge(sem["ga"], g)
                pool.wait_ge(sem["rbm"], g + 1)
                pool.wait_ge(sem["cols"], COL_STEPS * g + COL_STEPS)
                pool.wait_ge(sem["bm"], g + 1)
                tt(held, fresh, ones_f[:, 0:6 * GB], ALU.mult).then_inc(sem["held"], 1)

            def cols_1(g):
                cols.start(g)
                pool.wait_ge(sem["x2"], g + 1)
                pool.wait_ge(sem["bc"], g + 1)
                pool.wait_ge(sem["const"], 16 * 11)
                pool.wait_ge(sem["ones"], 2)
                if not first(g):
                    pool.wait_ge(sem["held"], g)
                cols(tt(vv[:, BB, :], c["bc"], ones_c, ALU.mult), wait=False)
                cols(tt(vv[:, X2, :], c["x2"], ones_c, ALU.mult), wait=False)
                pool.wait_ge(sem["bm"], g + 1)
                cols(tt(c["hbm"], c["bm"], half_c[:, :], ALU.mult))
                cols(tt(c["be"], c["hbm"], c["bc"], ALU.mult), wait=False)

            def keep_x2(g):
                pool.wait_ge(sem["x2"], g + 1)
                if not first(g):
                    pool.wait_ge(sem["sw"], g)
                tt(onex2[:, 1:2 * GB:2], c["x2"], ones_c, ALU.mult).then_inc(sem["xcol"], 1)

            def cols_2(g):
                pool.wait_ge(sem["at1"], g + 1)
                pool.wait_ge(sem["at2"], g + 1)
                cols(tt(c["dat"], c["at1"], c["at2"], ALU.subtract))
                pool.wait_ge(sem["rpn"], g + 1)
                cols(tt(c["fac0"], c["dat"], c["rpn"], ALU.mult))
                cols(tt(c["fac"], c["fac0"], half_c[:, :], ALU.mult))
                pool.wait_ge(sem["lrc"], g + 1)
                cols(tt(vv[:, RR, :], lrs[:, 1:2 * GB:2], c["fac"], ALU.mult), wait=False)
                cols(tt(c["lcol"], lrs[:, 0:2 * GB:2], c["fac"], ALU.mult))
                cols(tt(vv[:, LL, :], c["lcol"], attb[:, :].to_broadcast([128, GB]), ALU.add))

            def split_rows(g):
                if not first(g):
                    pool.wait_ge(sem["rowst_ps"], g)
                ones_r = ones_f[:, 0:ROWS]
                cols(tt(rowsb[:, 0:ROWS], vals[:, :], ones_r, ALU.mult))
                cols(tt(q1[:, :], vals[:, :], rowsb[:, 0:ROWS], ALU.subtract))
                cols(tt(rowsb[:, ROWS:2 * ROWS], q1[:, :], ones_r, ALU.mult))
                cols(tt(q2[:, :], q1[:, :], rowsb[:, ROWS:2 * ROWS], ALU.subtract))
                tt(rowsb[:, 2 * ROWS:3 * ROWS], q2[:, :], ones_r, ALU.mult).then_inc(sem["rowsb"], 1)
                pool.wait_ge(sem["rowsb"], g + 1)
                cols.end()

            def rows_1(g):
                rows.start(g)
                pool.wait_ge(sem["held"], g + 1)
                pool.wait_ge(sem["sws"], g + 1)
                rows(tt(c["c1"], sws[:, 0:2 * GB:2], sws[:, 1:2 * GB:2], ALU.add))
                rows(tt(c["m1"], h["hbm"], c["c1"], ALU.mult), wait=False)
                pool.wait_ge(sem["xmr"], g + 1)
                rows(tt(c["bx"], h["be"], c["xmr"], ALU.mult), wait=False)
                rows(tt(c["m2"], h["bm"], c["xmr"], ALU.mult))
                rows(tt(c["al"], c["m2"], c["m1"], ALU.subtract))
                rows(tt(c["ax"], c["al"], h["x2"], ALU.mult))
                rows(tt(c["xu"], c["ax"], c["bx"], ALU.add))
                rows(tt(c["t2"], c["al"], c["xu"], ALU.mult), wait=False)
                rows(tt(c["t3"], c["al"], c["xmr"], ALU.mult), wait=False)
                pool.wait_ge(sem["mmr"], g + 1)
                rows(tt(c["t4"], h["be"], c["mmr"], ALU.mult))
                rows(tt(c["t5"], c["t3"], c["t4"], ALU.add))
                rows(tt(c["t6"], h["be"], c["t5"], ALU.mult))
                rows(tt(c["uq"], c["t2"], c["t6"], ALU.add))

            def rows_2(g):
                pool.wait_ge(sem["un"], g + 1)
                tt(c["zz"], c["un"], h["rbm"], ALU.mult).then_inc(sem["zz"], 1)

            def rows_3(g):
                pool.wait_ge(sem["run"], g + 1)
                pool.wait_ge(sem["th"], 3 * g + 3)
                rows(tt(c["rho"], c["th"], c["run"], ALU.mult))
                rows(tt(c["rxu"], c["rho"], c["xu"], ALU.mult), wait=False)
                rows(tt(c["r2"], c["rho"], c["rho"], ALU.mult))
                rows(tt(c["tw0"], c["rxu"], c["rxu"], ALU.add), wait=False)
                rows(tt(c["s1"], c["r2"], c["uqm"], ALU.mult))
                rows(tt(c["tw"], c["tw0"], ones_c, ALU.add), wait=False)
                rows(tt(c["t7"], h["x2"], c["s1"], ALU.mult))
                rows(tt(c["de"], c["t7"], c["tw"], ALU.add), wait=False)
                rows(tt(c["nx"], c["tw"], c["s1"], ALU.add))

            def rows_4(g):
                rows(tt(c["gg"], c["rho"], h["bc"], ALU.mult), wait=False)
                pool.wait_ge(sem["rd"], g + 1)
                rows(tt(c["t9"], c["rd"], c["nx"], ALU.mult))
                rows(tt(c["rr"], c["gg"], c["rd"], ALU.mult))
                rows(tt(c["t8"], c["rr"], c["al"], ALU.mult), wait=False)
                rows(tt(c["ga2"], c["rr"], h["be"], ALU.mult))
                rows(tt(c["ga0"], c["t8"], c["t9"], ALU.add))
                tt(c["ga"], c["ga0"], ones_c, ALU.add).then_inc(sem["ga"], 1)
                rows.end()

            def h_part(g):
                settle(pool)
                pool.wait_ge(sem["ga"], g + 1)
                if not first(g):
                    pool.wait_ge(sem["hh"], g)
                tt(wide(tx[:, :]), wide(grp(x_all, g)), spread(c["ga"]), ALU.mult).then_inc(sem["tx"], 1)

            def finish_1(g):
                settle(pool)
                if not first(g):
                    pool.wait_ge(sem["fbns"], g)
                    pool.wait_ge(sem["fout"], g)
                pool.wait_ge(sem["dega"], 2 * g + 2)
                pool.wait_ge(sem["const"], 16 * 11)
                tt(wide(fin1[:, :]), beb[:, :].unsqueeze(1).to_broadcast([128, GB, 128]),
                   spread(bt(deg_all, g, GB)), ALU.mult).then_inc(sem["fin1"], 1)

            def finish_2(g):
                pool.wait_ge(sem["fin1"], g + 1)
                pool.wait_ge(sem["e_osb"], GB * g + GB)
                tt(fin1[:, :], fin1[:, :], osb[:, :], ALU.add).then_inc(sem["fin2"], 1)

            def finish_3(g):
                settle(pool)
                pool.wait_ge(sem["fin2"], g + 1)
                pool.wait_ge(sem["x1a"], 16 * g + 16)
                tt(fin1[:, :], fin1[:, :], grp(x1_all, g), ALU.add).then_inc(sem["fin3"], 1)

            def body(a, b, e, f):
                if a is not None:
                    cols_1(a)
                    cols_2(a)
                    split_rows(a)
                    keep_x2(a)
                if b is not None:
                    rows_1(b)
                    rows_2(b)
                    rows_3(b)
                    rows_4(b)
                    h_part(b)
                if a is not None:
                    rank_edges(a)
                    mask_ranks(a)
                    hold(a)
                if e is not None:
                    finish_1(e)
                if a is not None:
                    badness(a)
                    weights_1(a)
                    weights_2(a)
                    weights_3(a)
                    weights_4(a)
                if e is not None:
                    finish_2(e)
                    finish_3(e)

            run_groups(pool, body)

        @block.scalar
        def _(act):
            fn = nc.scalar.activation

            nc.scalar.preload_act_table_set("natural_log_exp_and_others")
            act.wait_ge(sem["const"], 16 * 11)
            act.wait_ge(sem["ones"], 1)
            fn(selb[:, :], self_, ACT.Copy).then_inc(sem["selb"], 1)
            fn(identb[:, :], ident, ACT.Copy).then_inc(sem["selb"], 1)
            fn(colb[:, :], col_i1, ACT.Copy).then_inc(sem["selb"], 1)

            def l0_x(g):
                act.wait_ge(sem["xt_loaded"], 16 * g + 16)
                if not first(g):
                    act.wait_ge(sem["d2"], g)
                fn(xm2[:, :], xts[:, :], ACT.Copy, scale=-2.0).then_inc(sem["xm2"], 1)

            def l0_sqx(g):
                settle(act)
                act.wait_ge(sem["loaded"], 16 * g + 16)
                if not first(g):
                    act.wait_ge(sem["x2"], g)
                fn(sqx[:, :], grp(x_all, g), ACT.Square).then_inc(sem["sqx"], 1)

            def l0_norm(g):
                act.wait_ge(sem["x2m"], g + 1)
                fn(c["lpn"], c["x2m"], ACT.Ln).then_inc(sem["lpn"], 1)
                act.wait_ge(sem["lpn"], g + 1)
                fn(c["pn"], c["lpn"], ACT.Exp, scale=0.5).then_inc(sem["pn"], 1)

            def l0_atanh(g):
                act.wait_ge(sem["pcl"], g + 1)
                fn(c["at1"], c["pcl"], ACT.Ln, bias=one1[:, :]).then_inc(sem["at1"], 1)
                fn(c["at2"], c["pcl"], ACT.Ln, bias=one1[:, :], scale=-1.0).then_inc(sem["at2"], 1)

            def l0_rows(g):
                act.wait_ge(sem["rowst_ps"], g + 1)
                if not first(g):
                    act.wait_ge(sem["d2"], g)
                    act.wait_ge(sem["bj_ps"], g)
                    act.wait_ge(sem["lg"], g)
                fn(rowst[:, :], rt_ps[0:PARTS * ROWS, :], ACT.Copy).then_inc(sem["rowst"], 1)

            def l0_bc(g):
                act.wait_ge(sem["bj_ps"], g + 1)
                if not first(g):
                    act.wait_ge(sem["den"], g)
                fn(bjs[:, :], bj_ps, ACT.Copy).then_inc(sem["bjs"], 1)

            def l0_esig(g):
                act.wait_ge(sem["lg"], g + 1)
                if not first(g):
                    act.wait_ge(sem["lse"], g)
                fn(esig[:, :], lg_ps, ACT.Exp, scale=-1.0).then_inc(sem["esig"], 1)

            def l0_lse(g):
                act.wait_ge(sem["esigc"], g + 1)
                if not first(g):
                    act.wait_ge(sem["q2e"], g)
                fn(lse[:, :], esig[:, :], ACT.Ln, bias=one1[:, :]).then_inc(sem["lse"], 1)

            def l0_logs(g):
                act.wait_ge(sem["nm"], g + 1)
                fn(lnn[:, :], nm[:, :], ACT.Ln).then_inc(sem["lnn"], 1)

            def l0_lnd(g):
                act.wait_ge(sem["denc"], g + 1)
                if not first(g):
                    act.wait_ge(sem["q2e"], g)
                fn(lnd[:, :], den[:, :], ACT.Ln).then_inc(sem["lnd"], 1)

            def l0_u(g):
                act.wait_ge(sem["lsc"], g + 1)
                fn(uw[:, :], ls[:, :], ACT.Exp, scale=0.5).then_inc(sem["uu"], 1)

            def l0_at(g):
                act.wait_ge(sem["ucl"], g + 1)
                if not first(g):
                    act.wait_ge(sem["dl"], g)
                fn(l1[:, :], ucl[:, :], ACT.Ln, bias=one1[:, :]).then_inc(sem["l1"], 1)

            def l0_at2(g):
                act.wait_ge(sem["ucl"], g + 1)
                if not first(g):
                    act.wait_ge(sem["dl"], g)
                fn(l2[:, :], ucl[:, :], ACT.Ln, bias=one1[:, :], scale=-1.0).then_inc(sem["l2"], 1)

            def l0_w0(g):
                act.wait_ge(sem["qe"], g + 1)
                if not first(g):
                    act.wait_ge(sem["w1"], g)
                fn(w0[:, :], qe[:, :], ACT.Exp, scale=-1.0).then_inc(sem["w0"], 1)

            def l0_m(g):
                act.wait_ge(sem["sw"], g + 1)
                if not first(g):
                    act.wait_ge(sem["rows"], ROW_STEPS * g - ROW_STEPS + 1)
                fn(sws[:, :], sw_ps, ACT.Copy).then_inc(sem["sws"], 1)

            def l0_sqm(g):
                act.wait_ge(sem["xmp"], g + 1)
                if not first(g):
                    act.wait_ge(sem["mmr"], g)
                fn(sqm[:, :], m_ps, ACT.Square).then_inc(sem["sqm"], 1)

            def l0_un(g):
                act.wait_ge(sem["uqm"], g + 1)
                fn(c["lun"], c["uqm"], ACT.Ln).then_inc(sem["lun"], 1)
                act.wait_ge(sem["lun"], g + 1)
                fn(c["un"], c["lun"], ACT.Exp, scale=0.5).then_inc(sem["un"], 1)

            def l0_ez(g):
                act.wait_ge(sem["zz"], g + 1)
                fn(c["ez"], c["zz"], ACT.Exp, scale=2.0).then_inc(sem["ez"], 1)

            def l0_rs(g):
                act.wait_ge(sem["vare"], g + 1)
                fn(c["lv"], c["vare"], ACT.Ln).then_inc(sem["lv"], 1)
                act.wait_ge(sem["lv"], g + 1)
                fn(c["rs"], c["lv"], ACT.Exp, scale=-0.5).then_inc(sem["rs"], 1)

            def keep_x1(g):
                act.wait_ge(sem["x1s"], g + 1)
                act.dma_start(grp(x1_all, g), x1s[:, :]).then_inc(sem["x1a"], 16)

            def l0_x1t(g):
                act.wait_ge(sem["x1t_ps"], g + 1)
                if not first(g):
                    act.wait_ge(sem["e_tab"], 2 * g)
                fn(x1t[:, :], lg_ps, ACT.Copy).then_inc(sem["x1t"], 1)

            def bad(g):
                settle(act)
                act.wait_ge(sem["bdiff"], g + 1)
                fn(bsq[:, :], bsq[:, :], ACT.Abs, accum_out=bt(bad_all, g, 1)).then_inc(sem["bad"], 1)

            def split0(g, half):
                act.wait_ge(sem["e_tab"], 2 * g + half + 1)
                if not first(g):
                    act.wait_ge(sem["e_hps"], TILES * g)
                fn(tb[:, 2 * half:2 * half + 2, 0, :], tab_ps[half].rearrange("p (b k) -> p b k", b=2),
                   ACT.Copy).then_inc(sem["e_t0"], 1)

            def split1(g, half):
                act.wait_ge(sem["e_r1"], 2 * g + half + 1)
                fn(tb[:, 2 * half:2 * half + 2, 1, :], r1[:, half, :].rearrange("p (b k) -> p b k", b=2),
                   ACT.Copy).then_inc(sem["e_t1"], 1)

            def distance(g, k):
                q = TILES * g + k
                if not isinstance(q, int):
                    q = act.to_reg(q)
                settle(act)
                act.wait_ge(sem["mid"], g + 1)
                if not (first(g) and k == 0):
                    act.wait_ge(sem["e_si"], q)
                if k == 0:
                    for u in range(GB):
                        last = fn(absd[:, cut(u)], iota_e[:, T:CAP], ACT.Abs, bias=bt(mid_all, GB * g + u, 1), scale=-1.0)
                else:
                    last = fn(absd[:, :], iota_e[:, 0:T], ACT.Abs, bias=bt(mid_all, GB * g + k - 1, 1), scale=-1.0)
                last.then_inc(sem["e_absd"], 1)

            def relu(g, k):
                q = TILES * g + k
                act.wait_ge(sem["e_hps"], q + 1)
                if not (first(g) and k == 0):
                    act.wait_ge(sem["e_yps"], q)
                fn(ht[:, :], h_ps, ACT.Relu, bias=b1c[:, :]).then_inc(sem["e_ht"], 1)

            def keep_y(g, k):
                q, s = TILES * g + k, slot(k)
                act.wait_ge(sem["e_yps"], q + 1)
                if reuse(g, k) is not None:
                    act.wait_ge(sem["e_ops"], GB * g if k == 0 else GB * g + k - 2)
                fn(z[:, s, :], y_ps, ACT.Copy).then_inc(sem["e_z"], 1)

            def squares(g, k):
                q, s = TILES * g + k, slot(k)
                act.wait_ge(sem["e_yps"], q + 1)
                if reuse(g, k) is not None:
                    act.wait_ge(sem["e_lnv"], reuse(g, k))
                if not (first(g) and k == 0):
                    act.wait_ge(sem["e_ss"], q)
                for n in range(CH):
                    last = fn(sq[:, cut(n)], y_ps[:, cut(n)], ACT.Square, accum_out=ss[:, s, n:n + 1])
                last.then_inc(sem["e_ss"], 1)

            def inv_std(g, k):
                q, s = TILES * g + k, slot(k)
                act.wait_ge(sem["e_ss"], q + 1)
                fn(lnv[:, s, :], ss[:, s, :], ACT.Ln, scale=1.0 / D, bias=eps1[:, :]).then_inc(sem["e_lnv"], 1)
                act.wait_ge(sem["e_lnv"], q + 1)
                if reuse(g, k) is not None:
                    act.wait_ge(sem["e_sit"], reuse(g, k))
                fn(rstd[:, s, :], lnv[:, s, :], ACT.Exp, scale=-0.5).then_inc(sem["e_rstd"], 1)

            def finish(g):
                act.wait_ge(sem["fvare"], g + 1)
                fn(f["lv"], f["vare"], ACT.Ln).then_inc(sem["flv"], 1)
                act.wait_ge(sem["flv"], g + 1)
                fn(f["rs"], f["lv"], ACT.Exp, scale=-0.5).then_inc(sem["frs"], 1)

            def store(g):
                act.wait_ge(sem["fout"], g + 1)
                act.dma_start(grp(out, g), fo[:, :]).then_inc(sem["stored"], 16)

            def body(a, b, e, f):
                if a is not None:
                    l0_x(a)
                    l0_sqx(a)
                if e is not None:
                    relu(e, 0)
                if a is not None:
                    l0_norm(a)
                if e is not None:
                    distance(e, 2)
                if a is not None:
                    l0_atanh(a)
                if b is not None:
                    l0_m(b)
                    l0_sqm(b)
                if e is not None:
                    keep_y(e, 0)
                    squares(e, 0)
                    inv_std(e, 0)
                    relu(e, 1)
                if a is not None:
                    l0_rows(a)
                if e is not None:
                    distance(e, 3)
                    keep_y(e, 1)
                    squares(e, 1)
                    inv_std(e, 1)
                if b is not None:
                    l0_un(b)
                if e is not None:
                    relu(e, 2)
                if b is not None:
                    l0_ez(b)
                if a is not None:
                    l0_bc(a)
                if e is not None:
                    distance(e, 4)
                if f is not None:
                    finish(f)
                if a is not None:
                    l0_esig(a)
                if e is not None:
                    keep_y(e, 2)
                    squares(e, 2)
                    inv_std(e, 2)
                if b is not None:
                    distance(b, 0)
                if e is not None:
                    relu(e, 3)
                if a is not None:
                    l0_lse(a)
                if e is not None:
                    keep_y(e, 3)
                if a is not None:
                    l0_logs(a)
                if e is not None:
                    squares(e, 3)
                    relu(e, 4)
                    inv_std(e, 3)
                if b is not None:
                    l0_rs(b)
                if f is not None:
                    store(f)
                if a is not None:
                    l0_lnd(a)
                if b is not None:
                    distance(b, 1)
                if e is not None:
                    squares(e, 4)
                if b is not None:
                    l0_x1t(b)
                if a is not None:
                    l0_u(a)
                if b is not None:
                    keep_x1(b)
                if e is not None:
                    keep_y(e, 4)
                    inv_std(e, 4)
                if a is not None:
                    l0_at(a)
                if b is not None:
                    split0(b, 0)
                    split0(b, 1)
                if a is not None:
                    l0_w0(a)
                if b is not None:
                    split1(b, 0)
                    split1(b, 1)
                if a is not None:
                    l0_at2(a)
                    bad(a)

            run_groups(act, body)
            act.wait_ge(sem["stored"], 16 * groups)

            def dense():
                with act.Fori(0, NB) as b:
                    act.wait_ge(sem["dense_loaded"], 32 * b + 32)
                    fn(g_x1, bt(x1_all, b), ACT.Copy).then_inc(sem["dense_x1"], 1)
                    act.wait_ge(sem["dense_x1t_ps"], b + 1)
                    fn(g_x1t, lg_ps[:, 0:128], ACT.Copy).then_inc(sem["dense_x1t"], 1)
                    act.wait_ge(sem["dense_hps"], b + 1)
                    fn(g_hi, h_ps[:, 0:128], ACT.Identity, bias=b1c[:, :]).then_inc(sem["dense_hidden_ready"], 1)
                    fn(g_hj, h_ps[:, 128:256], ACT.Copy).then_inc(sem["dense_hidden_ready"], 1)
                    with act.Fori(0, N) as i:
                        q = N * b + i
                        act.wait_ge(sem["dense_z"], q + 1)
                        fn(g_sq, g_z, ACT.Square, accum_out=g_ss).then_inc(sem["dense_sq"], 1)
                        act.wait_ge(sem["dense_sq"], q + 1)
                        fn(g_lv, g_ss, ACT.Ln, scale=1.0 / D, bias=eps1[:, :]).then_inc(sem["dense_lv"], 1)
                        act.wait_ge(sem["dense_lv"], q + 1)
                        fn(g_r, g_lv, ACT.Exp, scale=-0.5).then_inc(sem["dense_r"], 1)
                        settle(act)
                        act.wait_ge(sem["dense_o"], q + 1)
                        fn(g_o[:, bass.ds(i, 1)], o_ps[:, 0:1], ACT.Copy).then_inc(sem["dense_hidden_ready"], 1)
                    act.wait_ge(sem["dense_var"], b + 1)
                    fn(g_lv2, g_var, ACT.Ln).then_inc(sem["dense_lv2"], 1)
                    act.wait_ge(sem["dense_lv2"], b + 1)
                    fn(g_rs, g_lv2, ACT.Exp, scale=-0.5).then_inc(sem["dense_rs"], 1)

            where_dense(act, dense)

        @block.vector
        def _(dve):
            v = nc.vector
            tt, ts, stt = v.tensor_tensor, v.tensor_scalar, v.scalar_tensor_tensor

            v.memset(one1[:, :], 1.0).then_inc(sem["ones"], 1)
            v.memset(half_c[:, :], 0.5)
            v.memset(eps1[:, :], LN_EPS)
            v.memset(rowsb[:, :], 0.0)
            v.memset(onex2[:, :], 1.0).then_inc(sem["ones"], 1)
            dve.wait_ge(sem["const"], 16 * 11)
            dve.wait_ge(sem["ones"], 2)
            v.tensor_reduce(w2s[:, :], w2[:, :], AX_X, ALU.add).then_inc(sem["w2sum"], 1)
            v.tensor_reduce(b2s[:, :], b2b[:, :], AX_X, ALU.add).then_inc(sem["b2c"], 1)
            dve.wait_ge(sem["w2sum"], 1)
            ts(w2s[:, :], w2s[:, :], -1.0 / D, None, ALU.mult).then_inc(sem["w2sum"], 1)
            dve.wait_ge(sem["b2c"], 1)
            ts(b2s[:, :], b2s[:, :], -1.0 / D, None, ALU.mult).then_inc(sem["b2c"], 1)
            dve.wait_ge(sem["w2sum"], 2)
            ts(w2c[:, :], w2[:, :], w2s[:, :], None, ALU.add).then_inc(sem["w2c"], 1)
            dve.wait_ge(sem["b2c"], 2)
            ts(b2c[:, :], b2b[:, :], b2s[:, :], None, ALU.add).then_inc(sem["b2c"], 1)
            dve.wait_ge(sem["b2c"], 3)
            v.memset(onesb[:, :], 1.0)
            setup = Chain(dve, sem["b2c"], 7)
            setup.base, setup.k = 3, 0
            setup(ts(b2p[:, 0, :], b2c[:, :], 1.0, None, ALU.mult))
            setup(tt(b2r[:, :], b2c[:, :], b2p[:, 0, :], ALU.subtract))
            setup(ts(b2p[:, 1, :], b2r[:, :], 1.0, None, ALU.mult))
            setup(tt(b2p[:, 2, :], b2r[:, :], b2p[:, 1, :], ALU.subtract))
            setup(ts(b2k[:, :], b2p[:, 0, :], ident[:, 0:1], None, ALU.mult))
            for n in range(1, PARTS):
                setup(stt(b2k[:, :], b2p[:, n, :], ident[:, n:n + 1], b2k[:, :], ALU.mult, ALU.add))
            setup.end()

            rows, frows = Chain(dve, sem["newton"], 3), Chain(dve, sem["frows"], 3)

            def x_sq(g):
                dve.wait_ge(sem["sqx"], g + 1)
                if not first(g):
                    dve.wait_ge(sem["held"], g)
                    dve.wait_ge(sem["cols"], COL_STEPS * g)
                    dve.wait_ge(sem["xcol"], g)
                v.tensor_reduce(c["x2"], wide(sqx[:, :]), AX_X, ALU.add).then_inc(sem["x2"], 1)
                dve.wait_ge(sem["x2"], g + 1)
                ts(c["x2m"], c["x2"], MIN_NORM, None, ALU.max).then_inc(sem["x2m"], 1)
                ts(c["bc"], c["x2"], -1.0, 1.0, ALU.mult, ALU.add).then_inc(sem["bc"], 1)
                dve.wait_ge(sem["bc"], g + 1)
                if not first(g):
                    dve.wait_ge(sem["rbm"], g)
                ts(c["bm"], c["bc"], MIN_NORM, None, ALU.max).then_inc(sem["bm"], 1)

            def reciprocals(g):
                dve.wait_ge(sem["bm"], g + 1)
                v.reciprocal(c["rbm"], c["bm"]).then_inc(sem["rbm"], 1)
                dve.wait_ge(sem["pn"], g + 1)
                ts(c["pcl"], c["pn"], CLIP, None, ALU.min).then_inc(sem["pcl"], 1)
                v.reciprocal(c["rpn"], c["pn"]).then_inc(sem["rpn"], 1)

            def keep_lr(g):
                dve.wait_ge(sem["lr"], g + 1)
                if not first(g):
                    dve.wait_ge(sem["cols"], COL_STEPS * g)
                ts(lrs[:, :], lr_ps, 1.0, None, ALU.mult).then_inc(sem["lrc"], 1)

            def clip_esig(g):
                dve.wait_ge(sem["esig"], g + 1)
                ts(esig[:, :], esig[:, :], SIG_MAX, None, ALU.min).then_inc(sem["esigc"], 1)

            def pairs_a(g):
                dve.wait_ge(sem["d2"], g + 1)
                if not first(g):
                    dve.wait_ge(sem["lnn"], g)
                    dve.wait_ge(sem["lnd"], g)
                ts(nm[:, :], d2_ps, TINY, None, ALU.max).then_inc(sem["nm"], 1)

            def denominator(g):
                dve.wait_ge(sem["d2"], g + 1)
                if not first(g):
                    dve.wait_ge(sem["lnd"], g)
                dve.wait_ge(sem["bjs"], g + 1)
                for u in range(GB):
                    last = stt(den[:, cut(u)], bjs[:, cut(u)], c["bc"][:, u:u + 1], d2_ps[:, cut(u)], ALU.mult, ALU.add)
                last.then_inc(sem["den"], 1)
                dve.wait_ge(sem["den"], g + 1)
                ts(den[:, :], den[:, :], MIN_NORM, None, ALU.max).then_inc(sem["denc"], 1)

            def pairs_b(g):
                dve.wait_ge(sem["lnn"], g + 1)
                dve.wait_ge(sem["lnd"], g + 1)
                tt(ls[:, :], lnn[:, :], lnd[:, :], ALU.subtract).then_inc(sem["ls"], 1)
                dve.wait_ge(sem["ls"], g + 1)
                ts(ls[:, :], ls[:, :], LOG_MIN_NORM, None, ALU.max).then_inc(sem["lsc"], 1)

            def exponent(g):
                dve.wait_ge(sem["lsc"], g + 1)
                dve.wait_ge(sem["q2e"], g + 1)
                if not first(g):
                    dve.wait_ge(sem["w0"], g)
                stt(qe[:, :], ls[:, :], 0.5, q2e[:, :], ALU.mult, ALU.add).then_inc(sem["qe"], 1)

            def clip_u(g):
                dve.wait_ge(sem["uu"], g + 1)
                if not first(g):
                    dve.wait_ge(sem["l1"], g)
                    dve.wait_ge(sem["l2"], g)
                ts(ucl[:, :], uw[:, :], CLIP, None, ALU.min).then_inc(sem["ucl"], 1)

            def dot_x(g):
                dve.wait_ge(sem["mm"], g + 1)
                tt(xmp[:, :], m_ps, grp(x_all, g), ALU.mult).then_inc(sem["xmp"], 1)

            def sum_xm(g):
                dve.wait_ge(sem["xmp"], g + 1)
                if not first(g):
                    dve.wait_ge(sem["rows"], ROW_STEPS * g)
                v.tensor_reduce(c["xmr"], wide(xmp[:, :]), AX_X, ALU.add).then_inc(sem["xmr"], 1)

            def dot_m(g):
                dve.wait_ge(sem["sqm"], g + 1)
                v.tensor_reduce(c["mmr"], wide(sqm[:, :]), AX_X, ALU.add).then_inc(sem["mmr"], 1)

            def clip_uq(g):
                dve.wait_ge(sem["rows"], ROW_STEPS * g + UQ_STEP)
                ts(c["uqm"], c["uq"], MIN_NORM, None, ALU.max).then_inc(sem["uqm"], 1)

            def recip_un(g):
                dve.wait_ge(sem["un"], g + 1)
                v.reciprocal(c["run"], c["un"]).then_inc(sem["run"], 1)

            def tanh(g):
                dve.wait_ge(sem["ez"], g + 1)
                ts(c["e1"], c["ez"], 1.0, None, ALU.add).then_inc(sem["th"], 1)
                dve.wait_ge(sem["th"], 3 * g + 1)
                v.reciprocal(c["re"], c["e1"]).then_inc(sem["th"], 1)
                dve.wait_ge(sem["th"], 3 * g + 2)
                ts(c["th"], c["re"], -2.0, 1.0, ALU.mult, ALU.add).then_inc(sem["th"], 1)

            def recip_de(g):
                dve.wait_ge(sem["rows"], ROW_STEPS * g + DE_STEP)
                ts(c["dec"], c["de"], MIN_NORM, None, ALU.max).then_inc(sem["dec"], 1)
                dve.wait_ge(sem["dec"], g + 1)
                v.reciprocal(c["rd"], c["dec"]).then_inc(sem["rd"], 1)

            def newton(w, chain):
                chain(tt(w["ra"], w["rs"], w["rs"], ALU.mult))
                chain(stt(w["rb"], w["ra"], -0.5, w["vare"], ALU.mult, ALU.mult))
                chain(stt(w["rsn"], w["rb"], 1.5, w["rs"], ALU.add, ALU.mult))
                chain.end()

            def norm0_a(g):
                dve.wait_ge(sem["tx"], g + 1)
                dve.wait_ge(sem["sqm"], g + 1)
                for u in range(GB):
                    last = stt(hh[:, cut(u)], m_ps[:, cut(u)], c["ga2"][:, u:u + 1], tx[:, cut(u)], ALU.mult, ALU.add)
                last.then_inc(sem["hh"], 1)

            def stats0(g):
                dve.wait_ge(sem["hh"], g + 1)
                for u in range(GB):
                    last = v.bn_stats(bns[:, 6 * u:6 * u + 6], hh[:, cut(u)])
                last.then_inc(sem["bns"], 1)
                settle(dve)
                dve.wait_ge(sem["bns"], g + 1)
                for u in range(GB):
                    last = v.bn_aggr(mv[:, 2 * u:2 * u + 2], bns[:, 6 * u:6 * u + 6])
                last.then_inc(sem["bna"], 1)
                dve.wait_ge(sem["bna"], g + 1)
                ts(c["vare"], mv[:, 1:2 * GB:2], LN_EPS, None, ALU.add).then_inc(sem["vare"], 1)

            def norm0_b(g):
                rows.start(g)
                dve.wait_ge(sem["rs"], g + 1)
                newton(c, rows)
                if not first(g):
                    dve.wait_ge(sem["x1t_ps"], g)
                    dve.wait_ge(sem["x1a"], 16 * g)
                for u in range(GB):
                    last = ts(x1s[:, cut(u)], hh[:, cut(u)], mv[:, 2 * u:2 * u + 1], c["rsn"][:, u:u + 1],
                              ALU.subtract, ALU.mult)
                last.then_inc(sem["x1s"], 1)

            def ranks_a(g):
                dve.wait_ge(sem["adj_loaded"], 16 * g + 16)
                if not first(g):
                    dve.wait_ge(sem["rank"], g)
                v.tensor_tensor_scan(scan[:, :], reset, adjs[:, :], 0.0, ALU.mult, ALU.add).then_inc(sem["scan"], 1)
                dve.wait_ge(sem["scan"], g + 1)
                if not first(g):
                    dve.wait_ge(sem["off"], g)
                ts(c["dg"], scan[:, 127:W:128], 1.0, None, ALU.mult).then_inc(sem["degs"], 1)

            def degrees(g):
                dve.wait_ge(sem["degs"], g + 1)
                ts(bt(deg_all, g, GB), c["dg"], 1.0, None, ALU.mult).then_inc(sem["dega"], 1)
                ts(bt(half_all, g, GB), c["dg"], 0.5, -0.5, ALU.mult, ALU.add).then_inc(sem["dega"], 1)

            def ranks_b(g):
                dve.wait_ge(sem["off"], g + 1)
                if not first(g):
                    dve.wait_ge(sem["rank"], g)
                    dve.wait_ge(sem["mid"], g)
                ts(offc[:, :], off_ps, 1.0, None, ALU.mult).then_inc(sem["offc"], 1)
                dve.wait_ge(sem["offc"], g + 1)
                dve.wait_ge(sem["dega"], 2 * g + 2)
                tt(bt(mid_all, g, GB), offc[:, :], bt(half_all, g, GB), ALU.add).then_inc(sem["mid"], 1)

            def split_r1(g, half):
                dve.wait_ge(sem["e_t0"], 2 * g + half + 1)
                if not first(g):
                    dve.wait_ge(sem["e_t1"], 2 * g)
                    dve.wait_ge(sem["e_t2b"], 2 * g)
                tt(r1[:, half, :].rearrange("p (b k) -> p b k", b=2), tab_ps[half].rearrange("p (b k) -> p b k", b=2),
                   tb[:, 2 * half:2 * half + 2, 0, :], ALU.subtract).then_inc(sem["e_r1"], 1)

            def split_t2(g, half):
                dve.wait_ge(sem["e_t1"], 2 * g + half + 1)
                tt(tb[:, 2 * half:2 * half + 2, 2, :], r1[:, half, :].rearrange("p (b k) -> p b k", b=2),
                   tb[:, 2 * half:2 * half + 2, 1, :], ALU.subtract).then_inc(sem["e_t2b"], 1)

            def row_hot(g, k):
                q, s = TILES * g + k, slot(k)
                dve.wait_ge(sem["e_absd"], q + 1)
                if reuse(g, k) is not None:
                    dve.wait_ge(sem["e_hps"], reuse(g, k))
                    dve.wait_ge(sem["e_ie"], reuse(g, k))
                if k == 0:
                    for u in range(GB):
                        last = ts(si[:, s, cut(u)], absd[:, cut(u)], bt(half_all, GB * g + u, 1), None, ALU.is_le)
                else:
                    last = ts(si[:, s, :], absd[:, :], bt(half_all, GB * g + k - 1, 1), None, ALU.is_le)
                last.then_inc(sem["e_si"], 1)

            def col_hot(g, k):
                q, s = TILES * g + k, slot(k)
                dve.wait_ge(sem["e_vg"], q + 1)
                if reuse(g, k) is not None:
                    dve.wait_ge(sem["e_hps"], reuse(g, k))
                tt(sj[:, s, :], vg_ps, rank_tail if k == 0 else rank_main, ALU.is_equal).then_inc(sem["e_sj"], 1)

            def keep_numbers(g, k):
                tiles = (0, 1) if k == 1 else (k,)
                dve.wait_ge(sem["e_ie"], TILES * g + k + 1)
                if reuse(g, k) is not None:
                    dve.wait_ge(sem["e_sit"], reuse(g, k))
                a = slot(tiles[0])
                ts(ies[:, a:a + len(tiles), :].rearrange("p t c -> p (t c)"), ie_ps[:, 0:CH * len(tiles)], 1.0, None,
                   ALU.mult).then_inc(sem["e_ies"], len(tiles))

            def row_hot_t(g, k):
                q, s = TILES * g + k, slot(k)
                dve.wait_ge(sem["e_rstd"], q + 1)
                dve.wait_ge(sem["e_ies"], q + 1)
                if reuse(g, k) is not None:
                    dve.wait_ge(sem["e_ops"], GB * g if k == 0 else GB * g + k - 1 - (0, 2, 2, 2, 2)[k] + 1)
                for n in range(CH):
                    last = ts(sit[:, s, cut(n)], iota_i1, ies[:, s, n:n + 1], rstd[:, s, n:n + 1],
                              ALU.is_equal, ALU.mult)
                last.then_inc(sem["e_sit"], 1)

            def gamma_out(g, u):
                dve.wait_ge(sem["e_ops"], GB * g + u + 1)
                if not first(g):
                    dve.wait_ge(sem["fin2"], g)
                tt(osb[:, cut(u)], o_ps, gab[:, :], ALU.mult).then_inc(sem["e_osb"], 1)

            def finish_a(g):
                dve.wait_ge(sem["fin3"], g + 1)
                for u in range(GB):
                    last = v.bn_stats(fbns[:, 6 * u:6 * u + 6], fin1[:, cut(u)])
                last.then_inc(sem["fbns"], 1)
                settle(dve)
                dve.wait_ge(sem["fbns"], g + 1)
                for u in range(GB):
                    last = v.bn_aggr(fmv[:, 2 * u:2 * u + 2], fbns[:, 6 * u:6 * u + 6])
                last.then_inc(sem["fbna"], 1)
                dve.wait_ge(sem["fbna"], g + 1)
                ts(f["vare"], fmv[:, 1:2 * GB:2], LN_EPS, None, ALU.add).then_inc(sem["fvare"], 1)

            def finish_b(g):
                frows.start(g)
                dve.wait_ge(sem["frs"], g + 1)
                newton(f, frows)
                if not first(g):
                    dve.wait_ge(sem["stored"], 16 * g)
                for u in range(GB):
                    last = ts(fo[:, cut(u)], fin1[:, cut(u)], fmv[:, 2 * u:2 * u + 1], f["rsn"][:, u:u + 1],
                              ALU.subtract, ALU.mult)
                last.then_inc(sem["fout"], 1)

            def body(a, b, e, f):
                if a is not None:
                    keep_lr(a)
                    ranks_a(a)
                    degrees(a)
                if e is not None:
                    col_hot(e, 1)
                if a is not None:
                    ranks_b(a)
                    x_sq(a)
                    reciprocals(a)
                if e is not None:
                    keep_numbers(e, 1)
                if b is not None:
                    dot_x(b)
                if e is not None:
                    row_hot(e, 2)
                if b is not None:
                    sum_xm(b)
                    dot_m(b)
                if f is not None:
                    finish_a(f)
                if e is not None:
                    row_hot_t(e, 0)
                    row_hot(e, 3)
                    keep_numbers(e, 2)
                    col_hot(e, 2)
                if b is not None:
                    clip_uq(b)
                if e is not None:
                    row_hot_t(e, 1)
                if b is not None:
                    recip_un(b)
                if e is not None:
                    col_hot(e, 3)
                    row_hot(e, 4)
                    keep_numbers(e, 3)
                if b is not None:
                    tanh(b)
                if a is not None:
                    clip_esig(a)
                if f is not None:
                    finish_b(f)
                if b is not None:
                    recip_de(b)
                if e is not None:
                    gamma_out(e, 0)
                    row_hot_t(e, 2)
                    keep_numbers(e, 4)
                    col_hot(e, 4)
                if b is not None:
                    row_hot(b, 0)
                    norm0_a(b)
                if a is not None:
                    pairs_a(a)
                if b is not None:
                    stats0(b)
                if a is not None:
                    denominator(a)
                if e is not None:
                    gamma_out(e, 1)
                    row_hot_t(e, 3)
                if b is not None:
                    norm0_b(b)
                    col_hot(b, 0)
                if a is not None:
                    pairs_b(a)
                if b is not None:
                    row_hot(b, 1)
                if e is not None:
                    gamma_out(e, 2)
                if a is not None:
                    clip_u(a)
                    exponent(a)
                if e is not None:
                    row_hot_t(e, 4)
                if b is not None:
                    split_r1(b, 0)
                    split_r1(b, 1)
                if e is not None:
                    gamma_out(e, 3)
                if b is not None:
                    split_t2(b, 0)
                    split_t2(b, 1)

            run_groups(dve, body)

            dve.wait_ge(sem["bad"], groups)
            v.tensor_reduce(fl[:, 0:1], bad_all[:, 0:groups], AX_X, ALU.add).then_inc(sem["badr"], 1)
            dve.wait_ge(sem["nall"], 2)
            ts(okn[:, 0:GB * groups], y_ps[:, 0:GB * groups], float(CAP), None, ALU.is_le).then_inc(sem["okn"], 1)
            ts(fl[:, 1:2], y_ps[:, 128:129], 0.0, None, ALU.is_le).then_inc(sem["okn"], 1)
            dve.wait_ge(sem["okn"], 2)
            v.tensor_reduce(fl[:, 2:3], okn[:, 0:GB * groups], AX_X, ALU.min).then_inc(sem["okn"], 1)
            dve.wait_ge(sem["okn"], 3)
            tt(fl[:, 3:4], fl[:, 1:2], fl[:, 2:3], ALU.mult).then_inc(sem["flagf"], 1)
            dve.wait_ge(sem["flagf"], 1)
            dve.wait_ge(sem["e_osb"], GB * groups)
            ts(flagi[:, :], fl[:, 3:4], -1.0, 1.0, ALU.mult, ALU.add).then_inc(sem["flag"], 1)

            def dense():
                drows = Chain(dve, sem["dense_rows"], DENSE_ROW_STEPS)
                with dve.Fori(0, NB) as b:
                    with dve.Fori(0, N) as i:
                        q = N * b + i
                        settle(dve)
                        dve.wait_ge(sem["dense_hidden_ready"], (N + 2) * b + i + 2)
                        ts(g_h, g_hj, g_hi[:, bass.ds(i, 1)], 0.0, ALU.add, ALU.max).then_inc(sem["dense_h"], 1)
                        dve.wait_ge(sem["dense_y"], q + 1)
                        tt(g_z, y_ps[:, 0:128], b2c[:, :], ALU.add).then_inc(sem["dense_z"], 1)
                        settle(dve)
                        dve.wait_ge(sem["dense_r"], q + 1)
                        tt(g_w, g_r, g_adjt[:, bass.ds(i, 1)], ALU.mult).then_inc(sem["dense_w"], 1)
                    drows.start(b)
                    dve.wait_ge(sem["dense_turned"], b + 1)
                    drows(tt(g_rows, lg_ps[:, 0:128], gab[:, :], ALU.mult))
                    drows(v.tensor_reduce(g_deg, g_adj, AX_X, ALU.add))
                    drows(stt(g_rows, beb[:, :], g_deg, g_rows, ALU.mult, ALU.add))
                    drows(tt(g_rows, g_rows, g_x1, ALU.add))
                    v.bn_stats(g_bns, g_rows).then_inc(sem["dense_bns"], 1)
                    settle(dve)
                    dve.wait_ge(sem["dense_bns"], b + 1)
                    v.bn_aggr(g_mv, g_bns).then_inc(sem["dense_rows"], 1)
                    drows.k += 1
                    dve.wait_ge(sem["dense_rows"], drows.base + drows.k)
                    ts(g_var, g_mv[:, 1:2], LN_EPS, None, ALU.add).then_inc(sem["dense_var"], 1)
                    dve.wait_ge(sem["dense_rs"], b + 1)
                    newton(g_tiny, drows)
                    dve.wait_ge(sem["dense_stored"], 16 * b + 16)
                    ts(g_out, g_rows, g_mv[:, 0:1], g_tiny["rsn"], ALU.subtract, ALU.mult).then_inc(sem["dense_out"], 1)

            where_dense(dve, dense)

        @block.tensor
        def _(pe):
            mm = nc.tensor.matmul

            pe.wait_ge(sem["const"], 16 * 11)
            pe.wait_ge(sem["selb"], 3)
            pe.wait_ge(sem["w2c"], 1)
            pe.wait_ge(sem["b2c"], 10)

            def logits_raw(g, e):
                pe.wait_ge(sem["xt_loaded"], 16 * g + 16)
                if not first(g):
                    pe.wait_ge(sem["offc"], g)
                    pe.wait_ge(sem["lrc"], g)
                if e is not None and not first(e):
                    pe.wait_ge(sem["e_ies"], TILES * e)
                    pe.wait_ge(sem["e_osb"], GB * e)
                for u in range(GB):
                    last = mm(lr_ps[:, 2 * u:2 * u + 2], xts[:, cut(u)], wlr[:, :], start=True, stop=True)
                last.then_inc(sem["lr"], 1)

            def turn_rows(g):
                pe.wait_ge(sem["rowsb"], g + 1)
                if not first(g):
                    pe.wait_ge(sem["sws"], g)
                    pe.wait_ge(sem["bjs"], g)
                nc.tensor.transpose(rt_ps, rowsb[:, :], identb[:, :]).then_inc(sem["rowst_ps"], 1)

            def spread_rows(g):
                pe.wait_ge(sem["rowst"], g + 1)
                for u in range(GB):
                    last = mm(bj_ps[:, cut(u)], selv[:, BB, u, :], rowst[:, :], start=True, stop=True)
                last.then_inc(sem["bj_ps"], 1)

            def spread_logits(g):
                pe.wait_ge(sem["rowst"], g + 1)
                if not first(g):
                    pe.wait_ge(sem["esig"], g)
                if not (isinstance(g, int) and g < 2):
                    pe.wait_ge(sem["e_r1"], 2 * g - 2)
                for u in range(GB):
                    mm(lg_ps[:, cut(u)], rowst[:, :], selv[:, RR, u, :], start=True, stop=False)
                    last = mm(lg_ps[:, cut(u)], selv[:, LL, u, :], rowst[:, :], start=False, stop=True)
                last.then_inc(sem["lg"], 1)

            def gram(g):
                pe.wait_ge(sem["xm2"], g + 1)
                if not first(g):
                    pe.wait_ge(sem["nm"], g)
                    pe.wait_ge(sem["den"], g)
                for u in range(GB):
                    d2 = d2_ps[:, cut(u)]
                    mm(d2, xts[:, cut(u)], xm2[:, cut(u)], start=True, stop=False)
                    mm(d2, rowst[:, :], selv[:, X2, u, :], start=False, stop=False)
                    last = mm(d2, selv[:, X2, u, :], rowst[:, :], start=False, stop=True)
                last.then_inc(sem["d2"], 1)

            def with_x(g):
                pe.wait_ge(sem["wt"], g + 1)
                if not first(g):
                    pe.wait_ge(sem["e_r1"], 2 * g)
                pe.wait_ge(sem["bjs"], g + 1)
                pe.wait_ge(sem["xcol"], g + 1)
                for u in range(GB):
                    last = mm(sw_ps[:, 2 * u:2 * u + 2], wt[:, cut(u)], onex2[:, 2 * u:2 * u + 2], start=True, stop=True)
                last.then_inc(sem["sw"], 1)

            def with_x_m(g):
                pe.wait_ge(sem["wt"], g + 1)
                if not first(g):
                    pe.wait_ge(sem["e_r1"], 2 * g)
                for u in range(GB):
                    last = mm(m_ps[:, cut(u)], wt[:, cut(u)], bt(x_all, GB * g + u), start=True, stop=True)
                last.then_inc(sem["mm"], 1)

            def turn_x1(g, a):
                pe.wait_ge(sem["x1s"], g + 1)
                pe.wait_ge(sem["esig"], groups if a is None else a + 1)
                if not first(g):
                    pe.wait_ge(sem["e_r1"], 2 * g)
                for u in range(GB):
                    last = nc.tensor.transpose(lg_ps[:, cut(u)], x1s[:, cut(u)], ident)
                last.then_inc(sem["x1t_ps"], 1)

            def offsets(g):
                pe.wait_ge(sem["degs"], g + 1)
                pe.wait_ge(sem["lrc"], g + 1)
                mm(off_ps, tri, c["dg"], start=True, stop=True).then_inc(sem["off"], 1)

            def tables(g, half):
                pe.wait_ge(sem["x1t"], g + 1)
                if half == 1:
                    pe.wait_ge(sem["hh"], g + 1)
                for u in range(2):
                    last = mm(tab_ps[half][:, 256 * u:256 * u + 256], x1t[:, cut(2 * half + u)], w1c[:, :], start=True, stop=True)
                last.then_inc(sem["e_tab"], 1)

            def row_ranks(g, k):
                q, s = TILES * g + k, slot(k)
                pe.wait_ge(sem["e_si"], q + 1)
                pe.wait_ge(sem["vt"], g + 1)
                if not (first(g) and k == 0):
                    pe.wait_ge(sem["e_sj"], q)
                if k == 0:
                    for u in range(GB):
                        last = mm(vg_ps[:, cut(u)], bt(vt_all, GB * g + u), si[:, s, cut(u)], start=True, stop=True)
                else:
                    last = mm(vg_ps, bt(vt_all, GB * g + k - 1), si[:, s, :], start=True, stop=True)
                last.then_inc(sem["e_vg"], 1)

            def row_numbers(g, k, a):
                tiles = (0, 1) if k == 1 else (k,)
                pe.wait_ge(sem["e_si"], TILES * g + k + 1)
                pe.wait_ge(sem["offc"], groups if a is None else a + 1)
                if not (first(g) and k == 1):
                    pe.wait_ge(sem["e_ies"], TILES * g + tiles[0])
                if k > 3:
                    pe.wait_ge(sem["e_osb"], GB * g + k - 3)
                elif not first(g):
                    pe.wait_ge(sem["e_osb"], GB * g)
                for m, t in enumerate(tiles):
                    for n in range(CH):
                        last = mm(ie_ps[:, CH * m + n:CH * m + n + 1], si[:, slot(t), cut(n)], colb[:, :],
                                  start=True, stop=True)
                last.then_inc(sem["e_ie"], len(tiles))

            def gather(g, k):
                q, s = TILES * g + k, slot(k)
                pe.wait_ge(sem["e_sj"], q + 1)
                if not (first(g) and k == 0):
                    pe.wait_ge(sem["e_ht"], q)
                spans = [(u, cut(u)) for u in range(GB)] if k == 0 else [(k - 1, slice(0, T))]
                for u, cols_ in spans:
                    if k == 0 and u % 2 == 0:
                        pe.wait_ge(sem["e_t2b"], 2 * g + u // 2 + 1)
                    for n in range(PARTS):
                        mm(h_ps[:, cols_], tb[:, u, n, 0:128], si[:, s, cols_], start=(n == 0), stop=False)
                        last = mm(h_ps[:, cols_], tb[:, u, n, 128:256], sj[:, s, cols_],
                                  start=False, stop=(n == PARTS - 1))
                last.then_inc(sem["e_hps"], 1)

            def second(g, k):
                q = TILES * g + k
                pe.wait_ge(sem["e_ht"], q + 1)
                if not (first(g) and k == 0):
                    pe.wait_ge(sem["e_z"], q)
                    pe.wait_ge(sem["e_ss"], q)
                for n in range(CH):
                    mm(y_ps[:, cut(n)], onesb[:, :], b2k[0:PARTS, :], start=True, stop=False)
                    last = mm(y_ps[:, cut(n)], ht[:, cut(n)], w2c[:, :], start=False, stop=True)
                last.then_inc(sem["e_yps"], 1)

            def add_rows(g, k):
                q, s = TILES * g + k, slot(k)
                pe.wait_ge(sem["e_sit"], q + 1)
                pe.wait_ge(sem["e_z"], q + 1)
                pe.wait_ge(sem["e_ies"], TILES * g + min(k + 2, TILES - 1) + 1)
                if not (first(g) and k == 1):
                    pe.wait_ge(sem["e_osb"], GB * g + k - 1)
                mm(o_ps, sit[:, 0, cut(k - 1)], z[:, 0, cut(k - 1)], start=True, stop=False)
                for n in range(CH):
                    last = mm(o_ps, sit[:, s, cut(n)], z[:, s, cut(n)], start=False, stop=(n == CH - 1))
                last.then_inc(sem["e_ops"], 1)

            def body(a, b, e, f):
                if a is not None:
                    logits_raw(a, e)
                if e is not None:
                    gather(e, 0)
                    row_ranks(e, 1)
                if a is not None:
                    offsets(a)
                if b is not None:
                    with_x(b)
                    with_x_m(b)
                if e is not None:
                    row_numbers(e, 1, a)
                    second(e, 0)
                    gather(e, 1)
                    row_ranks(e, 2)
                    row_numbers(e, 2, a)
                if a is not None:
                    turn_rows(a)
                if e is not None:
                    second(e, 1)
                if a is not None:
                    spread_logits(a)
                if e is not None:
                    gather(e, 2)
                if a is not None:
                    spread_rows(a)
                if e is not None:
                    row_ranks(e, 3)
                    row_numbers(e, 3, a)
                    second(e, 2)
                if a is not None:
                    gram(a)
                if e is not None:
                    add_rows(e, 1)
                    gather(e, 3)
                    row_ranks(e, 4)
                    row_numbers(e, 4, a)
                    second(e, 3)
                    gather(e, 4)
                if b is not None:
                    row_ranks(b, 0)
                if e is not None:
                    add_rows(e, 2)
                    second(e, 4)
                if b is not None:
                    turn_x1(b, a)
                if e is not None:
                    add_rows(e, 3)
                if b is not None:
                    tables(b, 0)
                    tables(b, 1)
                if e is not None:
                    add_rows(e, 4)

            run_groups(pe, body)
            pe.wait_ge(sem["dega"], 2 * groups)
            pe.wait_ge(sem["badr"], 1)
            mm(y_ps[:, 0:GB * groups], ones_f, deg_all[:, 0:GB * groups], start=True, stop=True).then_inc(sem["nall"], 1)
            mm(y_ps[:, 128:129], ones_f, fl[:, 0:1], start=True, stop=True).then_inc(sem["nall"], 1)

            def dense():
                with pe.Fori(0, NB) as b:
                    pe.wait_ge(sem["dense_x1"], b + 1)
                    nc.tensor.transpose(lg_ps[:, 0:128], g_x1, ident).then_inc(sem["dense_x1t_ps"], 1)
                    pe.wait_ge(sem["dense_x1t"], b + 1)
                    mm(h_ps[:, 0:128], w1c[:, 0:128], g_x1t, start=True, stop=True)
                    mm(h_ps[:, 128:256], w1c[:, 128:256], g_x1t, start=True, stop=True).then_inc(sem["dense_hps"], 1)
                    with pe.Fori(0, N) as i:
                        q = N * b + i
                        pe.wait_ge(sem["dense_h"], q + 1)
                        mm(y_ps[:, 0:128], g_h, w2c[:, :], start=True, stop=True).then_inc(sem["dense_y"], 1)
                        pe.wait_ge(sem["dense_w"], q + 1)
                        mm(o_ps[:, 0:1], g_z, g_w, start=True, stop=True).then_inc(sem["dense_o"], 1)
                    pe.wait_ge(sem["dense_hidden_ready"], (N + 2) * b + N + 2)
                    nc.tensor.transpose(lg_ps[:, 0:128], g_o, ident).then_inc(sem["dense_turned"], 1)

            where_dense(pe, dense)


def constants():
    import numpy as np

    k = np.arange(128)
    tri = (k[:, None] < k[None, :]).astype(np.float32)
    reset = np.tile((k > 0).astype(np.float32), (128, GB))
    f32 = np.concatenate([tri, np.eye(128, dtype=np.float32), np.ones((128, 128), np.float32), reset,
                          np.zeros((128, 1), np.float32)], 1)
    e = np.arange(CAP)
    fp16 = np.concatenate([np.tile(e, (128, 1)), np.tile(e[:T] + 1, (128, 1)),
                           np.tile(e[T:] + 1, (128, GB)), np.tile(k + 1, (128, 1)),
                           (k + 1)[:, None]], 1).astype(np.float16)
    rows = np.arange(PARTS * ROWS) % ROWS
    want = np.array([[4 * b + t for b in range(GB)] for t in range(4)])
    sel = (rows[:, None, None] == want[None]).astype(np.float16)
    sel = np.repeat(sel.reshape(PARTS * ROWS, 4 * GB), 128, axis=1)
    return {"c_f32": f32, "c_fp16": fp16, "c_sel": sel}


def kernel(**inputs):
    import numpy as np
    import concourse.bacc as bacc
    from concourse.bass_utils import run_bass_kernel_spmd

    a = {k: np.asarray(v) for k, v in inputs.items()}

    def flat(v):
        return np.ascontiguousarray(v).reshape(128, NB * 128)

    arrays = {
        "x_n": flat(a["x"].transpose(1, 0, 2)), "x_t": flat(a["x"].transpose(2, 0, 1)),
        "adj_n": flat(a["adj"].transpose(1, 0, 2)), "adj_t": flat(a["adj"].transpose(2, 0, 1)),
        "att_w": a["L0_gnn_att_w"].reshape(2, 128).T, "att_b": a["L0_gnn_att_b"].reshape(1),
        "W1": a["L1_gnn_W1"].reshape(2, 128, 128).transpose(1, 0, 2).reshape(128, 256),
        "b1": a["L1_gnn_b1"].reshape(128, 1), "W2": a["L1_gnn_W2"], "b2": a["L1_gnn_b2"],
        "gamma": a["L1_gnn_gamma"], "beta": a["L1_gnn_beta"], **constants(),
    }
    nc = bacc.Bacc("TRN2", target_bir_lowering=False, num_devices=1)
    aps = {}
    for name, v in arrays.items():
        arrays[name] = v = np.ascontiguousarray(v)
        aps[name] = nc.dram_tensor(name, v.shape, mybir.dt.from_np(v.dtype), kind="ExternalInput").ap()
    out = nc.dram_tensor("out", (128, NB * 128), F32, kind="ExternalOutput").ap()
    two_graph_layers(nc, out=out, **aps)
    r = run_bass_kernel_spmd(nc, [arrays], core_ids=[0])
    return np.ascontiguousarray(r.results[0]["out"].reshape(128, NB, 128).transpose(1, 0, 2))
```
